# Optimizing a Trainium2 kernel written in Bass

```python
import numpy as np
import jax
import jax.numpy as jnp

def _softmax(x, axis=-1):
    return jax.nn.softmax(x, axis=axis)

def _gelu(x):
    return jax.nn.gelu(x, approximate=True)

def _silu(x):
    return jax.nn.silu(x)

def _sigmoid(x):
    return jax.nn.sigmoid(x)

def _layernorm(x, axis=-1, eps=1e-05):
    m = jnp.mean(x, axis=axis, keepdims=True)
    v = jnp.var(x, axis=axis, keepdims=True)
    return (x - m) / jnp.sqrt(v + eps)

def _scatter_add(tgt, idx, src, axis=0):
    return tgt.at[idx].add(src)

def _segment_sum(src, seg, n):
    return jax.ops.segment_sum(src, seg, n)
kernel_name = 'mk_xattn_ffn_d2_seqx_r8_b1a665'

def setup_inputs(seed: int=0):
    np.random.seed(seed)
    _w = jnp.asarray

    def _rec_inputs():
        import jax
        import jax.numpy as jnp
        _rk = jax.random.key(seed)
        x = -0.0002928 + 1 * jax.random.normal(jax.random.fold_in(_rk, 1), (8, 256, 128), jnp.float32)
        _lenS = 256 - jax.random.randint(jax.random.fold_in(_rk, 7), (8,), 0, max(1, 256 // 4) + 1, jnp.int32)
        _lenS2 = 256 - jax.random.randint(jax.random.fold_in(_rk, 8), (8,), 0, max(1, 256 // 4) + 1, jnp.int32)
        _ctx_1024P = jax.random.normal(jax.random.fold_in(_rk, 11), (8, 16, 128), jnp.float32)
        _ctx_1024c = jax.random.dirichlet(jax.random.fold_in(_rk, 511), 0.3 * jnp.ones((16,), jnp.float32), (8, 256))
        _ctx_1024t = jnp.einsum('bsk,bkd->bsd', _ctx_1024c, _ctx_1024P)
        _ctx_1024t = _ctx_1024t * jax.lax.rsqrt(jnp.mean(jnp.square(_ctx_1024t)) + 1e-12) * 0.953939
        ctx_1024 = -1.39393e-06 + 0.999914 * (_ctx_1024t + 0.3 * jax.random.normal(jax.random.fold_in(_rk, 611), (8, 256, 128), jnp.float32))
        _validS = jnp.arange(256)[None, :] < _lenS[:, None]
        _validS2 = jnp.arange(256)[None, :] < _lenS2[:, None]
        _causal = jnp.tril(jnp.ones((256, 256), dtype=bool))
        mask_Bx16xSxS2_ff0 = jnp.where(jnp.ones((8, 16, 256, 256), dtype=bool), 0.0, -1000000000.0).astype(jnp.float32)
        return (x, ctx_1024, mask_Bx16xSxS2_ff0)
    x, ctx_1024, mask_Bx16xSxS2_ff0 = _rec_inputs()

    def _L0_xattn_setup():
        import jax, jax.numpy as jnp
        import numpy as np
        B, S, D = (2, 256, 128)
        H = 16
        DH = D // H
        LAMBDA_INIT = 0.8
        EPS = 1e-05
        SCALE = 1.0 / np.sqrt(DH)
        key = jax.random.key(seed)
        ks = jax.random.split(key, 13)
        inp = {'query': jax.random.normal(ks[0], (B, S, D), jnp.float32), 'key': jax.random.normal(ks[1], (B, S, D), jnp.float32), 'value': jax.random.normal(ks[2], (B, S, D), jnp.float32), 'attn_mask': jnp.zeros((B, H, S, S), jnp.float32), 'W_q': jax.random.normal(ks[3], (D, 2 * DH * H), jnp.float32) * 0.02, 'W_k': jax.random.normal(ks[4], (D, 2 * DH * H), jnp.float32) * 0.02, 'W_v': jax.random.normal(ks[5], (D, DH * H), jnp.float32) * 0.02, 'W_o': jax.random.normal(ks[6], (DH * H, D), jnp.float32) * 0.02, 'lambda_q1': jax.random.normal(ks[7], (H, DH), jnp.float32) * 0.1, 'lambda_k1': jax.random.normal(ks[8], (H, DH), jnp.float32) * 0.1, 'lambda_q2': jax.random.normal(ks[9], (H, DH), jnp.float32) * 0.1, 'lambda_k2': jax.random.normal(ks[10], (H, DH), jnp.float32) * 0.1, 'rms_scale': jnp.ones((DH,), jnp.float32)}
        return inp
    _L0_xattn_all = _L0_xattn_setup()
    _L0_xattn_in = {k: v for k, v in _L0_xattn_all.items() if k in ('W_q', 'W_k', 'W_v', 'W_o', 'lambda_q1', 'lambda_k1', 'lambda_q2', 'lambda_k2', 'rms_scale')}
    del _L0_xattn_all

    def _L0_ffn_setup():
        import jax, jax.numpy as jnp
        import numpy as np
        TOP_K = 2
        ROUTE_SCALE = 1.0
        EPS = 1e-20
        key = jax.random.key(seed)
        ks = jax.random.split(key, 8)
        dim, hid, E, X = (128, 352, 8, 1)
        std = 0.02
        x = jax.random.normal(ks[0], (2, 256, dim), dtype=jnp.float32)
        w1 = jax.random.normal(ks[1], (E, hid, dim), dtype=jnp.float32) * std
        w2 = jax.random.normal(ks[2], (E, dim, hid), dtype=jnp.float32) * std
        w3 = jax.random.normal(ks[3], (E, hid, dim), dtype=jnp.float32) * std
        new_w1 = jax.random.normal(ks[4], (X, hid, dim), dtype=jnp.float32) * std
        new_w2 = jnp.zeros((X, dim, hid), dtype=jnp.float32)
        new_w3 = jax.random.normal(ks[5], (X, hid, dim), dtype=jnp.float32) * std
        gate_weight = jax.random.normal(ks[6], (E, dim), dtype=jnp.float32) * std
        new_gate_weight = jax.random.normal(ks[7], (X, dim), dtype=jnp.float32) * std
        gate_bias = jnp.zeros((X,), dtype=jnp.float32)
        return dict(x=x, w1=w1, w2=w2, w3=w3, new_w1=new_w1, new_w2=new_w2, new_w3=new_w3, gate_weight=gate_weight, new_gate_weight=new_gate_weight, gate_bias=gate_bias)
    _L0_ffn_all = _L0_ffn_setup()
    _L0_ffn_in = {k: v for k, v in _L0_ffn_all.items() if k in ('w1', 'w2', 'w3', 'new_w1', 'new_w2', 'new_w3', 'gate_weight', 'new_gate_weight', 'gate_bias')}
    del _L0_ffn_all

    def _L1_xattn_setup():
        import jax, jax.numpy as jnp
        import numpy as np
        DIM = 128
        HEADS = 16
        DIM_HEAD = 64
        INNER = HEADS * DIM_HEAD
        EPS = 1e-05

        def layer_norm(x, gamma, beta):
            mu = jnp.mean(x, axis=-1, keepdims=True)
            var = jnp.mean(jnp.square(x - mu), axis=-1, keepdims=True)
            return (x - mu) * jax.lax.rsqrt(var + EPS) * gamma + beta
        key = jax.random.key(seed)
        ks = jax.random.split(key, 6)
        b, n1, n2 = (8, 512, 32)
        x = jax.random.normal(ks[0], (b, n1, DIM), dtype=jnp.float32)
        latents = jax.random.normal(ks[1], (b, n2, DIM), dtype=jnp.float32)
        s = 1.0 / np.sqrt(DIM)
        Wq = jax.random.normal(ks[2], (DIM, INNER), dtype=jnp.float32) * s
        Wkv = jax.random.normal(ks[3], (DIM, 2 * INNER), dtype=jnp.float32) * s
        Wout = jax.random.normal(ks[4], (INNER, DIM), dtype=jnp.float32) * (1.0 / np.sqrt(INNER))
        g1 = jnp.ones((DIM,), jnp.float32)
        b1 = jnp.zeros((DIM,), jnp.float32)
        g2 = jnp.ones((DIM,), jnp.float32)
        b2 = jnp.zeros((DIM,), jnp.float32)
        return {'x': x, 'latents': latents, 'g1': g1, 'b1': b1, 'g2': g2, 'b2': b2, 'Wq': Wq, 'Wkv': Wkv, 'Wout': Wout}
    _L1_xattn_all = _L1_xattn_setup()
    _L1_xattn_in = {k: v for k, v in _L1_xattn_all.items() if k in ('g1', 'b1', 'g2', 'b2', 'Wq', 'Wkv', 'Wout')}
    del _L1_xattn_all

    def _L1_ffn_setup():
        import math
        import jax, jax.numpy as jnp
        import numpy as np
        B, S, D, F, E = (8, 256, 128, 512, 8)
        CAPACITY_FACTOR = 1.0
        key = jax.random.key(seed)
        k1, k2, k3, k4 = jax.random.split(key, 4)
        x = jax.random.normal(k1, (B, S, D), dtype=jnp.float32)
        Wr = jax.random.normal(k2, (D, E), dtype=jnp.float32) * (1.0 / math.sqrt(D))
        W1 = jax.random.normal(k3, (E, D, F), dtype=jnp.float32) * (1.0 / math.sqrt(D))
        W2 = jax.random.normal(k4, (E, F, D), dtype=jnp.float32) * (1.0 / math.sqrt(F))
        return {'x': x, 'Wr': Wr, 'W1': W1, 'W2': W2}
    _L1_ffn_all = _L1_ffn_setup()
    _L1_ffn_in = {k: v for k, v in _L1_ffn_all.items() if k in ('Wr', 'W1', 'W2')}
    del _L1_ffn_all
    return {'x': x, 'ctx_1024': ctx_1024, 'mask_Bx16xSxS2_ff0': mask_Bx16xSxS2_ff0, 'L0_xattn_W_q': _L0_xattn_in['W_q'], 'L0_xattn_W_k': _L0_xattn_in['W_k'], 'L0_xattn_W_v': _L0_xattn_in['W_v'], 'L0_xattn_W_o': _L0_xattn_in['W_o'], 'L0_xattn_lambda_q1': _L0_xattn_in['lambda_q1'], 'L0_xattn_lambda_k1': _L0_xattn_in['lambda_k1'], 'L0_xattn_lambda_q2': _L0_xattn_in['lambda_q2'], 'L0_xattn_lambda_k2': _L0_xattn_in['lambda_k2'], 'L0_xattn_rms_scale': _L0_xattn_in['rms_scale'], 'L0_ffn_w1': _L0_ffn_in['w1'], 'L0_ffn_w2': _L0_ffn_in['w2'], 'L0_ffn_w3': _L0_ffn_in['w3'], 'L0_ffn_new_w1': _L0_ffn_in['new_w1'], 'L0_ffn_new_w2': _L0_ffn_in['new_w2'], 'L0_ffn_new_w3': _L0_ffn_in['new_w3'], 'L0_ffn_gate_weight': _L0_ffn_in['gate_weight'], 'L0_ffn_new_gate_weight': _L0_ffn_in['new_gate_weight'], 'L0_ffn_gate_bias': _L0_ffn_in['gate_bias'], 'L1_xattn_g1': _L1_xattn_in['g1'], 'L1_xattn_b1': _L1_xattn_in['b1'], 'L1_xattn_g2': _L1_xattn_in['g2'], 'L1_xattn_b2': _L1_xattn_in['b2'], 'L1_xattn_Wq': _L1_xattn_in['Wq'], 'L1_xattn_Wkv': _L1_xattn_in['Wkv'], 'L1_xattn_Wout': _L1_xattn_in['Wout'], 'L1_ffn_Wr': _L1_ffn_in['Wr'], 'L1_ffn_W1': _L1_ffn_in['W1'], 'L1_ffn_W2': _L1_ffn_in['W2']}

def reference(x, ctx_1024, mask_Bx16xSxS2_ff0, L0_xattn_W_q, L0_xattn_W_k, L0_xattn_W_v, L0_xattn_W_o, L0_xattn_lambda_q1, L0_xattn_lambda_k1, L0_xattn_lambda_q2, L0_xattn_lambda_k2, L0_xattn_rms_scale, L0_ffn_w1, L0_ffn_w2, L0_ffn_w3, L0_ffn_new_w1, L0_ffn_new_w2, L0_ffn_new_w3, L0_ffn_gate_weight, L0_ffn_new_gate_weight, L0_ffn_gate_bias, L1_xattn_g1, L1_xattn_b1, L1_xattn_g2, L1_xattn_b2, L1_xattn_Wq, L1_xattn_Wkv, L1_xattn_Wout, L1_ffn_Wr, L1_ffn_W1, L1_ffn_W2):
    import jax
    import jax.numpy as jnp

    def _L0_xattn_ref(query, key, value, attn_mask, W_q, W_k, W_v, W_o, lambda_q1, lambda_k1, lambda_q2, lambda_k2, rms_scale):
        import jax, jax.numpy as jnp
        import numpy as np
        B, S, D = (2, 256, 128)
        H = 16
        DH = D // H
        LAMBDA_INIT = 0.8
        EPS = 1e-05
        SCALE = 1.0 / np.sqrt(DH)
        b, s, _ = value.shape
        q = (query @ W_q).reshape(b, s, H, 2 * DH).transpose(0, 2, 1, 3)
        k = (key @ W_k).reshape(b, s, H, 2 * DH).transpose(0, 2, 1, 3)
        v = (value @ W_v).reshape(b, s, H, DH).transpose(0, 2, 1, 3)
        q1, q2 = (q[..., :DH], q[..., DH:])
        k1, k2 = (k[..., :DH], k[..., DH:])
        lam = jnp.exp(jnp.sum(lambda_q1 * lambda_k1, -1)) - jnp.exp(jnp.sum(lambda_q2 * lambda_k2, -1)) + LAMBDA_INIT
        lam = lam[None, :, None, None]
        s1 = jnp.einsum('bhqd,bhkd->bhqk', q1, k1) * SCALE + attn_mask
        s2 = jnp.einsum('bhqd,bhkd->bhqk', q2, k2) * SCALE + attn_mask
        attn = jax.nn.softmax(s1, axis=-1) - lam * jax.nn.softmax(s2, axis=-1)
        out = jnp.einsum('bhqk,bhkd->bhqd', attn, v)
        rms = jnp.sqrt(jnp.mean(out * out, axis=-1, keepdims=True) + EPS)
        out = out / rms * rms_scale
        out = out * (1.0 - LAMBDA_INIT)
        out = out.transpose(0, 2, 1, 3).reshape(b, s, H * DH)
        return out @ W_o

    def _L0_ffn_ref(x, w1, w2, w3, new_w1, new_w2, new_w3, gate_weight, new_gate_weight, gate_bias):
        import jax, jax.numpy as jnp
        import numpy as np
        TOP_K = 2
        ROUTE_SCALE = 1.0
        EPS = 1e-20
        bs, slen, dim = x.shape
        x_flat = x.reshape(-1, dim)
        ew1 = jnp.concatenate([w1, new_w1], axis=0)
        ew2 = jnp.concatenate([w2, new_w2], axis=0)
        ew3 = jnp.concatenate([w3, new_w3], axis=0)
        gate = jnp.concatenate([gate_weight, new_gate_weight], axis=0)
        e_orig = w1.shape[0]
        e_tot = gate.shape[0]
        bias = jnp.concatenate([jnp.zeros((e_orig,), x.dtype), gate_bias])
        scores = jax.nn.sigmoid((x_flat @ gate.T + bias).astype(jnp.float32))
        top_scores, selected = jax.lax.top_k(scores, TOP_K)
        top_scores = top_scores / (jnp.sum(top_scores, axis=-1, keepdims=True) + EPS)
        top_scores = top_scores * ROUTE_SCALE
        onehot = jax.nn.one_hot(selected, e_tot, dtype=jnp.float32)
        cw = jnp.einsum('tk,tke->te', top_scores, onehot)
        out = jnp.zeros_like(x_flat)
        for e in range(e_tot):
            h = jax.nn.silu(x_flat @ ew1[e].T) * (x_flat @ ew3[e].T)
            out = out + cw[:, e:e + 1] * (h @ ew2[e].T)
        return out.reshape(bs, slen, dim)

    def _L1_xattn_ref(x, latents, g1, b1, g2, b2, Wq, Wkv, Wout):
        import jax, jax.numpy as jnp
        import numpy as np
        DIM = 128
        HEADS = 16
        DIM_HEAD = 64
        INNER = HEADS * DIM_HEAD
        EPS = 1e-05

        def layer_norm(x, gamma, beta):
            mu = jnp.mean(x, axis=-1, keepdims=True)
            var = jnp.mean(jnp.square(x - mu), axis=-1, keepdims=True)
            return (x - mu) * jax.lax.rsqrt(var + EPS) * gamma + beta
        b, l, _ = latents.shape
        xn = layer_norm(x, g1, b1)
        ln = layer_norm(latents, g2, b2)
        q = ln @ Wq
        kv_input = jnp.concatenate([xn, ln], axis=1)
        kv = kv_input @ Wkv
        k, v = jnp.split(kv, 2, axis=-1)

        def heads(t):
            return t.reshape(t.shape[0], t.shape[1], HEADS, DIM_HEAD).transpose(0, 2, 1, 3)
        q, k, v = (heads(q), heads(k), heads(v))
        scale = 1.0 / np.sqrt(np.sqrt(DIM_HEAD))
        logits = jnp.einsum('bhqd,bhkd->bhqk', q * scale, k * scale)
        w = jax.nn.softmax(logits.astype(jnp.float32), axis=-1).astype(logits.dtype)
        out = jnp.einsum('bhqk,bhkd->bhqd', w, v)
        out = out.transpose(0, 2, 1, 3).reshape(b, l, INNER)
        return out @ Wout

    def _L1_ffn_ref(x, Wr, W1, W2):
        import math
        import jax, jax.numpy as jnp
        import numpy as np
        B, S, D, F, E = (8, 256, 128, 512, 8)
        CAPACITY_FACTOR = 1.0
        b, s, d = x.shape
        t = b * s
        cap = max(math.ceil(t * CAPACITY_FACTOR / E), 1)
        xf = x.reshape(t, d)
        probs = jax.nn.softmax(xf.astype(jnp.float32) @ Wr, axis=-1)
        eidx = jnp.argmax(probs, axis=-1)
        p_tok = jnp.take_along_axis(probs, eidx[:, None], axis=1)[:, 0]
        onehot = jax.nn.one_hot(eidx, E, dtype=jnp.int32)
        rank_all = jnp.cumsum(onehot, axis=0) - onehot
        rank = jnp.take_along_axis(rank_all, eidx[:, None], axis=1)[:, 0]
        keep = rank < cap
        slot = jnp.where(keep, rank, cap)
        dispatch = jnp.zeros((E, cap + 1), dtype=jnp.int32).at[eidx, slot].set(jnp.arange(t, dtype=jnp.int32))
        valid = jnp.zeros((E, cap + 1), dtype=bool).at[eidx, slot].set(keep)
        dispatch = dispatch[:, :cap]
        valid = valid[:, :cap]
        xe = xf[dispatch]
        h = jnp.maximum(jnp.einsum('ecd,edf->ecf', xe, W1), 0.0)
        ye = jnp.einsum('ecf,efd->ecd', h, W2)
        pe = p_tok[dispatch]
        ye = ye * (pe * valid.astype(ye.dtype))[:, :, None]
        y = jnp.zeros((t, d), dtype=x.dtype).at[dispatch.reshape(-1)].add(ye.reshape(E * cap, d).astype(x.dtype))
        return y.reshape(b, s, d)
    x = x + _L0_xattn_ref(_layernorm(x, axis=-1), ctx_1024, ctx_1024, mask_Bx16xSxS2_ff0, L0_xattn_W_q, L0_xattn_W_k, L0_xattn_W_v, L0_xattn_W_o, L0_xattn_lambda_q1, L0_xattn_lambda_k1, L0_xattn_lambda_q2, L0_xattn_lambda_k2, L0_xattn_rms_scale)
    x = x + _L0_ffn_ref(_layernorm(x, axis=-1), L0_ffn_w1, L0_ffn_w2, L0_ffn_w3, L0_ffn_new_w1, L0_ffn_new_w2, L0_ffn_new_w3, L0_ffn_gate_weight, L0_ffn_new_gate_weight, L0_ffn_gate_bias)
    x = x + _L1_xattn_ref(ctx_1024, _layernorm(x, axis=-1), L1_xattn_g1, L1_xattn_b1, L1_xattn_g2, L1_xattn_b2, L1_xattn_Wq, L1_xattn_Wkv, L1_xattn_Wout)
    x = x + _L1_ffn_ref(_layernorm(x, axis=-1), L1_ffn_Wr, L1_ffn_W1, L1_ffn_W2)
    return x

_drawn_inputs = setup_inputs


def setup_inputs(seed=0):
    import zlib

    import numpy as np

    out = dict(_drawn_inputs(seed))
    spreads = {'L0_xattn_rms_scale': (1.0, 0.6),
     'L0_ffn_new_w2': (0.0, 0.364),
     'L1_xattn_g1': (1.0, 0.2),
     'L1_xattn_b1': (0.0, 0.1),
     'L1_xattn_g2': (1.0, 0.2),
     'L1_xattn_b2': (0.0, 0.1)}
    factors = {'L0_xattn_W_q': 2.902,
     'L0_xattn_W_k': 4.178,
     'L0_xattn_lambda_q1': 5.58,
     'L0_xattn_lambda_k1': 6.273,
     'L0_xattn_lambda_q2': 5.733,
     'L0_xattn_lambda_k2': 8.0,
     'L0_ffn_w1': 3.449,
     'L0_ffn_w3': 2.906,
     'L0_ffn_new_w1': 3.299,
     'L0_ffn_new_gate_weight': 2.973}
    for name, (base, spread) in spreads.items():
        noise = np.random.default_rng([zlib.crc32(name.encode()), seed]).standard_normal(out[name].shape)
        drawn = base * np.exp(spread * noise) if base else spread * noise
        out[name] = jnp.asarray(drawn.astype(out[name].dtype))
    for name, factor in factors.items():
        out[name] = (out[name] * factor).astype(out[name].dtype)
    return out
```

```python
from contextlib import ExitStack

import numpy as np

import concourse.bass as bass
from concourse import mybir

F32 = mybir.dt.float32
R32 = mybir.dt.float32r
U32 = mybir.dt.uint32
ALU = mybir.AluOpType
ACT = mybir.ActivationFunctionType
X = mybir.AxisListType.X

P = 128
B, S, D = 8, 256, 128
T = B * S
NT = T // P
TB = S // P
LOWEST = -3.0e38

H0, DH0 = 16, 8
SLOTS = 2 * H0 // 4
UNITS = 2 * H0
LAMBDA_INIT = 0.8
EPS = 1e-5

E0, HID = 9, 352
HCH = [(0, 128), (128, 128), (256, 96)]
GT = 512
TPG = GT // P

H1, DH1 = 16, 64
INNER = H1 * DH1
KV = 2 * S
UNITS1 = H1 * TB
SCALE1 = float(1.0 / np.sqrt(np.sqrt(DH1)))

E1, F1 = 8, 512
CAP = T // E1


def at_least(eng, sem, value):
    if isinstance(value, int) and value <= 0:
        return
    eng.wait_ge(sem, value)


def hold(eng, sem, value, passed):
    if isinstance(value, int):
        at_least(eng, sem, value)
    else:
        eng.wait_ge(sem, value)
        eng.sem_inc(passed, 1)


class OwnSteps:

    def __init__(self, eng, sem):
        self.eng, self.sem, self.n, self.base = eng, sem, 0, 0

    def did(self, instruction):
        instruction.then_inc(self.sem, 1)
        self.n += 1

    def settle(self):
        self.eng.wait_ge(self.sem, self.base + self.n)

    def loop(self, register, first, per_turn):
        self.start = self.n
        self.per_turn = per_turn
        self.base = (register - first) * per_turn if first else register * per_turn

    def end_loop(self, turns):
        assert self.n - self.start == self.per_turn, (self.n - self.start, self.per_turn)
        self.n = self.start + turns * self.per_turn
        self.base = 0


def bc(ap, n):
    return ap.unsqueeze(len(ap.shape)).to_broadcast([*ap.shape, n])


def build(nc, a, out, upto="D"):
    with ExitStack() as ctx:
        def sb(name, shape, dt=F32):
            return ctx.enter_context(nc.sbuf_tensor(name, shape, dt))

        def bank(name):
            return ctx.enter_context(nc.psum_tensor(name, [P, 512], F32))

        def sem(name):
            return ctx.enter_context(nc.semaphore(name))

        x = sb("x", [P, NT, D])
        const = sb("const", [P, 2 * P + 2 + E0])
        ident = const[:, 0:P]
        before = const[:, P:2 * P]
        low_part = const[:, 2 * P:2 * P + 2]
        iota9 = const[:, 2 * P + 2:2 * P + 2 + E0]
        ctxT = sb("ctxT", [P, T])
        xnT = sb("xnT", [P, T])
        xmT = sb("xmT", [P, T])
        xcT = sb("xcT", [P, T])
        ffnw = sb("ffnw", [P, 2 * E0 * HID + 3 * E0 * D])
        w1T = ffnw[:, 0:E0 * HID]
        w3T = ffnw[:, E0 * HID:2 * E0 * HID]
        w2s = ffnw[:, 2 * E0 * HID:].rearrange("p (e c d) -> p e c d", e=E0, c=3)
        W1 = ffnw[:, 0:E1 * F1].rearrange("p (e f) -> p e f", e=E1)
        W2 = ffnw[:, E1 * F1:2 * E1 * F1].rearrange("p (e c d) -> p e c d", e=E1, d=D)
        wqk = sb("wqk", [P, 2, 2 * P])
        wqk4 = sb("wqk4", [P, 2, 32, 4, DH0])
        wvo = sb("wvo", [P, 2, P])
        Wq = sb("Wq", [P, INNER])
        Wkv = sb("Wkv", [P, 2 * INNER])
        Wout = sb("Wout", [P, INNER // P, D])
        qk = sb("qk", [P, SLOTS, 2 * S], R32)
        high = sb("high", [P, 2, 2 * S], R32)
        small = sb("small", [P, 1024])
        work = sb("work", [P, 14400])

        masks = work[:, 0:4096].rearrange("p (r h t k) -> p r h t k", r=4, h=2, t=TB)
        zs = work[:, 4096:6144].rearrange("p (r t k) -> p r t k", r=4, t=TB)
        probsT = work[:, 6144:8192].rearrange("p (r n) -> p r n", r=4)
        V0 = work[:, 8192:8192 + NT * H0 * 9].rearrange("p (t h c) -> p t h c", t=NT, c=9)
        at = 8192 + NT * H0 * 9
        o1 = work[:, at:at + 256]
        o2 = work[:, at + 256:at + 512]
        oT = work[:, at + 512:at + 768]
        lnw = work[:, at + 768:at + 768 + 512].rearrange("p (k t d) -> p k t d", k=2, t=TB)
        xnb = sb("xnb", [P, 2, TB, D])
        ctx_tok = work[:, 0:NT * D].rearrange("p (t d) -> p t d", t=NT)
        hs = work[:, 0:3072].rearrange("p (r c n) -> p r c n", r=2, c=3)
        sil = work[:, 3072:4096].rearrange("p (r n) -> p r n", r=2)
        c0 = 0
        def take(n):
            nonlocal c0
            c0 += n
            return work[:, c0 - n:c0]
        KT = take(1024).rearrange("p (r k) -> p r k", r=2)
        QT = take(512).rearrange("p (r q) -> p r q", r=2)
        V1 = take(4 * H1 * 65).rearrange("p (t h c) -> p t h c", t=4, c=65)
        O1 = take(TB * INNER).rearrange("p (t n) -> p t n", t=TB)
        OT = take(TB * INNER).rearrange("p (t c n) -> p t c n", t=TB, c=8)
        P1 = take(2048).rearrange("p (r k) -> p r k", r=4)
        P1T = take(2048).rearrange("p (r k) -> p r k", r=4)
        kvT = take(512)
        xn_tok = work[:, 0:2048].rearrange("p (t d) -> p t d", t=NT)
        xe = work[:, 2048:4096].rearrange("p (t d) -> p t d", t=NT)
        xeT = work[:, 4096:6144]
        h1 = work[:, 6144:8192].rearrange("p (r c n) -> p r c n", r=2, c=4)
        ye = work[:, 8192:10240].rearrange("p (t d) -> p t d", t=NT)
        yg = work[:, 12288:14336].rearrange("p (t d) -> p t d", t=NT)

        off = 0
        def tiny(n):
            nonlocal off
            off += n
            return small[:, off - n:off]
        rowmax = tiny(8).rearrange("p (r t) -> p r t", t=TB)
        negmax = tiny(8).rearrange("p (r t) -> p r t", t=TB)
        lam_in = sb("lam_in", [P, 4, H0 * DH0])
        lam = tiny(32).rearrange("p (k h) -> p k h", k=2)
        rms_w = tiny(DH0)
        rs = tiny(64).rearrange("p (t h s) -> p t h s", t=TB, s=2)
        ms = tiny(32)
        rr = tiny(32)
        minus_half = tiny(32)
        mean = tiny(2)
        var = tiny(2)
        rstd = tiny(2)
        g1b1 = tiny(4)
        bias9 = tiny(E0)
        gateT = tiny(E0)
        WrT = tiny(E1)
        nm1 = tiny(4)
        rc1 = tiny(4)
        big = sb("big", [P, 1024])
        boff = 0
        def mid(n):
            nonlocal boff
            boff += n
            return big[:, boff - n:boff]
        score9 = mid(NT * E0).rearrange("p (t e) -> p t e", e=E0)
        cw = mid(NT * E0).rearrange("p (t e) -> p t e", e=E0)
        tmp9 = mid(NT * E0).rearrange("p (t e) -> p t e", e=E0)
        top8 = mid(NT * 8).rearrange("p (t e) -> p t e", e=8)
        idx8 = sb("idx8", [P, NT, 8], U32)
        idx_f = mid(NT * 2).rearrange("p (k t) -> p k t", k=2)
        wk = mid(NT * 2).rearrange("p (k t) -> p k t", k=2)
        wsum = mid(NT)
        keep = mid(NT)
        slot_f = mid(NT)
        slot_i = sb("slot_i", [P, NT], mybir.dt.uint32)
        p_tok = mid(NT)
        zeros = sb("zeros", [P, 512])
        ones = sb("ones", [P, P])
        probs8 = mid(NT * E1).rearrange("p (t e) -> p t e", e=E1)
        oneh = sb("oneh", [P, NT, E1])
        sums = sb("sums", [P, 2, NT, E1])

        xe_dram = nc.dram_tensor("xe_scratch", [E1 * CAP, D], F32, kind="Internal").ap()
        ye_dram = nc.dram_tensor("ye_scratch", [E1 * CAP, D], F32, kind="Internal").ap()

        banks = [bank(f"bank{i}") for i in range(8)]
        SC, PT, PO, PROJ, FIN = banks[0:2], banks[2:4], banks[4:6], banks[6], banks[7]

        def sems(names):
            return [sem(n) for n in names.split()]

        const_in, x_in, ctx_in, ctxT_in, w0_in, lam_sem, small_in = sems("const_in x_in ctx_in ctxT_in w0_in lam_sem small_in")
        ffn_in, w1_in, w1e_in = sems("ffn_in w1_in w1e_in")
        mask_in = [sem(f"mask_in{r}") for r in range(4)]
        dve_own = sem("dve_own")
        passed_dve, passed_pool, passed_act = sems("passed_dve passed_pool passed_act")
        setup_done, wqk4_ready, lam_sum, lam_exp = sems("setup_done wqk4_ready lam_sum lam_exp")
        ln_var, ln_rstd = sems("ln_var ln_rstd")
        prep_norm, prep_turned, prep_copied = sems("prep_norm prep_turned prep_copied")
        v0_made, v0_copied = sems("v0_made v0_copied")
        proj_made, high_ready, stack_ready = sems("proj_made high_ready stack_ready")
        scores_made, rowmax_done, negmax_ready, shifted = sems("scores_made rowmax_done negmax_ready shifted")
        z_turned, probs_ready, pv_done, pv_read = sems("z_turned probs_ready pv_done pv_read")
        rms_in, rms_out, heads_ready, heads_turned, headsT_ready, wo_done = sems("rms_in rms_out heads_ready heads_turned headsT_ready wo_done")
        next_norm, next_turned, next_copied = sems("next_norm next_turned next_copied")
        gate_made, gate_biased, gate_sig, cw_ready = sems("gate_made gate_biased gate_sig cw_ready")
        up_made, silu_done, h_ready, down_made, acc_done = sems("up_made silu_done h_ready down_made acc_done")
        c_norm, c_turned, c_copied, kv_copied, v1_ones = sems("c_norm c_turned c_copied kv_copied v1_ones")
        v1_made, v1_act, v1_dve, k1_made, q1_made, k1_ready, q1_ready = sems("v1_made v1_act v1_dve k1_made q1_made k1_ready q1_ready")
        s1_made, nm1_ready, p1_ready, p1_turned, p1t_act, p1t_dve = sems("s1_made nm1_ready p1_ready p1_turned p1t_act p1t_dve")
        pv1_done, o1_ready, o1_part, ot_ready, out1_made, x3_ready = sems("pv1_done o1_ready o1_part ot_ready out1_made x3_ready")
        d_norm, d_turned, d_copied, r_made, r_shift, r_exp = sems("d_norm d_turned d_copied r_made r_shift r_exp")
        oh_ready, rank_made, slots_ready = sems("oh_ready rank_made slots_ready")
        zero_ready, zeroed, scattered, xe_in, xe_turned, xe_copied = sems("zero_ready zeroed scattered xe_in xe_turned xe_copied")
        h1_made, h1_act, h1_dve, y1_made, y1_copied, ye_out = sems("h1_made h1_act h1_dve y1_made y1_copied ye_out")
        yg_zero, gathered, y_ready, stored = sems("yg_zero gathered y_ready stored")

        LT, LE, LP = 3, 3, 5
        LX, LT1, LP1, LN1 = 1, 2, 4, 5

        out_rows = out.rearrange("(t p) d -> p t d", p=P)
        mask_rows = a["mask"].rearrange("n (t p) k -> p n t k", p=P)

        block = ctx.enter_context(nc.Block())

        def over_batches(eng, step, own=None, per_turn=0):
            step(0, True, False, True)
            with eng.Fori(1, B - 1) as b:
                if own:
                    own.loop(b, 1, per_turn)
                step(b, True, True, True)
            if own:
                own.end_loop(B - 2)
            step(B - 1, True, True, False)
            step(B, False, True, False)

        def lagged(b, u, lag, new, old, units):
            if u >= lag:
                return (b, u - lag) if new else None
            return (b - 1, u - lag + units) if old else None

        @block.sync
        def _(sp):
            def load(dst, src, s):
                sp.dma_start(dst, src).then_inc(s, 16)

            load(ctx_tok, a["ctx"].rearrange("(t p) d -> p t d", p=P), ctx_in)
            load(x[:, :, :], a["x"].rearrange("(t p) d -> p t d", p=P), x_in)
            load(wqk[:, 0, :], a["W_q"], w0_in)
            load(wqk[:, 1, :], a["W_k"], w0_in)
            load(wvo[:, 0, :], a["W_v"], w0_in)
            load(wvo[:, 1, :], a["W_o"], w0_in)
            load(ctxT[:, :], a["ctxT"], ctxT_in)

            sp.wait_ge(prep_norm, 2 * B)

            def step(b, new, old, more):
                if not new:
                    return
                for pair in range(H0 // 2):
                    at_least(sp, rowmax_done, 2 * UNITS * b + 8 * (pair - 3))
                    sp.dma_start(masks[:, pair % 4], mask_rows[:, bass.ds(b * H0 + 2 * pair, 2)]).then_inc(mask_in[pair % 4], 16)
                if isinstance(b, int) and b == 0:
                    load(w1T, a["w1T"], ffn_in)
                    load(w3T, a["w3T"], ffn_in)
                    for c, (h0, m) in enumerate(HCH):
                        load(w2s[0:m, :, c, :], a["w2T"][:, h0:h0 + m, :].rearrange("e p d -> p e d"), ffn_in)
                    load(Wq[:, :], a["Wq"], w1_in)
                    load(Wkv[:, :], a["Wkv"], w1_in)
                    load(Wout[:, :, :], a["Wout"].rearrange("(c p) d -> p c d", p=P), w1_in)
            over_batches(sp, step)

            if upto == "A":
                sp.wait_ge(next_norm, B)
                sp.wait_ge(ffn_in, 16)
            if upto >= "B":
                sp.wait_ge(acc_done, 2 * TPG + TPG * E0 * (T // GT))
            if upto >= "C":
                for e0 in (0, 4):
                    load(W1[:, e0:e0 + 4], a["W1"][e0:e0 + 4].rearrange("e d f -> d e f"), w1e_in)
                    for e in range(e0, e0 + 4):
                        load(W2[:, e], a["W2"][e].rearrange("(c p) d -> p c d", p=P), w1e_in)
                sp.wait_ge(x3_ready, B)
            if upto == "D":
                sp.wait_ge(scattered, 16 * NT)
                load(xe, xe_dram.rearrange("(t p) d -> p t d", p=P), xe_in)
                for e in range(E1):
                    sp.wait_ge(y1_copied, e + 1)
                    sp.dma_start(ye_dram.rearrange("(t p) d -> p t d", p=P)[:, 2 * e:2 * e + 2], ye[:, 2 * e:2 * e + 2, :]).then_inc(ye_out, 16)
                for q in range(4):
                    sp.wait_ge(y_ready, q + 1)
                    sp.dma_start(out_rows[:, 4 * q:4 * q + 4], x[:, 4 * q:4 * q + 4, :]).then_inc(stored, 16)
                sp.wait_ge(stored, 64)
            else:
                sp.dma_start(out_rows, x[:, :, :]).then_inc(stored, 16)
                sp.wait_ge(stored, 16)

        @block.gpsimd
        def _(pool):
            pool.memset(minus_half, -0.5).then_inc(setup_done, 1)
            pool.memset(bias9[:, 0:E0 - 1], 0.0).then_inc(setup_done, 1)
            pool.memset(V0[:, :, :, DH0:DH0 + 1], 1.0).then_inc(setup_done, 1)
            pool.memset(ones[:, :], 1.0).then_inc(setup_done, 1)
            pool.memset(zeros[:, :], 0.0).then_inc(zero_ready, 1)
            pool.dma_start(const[:, :], a["const"]).then_inc(const_in, 16)
            for n, name in enumerate(("lambda_q1", "lambda_k1", "lambda_q2", "lambda_k2")):
                pool.dma_start(lam_in[:, n, :], a[name].to_broadcast([P, H0 * DH0])).then_inc(lam_sem, 16)
            pool.dma_start(rms_w, a["rms_scale"].to_broadcast([P, DH0])).then_inc(lam_sem, 16)
            for n, name in enumerate(("g1", "b1", "g2", "b2")):
                pool.dma_start(g1b1[:, n:n + 1], a[name]).then_inc(small_in, 16)
            pool.dma_start(bias9[:, E0 - 1:E0], a["gate_bias"].to_broadcast([P, 1])).then_inc(small_in, 16)
            pool.dma_start(gateT, a["gateT"]).then_inc(small_in, 16)
            pool.dma_start(WrT, a["Wr"]).then_inc(small_in, 16)
            pool.wait_ge(zero_ready, 1)
            for q in range(4):
                pool.dma_start(xe_dram.rearrange("(p t) d -> p (t d)", p=P)[:, 512 * q:512 * q + 512], zeros[:, :]).then_inc(zeroed, 16)

            def inverse_root(n):
                pool.wait_ge(ln_var, n)
                pool.tensor_tensor(rstd, var, minus_half[:, 0:2], ALU.pow).then_inc(ln_rstd, 1)

            pool.wait_ge(setup_done, 4)
            with pool.Fori(0, B) as b:
                inverse_root(b * 2 + 1)
                inverse_root(b * 2 + 2)

            def step(b, new, old, more):
                for u in range(UNITS):
                    if new:
                        hold(pool, negmax_ready, UNITS * b + u + 1, passed_pool)
                        for t in range(TB):
                            pool.tensor_scalar(zs[:, u % 4, t, :], zs[:, u % 4, t, :], negmax[:, u % 4, t:t + 1], 1.0,
                                               ALU.add, ALU.mult).then_inc(shifted, 1)
                    if old and u == 6:
                        pool.wait_ge(rms_in, b)
                        pool.tensor_tensor(rr, ms, minus_half, ALU.pow).then_inc(rms_out, 1)
                    if old and u == 16:
                        inverse_root(2 * B + b)
            over_batches(pool, step)

            if upto >= "C":
                with pool.Fori(0, B) as b:
                    inverse_root(3 * B + 2 * b + 1)
                    inverse_root(3 * B + 2 * b + 2)

                def copy_kv(b):
                    pool.tensor_copy(kvT[:, 0:S], xcT[:, bass.ds(b * S, S)]).then_inc(kv_copied, 1)
                    pool.tensor_copy(kvT[:, S:KV], xnT[:, bass.ds(b * S, S)]).then_inc(kv_copied, 1)
                pool.wait_ge(c_copied, B + 1)
                copy_kv(0)
                pool.memset(V1[:, :, :, DH1:DH1 + 1], 1.0).then_inc(v1_ones, 1)
                with pool.Fori(1, B) as b:
                    hold(pool, v1_made, 8 * b, passed_pool)
                    copy_kv(b)
            if upto == "D":
                with pool.Fori(0, B) as b:
                    inverse_root(5 * B + b + 1)
                pool.memset(yg, 0.0).then_inc(yg_zero, 1)
                pool.wait_ge(slots_ready, 1)
                pool.wait_ge(d_norm, B)
                pool.wait_ge(zeroed, 64)
                for t in range(NT):
                    pool.indirect_dma_start(xe_dram, bass.IndirectOffsetOnAxis(slot_i[:, t:t + 1], 0), xn_tok[:, t, :], None,
                                            bounds_check=E1 * CAP - 1, oob_is_err=False).then_inc(scattered, 16)
                pool.wait_ge(yg_zero, 1)
                pool.wait_ge(ye_out, 16 * E1)
                for t in range(NT):
                    pool.indirect_dma_start(yg[:, t, :], None, ye_dram, bass.IndirectOffsetOnAxis(slot_i[:, t:t + 1], 0),
                                            bounds_check=E1 * CAP - 1, oob_is_err=False).then_inc(gathered, 16)

        @block.vector
        def _(dve):
            own = OwnSteps(dve, dve_own)
            did, settle = own.did, own.settle

            def normalise(src, dst, n, done, wait_dst=None):
                did(dve.tensor_reduce(mean, src, X, ALU.add))
                settle()
                did(dve.tensor_scalar(mean, mean, 1.0 / D, None, ALU.mult))
                settle()
                did(dve.tensor_tensor(lnw[:, 0], src, bc(mean, D), ALU.subtract))
                settle()
                did(dve.tensor_tensor(lnw[:, 1], lnw[:, 0], lnw[:, 0], ALU.mult))
                settle()
                did(dve.tensor_reduce(var, lnw[:, 1], X, ALU.add))
                settle()
                dve.tensor_scalar(var, var, 1.0 / D, EPS, ALU.mult, ALU.add).then_inc(ln_var, 1)
                if wait_dst is not None:
                    dve.wait_ge(*wait_dst)
                dve.wait_ge(ln_rstd, n)
                dve.tensor_tensor(dst, lnw[:, 0], bc(rstd, D), ALU.mult).then_inc(done, 1)

            dve.wait_ge(w0_in, 64)
            for k, scale in enumerate((float(1.0 / np.sqrt(DH0)), 1.0)):
                dve.tensor_scalar(wqk4[:, k], wqk[:, k, :].rearrange("p (i d) -> p i d", d=DH0).unsqueeze(2).to_broadcast([P, 32, 4, DH0]),
                                  scale, None, ALU.mult).then_inc(wqk4_ready, 1)
            dve.wait_ge(lam_sem, 80)
            for k in range(2):
                did(dve.tensor_tensor(lam_in[:, 2 * k, :], lam_in[:, 2 * k, :], lam_in[:, 2 * k + 1, :], ALU.mult))
                settle()
                dve.tensor_reduce(lam[:, k, :], lam_in[:, 2 * k, :].rearrange("p (h d) -> p h d", d=DH0), X, ALU.add).then_inc(lam_sum, 1)
            dve.wait_ge(lam_exp, 1)
            did(dve.tensor_tensor(lam[:, 0, :], lam[:, 0, :], lam[:, 1, :], ALU.subtract))
            settle()
            did(dve.tensor_scalar(lam[:, 0, :], lam[:, 0, :], LAMBDA_INIT, None, ALU.add))
            did(dve.tensor_scalar(rms_w, rms_w, 1.0 - LAMBDA_INIT, None, ALU.mult))
            settle()
            dve.wait_ge(setup_done, 4)
            for g in range(4):
                dve.wait_ge(v0_made, g + 1)
                dve.tensor_copy(V0[:, 4 * g:4 * g + 4, :, 0:DH0], banks[g][:, :].rearrange("p (t h d) -> p t h d", t=4, d=DH0)).then_inc(v0_copied, 1)
            dve.wait_ge(x_in, 16)
            dve.wait_ge(ctx_in, 16)
            with dve.Fori(0, B) as b:
                own.loop(b, 0, 10)
                normalise(x[:, bass.ds(b * TB, TB), :], xnb[:, 0], b * 2 + 1, prep_norm, (prep_turned, 2 * b + 1))
                normalise(ctx_tok[:, bass.ds(b * TB, TB), :], xnb[:, 1], b * 2 + 2, prep_norm, (prep_turned, 2 * b + 2))
            own.end_loop(B)

            def split(b, sl):
                dve.wait_ge(high_ready, SLOTS * b + sl + 1)
                for k in range(2):
                    half = slice(k * S, (k + 1) * S)
                    dve.scalar_tensor_tensor(out=qk[:, sl, half], in0=high[:, sl % 2, half].bitcast(F32), scalar=low_part[:, k:k + 1],
                                             in1=PROJ[:, half], op0=ALU.mult, op1=ALU.add).then_inc(stack_ready, 1)

            dve.wait_ge(const_in, 16)
            for sl in range(SLOTS):
                split(0, sl)

            def step(b, new, old, more):
                for u in range(UNITS):
                    if new:
                        U = UNITS * b + u
                        if u % 4 == 0:
                            dve.wait_ge(mask_in[(u // 4) % 4], 16 * (2 * b + u // 16 + 1))
                        at_least(dve, z_turned, U - 3)
                        hold(dve, scores_made, U + 1, passed_dve)
                        for t in range(TB):
                            dve.tensor_tensor_reduce(zs[:, u % 4, t, :], SC[u % 2][:, t * S:(t + 1) * S], masks[:, (u // 4) % 4, (u // 2) % 2, t, :],
                                                     1.0, LOWEST, ALU.add, ALU.max, rowmax[:, u % 4, t:t + 1]).then_inc(rowmax_done, 1)
                        dve.wait_ge(rowmax_done, 2 * U + 2)
                        dve.tensor_scalar(negmax[:, u % 4, :], rowmax[:, u % 4, :], -1.0, None, ALU.mult).then_inc(negmax_ready, 1)
                        if more and u % 4 == 3:
                            split(b + 1, u // 4)
                    if old and u == 5:
                        dve.wait_ge(pv_done, UNITS * b)
                        po = [PO[t][:, 0:UNITS * 9].rearrange("p (h s c) -> p h s c", s=2, c=9) for t in range(TB)]
                        for t in range(TB):
                            did(dve.reciprocal(rs[:, t], po[t][:, :, :, DH0]))
                        settle()
                        for t in range(TB):
                            did(dve.tensor_tensor(rs[:, t, :, 1], rs[:, t, :, 1], lam[:, 0, :], ALU.mult))
                        settle()
                        for k, o in enumerate((o1, o2)):
                            for t in range(TB):
                                i = dve.tensor_tensor(o[:, t * P:(t + 1) * P].rearrange("p (h d) -> p h d", d=DH0), po[t][:, :, k, 0:DH0],
                                                      bc(rs[:, t, :, k], DH0), ALU.mult)
                                if (k, t) == (1, 1):
                                    i.then_inc(pv_read, 1)
                                else:
                                    did(i)
                        dve.wait_ge(pv_read, b)
                        did(dve.tensor_tensor(o1, o1, o2, ALU.subtract))
                        settle()
                        did(dve.tensor_tensor(o2, o1, o1, ALU.mult))
                        settle()
                        did(dve.tensor_reduce(ms, o2.rearrange("p (h d) -> p h d", d=DH0), X, ALU.add))
                        settle()
                        dve.tensor_scalar(ms, ms, 1.0 / DH0, EPS, ALU.mult, ALU.add).then_inc(rms_in, 1)
                    if old and u == 7:
                        dve.wait_ge(rms_out, b)
                        oh = o1.rearrange("p (h d) -> p h d", d=DH0)
                        did(dve.tensor_tensor(oh, oh, bc(rr, DH0), ALU.mult))
                        settle()
                        dve.tensor_tensor(oh, oh, rms_w.unsqueeze(1).to_broadcast([P, 32, DH0]), ALU.mult).then_inc(heads_ready, 1)
                    if old and u == 16:
                        dve.wait_ge(wo_done, b)
                        xb = x[:, bass.ds((b - 1) * TB, TB), :]
                        did(dve.tensor_tensor(xb, FIN[:, S:2 * S].rearrange("p (t d) -> p t d", t=TB), xb, ALU.add))
                        hold(dve, dve_own, own.base + own.n, passed_dve)
                        normalise(xb, xnb[:, 0], 2 * B + b, next_norm)
            over_batches(dve, step, own, 17)

            if upto >= "B":
                dve.wait_ge(gate_made, 1)
                dve.wait_ge(small_in, 112)
                gate = banks[0][:, 0:NT * E0].rearrange("p (t e) -> p t e", e=E0)
                dve.tensor_tensor(score9, gate, bias9.unsqueeze(1).to_broadcast([P, NT, E0]), ALU.add).then_inc(gate_biased, 1)
                dve.wait_ge(gate_sig, 1)
                for t in range(NT):
                    did(dve.max(top8[:, t, :], score9[:, t, :]))
                settle()
                for t in range(NT):
                    did(dve.max_index(idx8[:, t, :], top8[:, t, :], score9[:, t, :]))
                settle()
                did(dve.tensor_copy(idx_f, idx8[:, :, 0:2].rearrange("p t k -> p k t")))
                did(dve.tensor_tensor(wsum, top8[:, :, 0], top8[:, :, 1], ALU.add))
                settle()
                did(dve.tensor_scalar(wsum, wsum, 1e-20, None, ALU.add))
                settle()
                did(dve.reciprocal(wsum, wsum))
                settle()
                did(dve.tensor_tensor(wk, top8[:, :, 0:2].rearrange("p t k -> p k t"), wsum.unsqueeze(1).to_broadcast([P, 2, NT]), ALU.mult))
                iota = iota9.unsqueeze(1).to_broadcast([P, NT, E0])
                did(dve.tensor_tensor(cw, iota, bc(idx_f[:, 0], E0), ALU.is_equal))
                did(dve.tensor_tensor(tmp9, iota, bc(idx_f[:, 1], E0), ALU.is_equal))
                settle()
                did(dve.tensor_tensor(cw, cw, bc(wk[:, 0], E0), ALU.mult))
                did(dve.tensor_tensor(tmp9, tmp9, bc(wk[:, 1], E0), ALU.mult))
                settle()
                did(dve.tensor_tensor(cw, cw, tmp9, ALU.add))
                settle()

                with dve.Fori(0, T // GT // 2) as gg:
                    def add_expert(i):
                        G, e = divmod(i, E0)
                        N = gg * 2 * E0 + i
                        dve.wait_ge(acc_done, 2 * TPG + TPG * N)
                        dve.wait_ge(down_made, N + 1)
                        for t in range(TPG):
                            tile = gg * 2 * TPG + G * TPG + t
                            xt = x[:, bass.ds(tile, 1), :].rearrange("p a d -> p (a d)")
                            w = cw[:, bass.ds(tile, 1), e:e + 1].rearrange("p a e -> p (a e)")
                            dve.scalar_tensor_tensor(out=xt, in0=banks[4 + i % 2][:, t * P:(t + 1) * P], scalar=w,
                                                     in1=xt, op0=ALU.mult, op1=ALU.add).then_inc(acc_done, 1)
                    for i in range(2 * E0):
                        for c, (_, m) in enumerate(HCH):
                            k = i * 3 + c
                            dve.wait_ge(silu_done, gg * 54 + k + 1)
                            dve.tensor_tensor(hs[0:m, i % 2, c, :], banks[2 + k % 2][0:m, :], sil[0:m, k % 2, :], ALU.mult).then_inc(h_ready, 1)
                        if i > 0:
                            add_expert(i - 1)
                    add_expert(2 * E0 - 1)
                dve.wait_ge(acc_done, 2 * TPG + TPG * E0 * (T // GT))

            if upto >= "C":
                with dve.Fori(0, B) as b:
                    own.loop(b, 0, 11)
                    normalise(x[:, bass.ds(b * TB, TB), :], xnb[:, 0], 3 * B + 2 * b + 1, dve_own)
                    own.n += 1
                    settle()
                    normalise(xnb[:, 0], xnb[:, 1], 3 * B + 2 * b + 2, c_norm, (c_turned, b + 1))
                own.end_loop(B)

                def q_out(n, c):
                    dve.wait_ge(q1_made, n + 1)
                    dve.tensor_scalar(QT[:, c % 2, :], banks[7][:, 0:S], SCALE1, None, ALU.mult).then_inc(q1_ready, 1)

                q_out(0, 0)

                def step(b, new, old, more):
                    for u in range(UNITS1):
                        if new:
                            dve.wait_ge(s1_made, UNITS1 * b + u + 1)
                            dve.tensor_reduce(nm1[:, u % 4:u % 4 + 1], banks[u % 2][:, :], X, ALU.max, negate=True).then_inc(nm1_ready, 1)
                        unit = lagged(b, u, LT1, new, old, UNITS1)
                        if unit and unit[1] % 2 == 0:
                            bv, v = unit
                            dve.wait_ge(p1_turned, UNITS1 * bv + v + 1)
                            at_least(dve, pv1_done, UNITS1 * bv + v - 3)
                            dve.tensor_copy(P1T[:, v % 4, :], banks[2 + v % 2][:, :]).then_inc(p1t_dve, 1)
                        unit = lagged(b, u, LN1, new, old, UNITS1)
                        if unit:
                            bv, v = unit
                            h, t = divmod(v, TB)
                            dve.wait_ge(pv1_done, UNITS1 * bv + v + 1)
                            did(dve.reciprocal(rc1[:, v % 4:v % 4 + 1], banks[4 + v % 2][:, DH1:DH1 + 1]))
                            if v == 0 and old:
                                dve.wait_ge(o1_part, 4 * b)
                            settle()
                            dve.tensor_scalar(O1[:, t, h * DH1:(h + 1) * DH1], banks[4 + v % 2][:, 0:DH1], rc1[:, v % 4:v % 4 + 1], None,
                                              ALU.mult).then_inc(o1_ready, 1)
                        if new and u == 4:
                            for tt in range(4):
                                dve.wait_ge(v1_made, 8 * b + 2 * tt + 2)
                                dve.tensor_copy(V1[:, tt, 8:16, 0:DH1], banks[7][:, :].rearrange("p (h d) -> p h d", d=DH1)).then_inc(v1_dve, 1)
                        if new and u % 4 == 3 and (u < UNITS1 - 1 or more):
                            q_out(8 * b + u // 4 + 1, (u // 4 + 1) % 8)
                        if old and u == 6:
                            dve.wait_ge(out1_made, b)
                            xb = x[:, bass.ds((b - 1) * TB, TB), :]
                            dve.tensor_tensor(xb, banks[6][:, 0:TB * D].rearrange("p (t d) -> p t d", t=TB), xb, ALU.add).then_inc(x3_ready, 1)
                over_batches(dve, step, own, 32)
                dve.wait_ge(x3_ready, B)

            if upto == "D":
                with dve.Fori(0, B) as b:
                    own.loop(b, 0, 5)
                    normalise(x[:, bass.ds(b * TB, TB), :], xn_tok[:, bass.ds(b * TB, TB), :], 5 * B + b + 1, d_norm)
                own.end_loop(B)
                dve.wait_ge(r_made, 1)
                logits = banks[4][:, 0:NT * E1].rearrange("p (t e) -> p t e", e=E1)
                did(dve.tensor_reduce(wsum, logits, X, ALU.max))
                settle()
                dve.tensor_tensor(probs8, logits, bc(wsum, E1), ALU.subtract).then_inc(r_shift, 1)
                dve.wait_ge(r_exp, 1)
                did(dve.tensor_reduce(wsum, probs8, X, ALU.add))
                settle()
                did(dve.reciprocal(wsum, wsum))
                settle()
                did(dve.tensor_tensor(probs8, probs8, bc(wsum, E1), ALU.mult))
                settle()
                for t in range(NT):
                    did(dve.max(top8[:, t, :], probs8[:, t, :]))
                settle()
                for t in range(NT):
                    did(dve.max_index(idx8[:, t, :], top8[:, t, :], probs8[:, t, :]))
                settle()
                did(dve.tensor_copy(idx_f[:, 0], idx8[:, :, 0]))
                settle()
                dve.tensor_tensor(oneh[:, :, :], iota9[:, 0:E1].unsqueeze(1).to_broadcast([P, NT, E1]), bc(idx_f[:, 0], E1), ALU.is_equal).then_inc(oh_ready, 1)
                dve.wait_ge(rank_made, 1)
                tile_rank = banks[5][:, 0:NT * E1].rearrange("p (t e) -> p t e", e=E1)
                totals = banks[5][:, NT * E1:2 * NT * E1].rearrange("p (t e) -> p t e", e=E1)
                did(dve.tensor_copy(sums[:, 0], totals))
                settle()
                cur = 0
                for d in (1, 2, 4, 8):
                    did(dve.tensor_tensor(sums[:, 1 - cur, d:, :], sums[:, cur, d:, :], sums[:, cur, 0:NT - d, :], ALU.add))
                    did(dve.tensor_copy(sums[:, 1 - cur, 0:d, :], sums[:, cur, 0:d, :]))
                    settle()
                    cur = 1 - cur
                did(dve.tensor_tensor(sums[:, 1 - cur], tile_rank, sums[:, cur], ALU.add))
                settle()
                did(dve.tensor_tensor(sums[:, cur], totals, sums[:, 1 - cur], ALU.subtract))
                settle()
                did(dve.tensor_tensor(sums[:, 1 - cur], sums[:, cur], oneh[:, :, :], ALU.mult))
                settle()
                did(dve.tensor_reduce(keep, sums[:, 1 - cur], X, ALU.add, negate=True))
                settle()
                did(dve.tensor_scalar(slot_f, idx_f[:, 0], float(CAP), None, ALU.mult))
                settle()
                did(dve.tensor_tensor(slot_f, slot_f, keep, ALU.add))
                did(dve.tensor_scalar(keep, keep, float(CAP), float(E1 * CAP), ALU.is_ge, ALU.mult))
                settle()
                did(dve.tensor_tensor(slot_f, slot_f, keep, ALU.add))
                settle()
                dve.tensor_copy(slot_i[:, :], slot_f).then_inc(slots_ready, 1)
                for i in range(2 * E1):
                    if i % 2 == 1:
                        dve.wait_ge(h1_made, i + 1)
                        e = i // 2
                        if e >= 2:
                            dve.wait_ge(y1_made, e - 1)
                        dve.tensor_scalar(h1[:, e % 2, 2:4, :], banks[4 + i % 2][:, :].rearrange("p (c n) -> p c n", c=2), 0.0, None,
                                          ALU.max).then_inc(h1_dve, 1)
                dve.wait_ge(gathered, 16 * NT)
                for q in range(4):
                    g = yg[:, 4 * q:4 * q + 4, :]
                    did(dve.tensor_tensor(g, g, bc(top8[:, 4 * q:4 * q + 4, 0], D), ALU.mult))
                    settle()
                    dve.tensor_tensor(x[:, 4 * q:4 * q + 4, :], x[:, 4 * q:4 * q + 4, :], g, ALU.add).then_inc(y_ready, 1)

        @block.scalar
        def _(act):
            act.sem_inc(prep_copied, 1)
            act.sem_inc(next_copied, 1)
            act.sem_inc(c_copied, 1)
            act.wait_ge(lam_sum, 2)
            act.activation(lam[:, :, :], lam[:, :, :], ACT.Exp).then_inc(lam_exp, 1)
            act.wait_ge(small_in, 112)
            with act.Fori(0, B) as b:
                hold(act, prep_turned, 2 + 2 * b + 1, passed_act)
                act.activation(xnT[:, bass.ds(b * S, S)], banks[4][:, 0:S], ACT.Copy).then_inc(prep_copied, 1)
                hold(act, prep_turned, 2 + 2 * b + 2, passed_act)
                act.activation(xcT[:, bass.ds(b * S, S)], banks[5][:, 0:S], ACT.Identity, bias=g1b1[:, 1:2], scale=g1b1[:, 0:1]).then_inc(prep_copied, 1)

            def high_parts(b, sl):
                n = SLOTS * b + sl
                act.wait_ge(proj_made, n + 1)
                at_least(act, stack_ready, 2 * (n - 1))
                act.activation(high[:, sl % 2, :], PROJ[:, :], ACT.Copy).then_inc(high_ready, 1)

            for sl in range(SLOTS):
                high_parts(0, sl)

            def step(b, new, old, more):
                for u in range(UNITS):
                    unit = lagged(b, u, LE, new, old, UNITS)
                    if unit:
                        bv, v = unit
                        V = UNITS * bv + v
                        act.wait_ge(z_turned, V + 1)
                        at_least(act, pv_done, V - 3)
                        act.activation(probsT[:, v % 4, :], PT[v % 2][:, :], ACT.Exp).then_inc(probs_ready, 1)
                    if more and u % 4 == 3:
                        high_parts(b + 1, u // 4)
                    if old and u == 10:
                        act.wait_ge(heads_turned, b)
                        act.activation(oT, FIN[:, 0:S], ACT.Copy).then_inc(headsT_ready, 1)
                    if old and u == 21:
                        hold(act, next_turned, b, passed_act)
                        act.activation(xmT[:, bass.ds((b - 1) * S, S)], FIN[:, 0:S], ACT.Copy).then_inc(next_copied, 1)
            over_batches(act, step)

            if upto >= "B":
                act.wait_ge(gate_biased, 1)
                act.activation(score9, score9, ACT.Sigmoid).then_inc(gate_sig, 1)
                with act.Fori(0, T // GT // 2) as gg:
                    for i in range(2 * E0):
                        for c, (_, m) in enumerate(HCH):
                            k = i * 3 + c
                            act.wait_ge(up_made, gg * 54 + k + 1)
                            act.wait_ge(h_ready, gg * 54 + k + 1)
                            act.activation(sil[0:m, k % 2, :], banks[k % 2][0:m, :], ACT.Silu).then_inc(silu_done, 1)
            if upto >= "C":
                with act.Fori(0, B) as b:
                    hold(act, c_turned, b + 2, passed_act)
                    act.activation(xnT[:, bass.ds(b * S, S)], banks[6][:, 0:S], ACT.Identity, bias=g1b1[:, 3:4], scale=g1b1[:, 2:3]).then_inc(c_copied, 1)

                def k_out(n, c):
                    act.wait_ge(k1_made, n + 1)
                    act.activation(KT[:, c % 2, :], banks[6][:, :], ACT.Copy, scale=SCALE1).then_inc(k1_ready, 1)

                k_out(0, 0)

                def step(b, new, old, more):
                    for u in range(UNITS1):
                        unit = lagged(b, u, LX, new, old, UNITS1)
                        if unit:
                            bv, v = unit
                            V = UNITS1 * bv + v
                            act.wait_ge(nm1_ready, V + 1)
                            at_least(act, p1_turned, V - 3)
                            act.activation(P1[:, v % 4, :], banks[v % 2][:, :], ACT.Exp, bias=nm1[:, v % 4:v % 4 + 1]).then_inc(p1_ready, 1)
                        unit = lagged(b, u, LT1, new, old, UNITS1)
                        if unit and unit[1] % 2 == 1:
                            bv, v = unit
                            act.wait_ge(p1_turned, UNITS1 * bv + v + 1)
                            at_least(act, pv1_done, UNITS1 * bv + v - 3)
                            act.activation(P1T[:, v % 4, :], banks[2 + v % 2][:, :], ACT.Copy).then_inc(p1t_act, 1)
                        if new and u == 4:
                            for tt in range(4):
                                act.wait_ge(v1_made, 8 * b + 2 * tt + 1)
                                act.activation(V1[:, tt, 0:8, 0:DH1], banks[6][:, :].rearrange("p (h d) -> p h d", d=DH1), ACT.Copy).then_inc(v1_act, 1)
                        if old and u == 5:
                            for f in range(4):
                                act.wait_ge(o1_part, 4 * (b - 1) + f + 1)
                                act.activation(OT[:, f // 2, 4 * (f % 2):4 * (f % 2) + 4, :], banks[6 + f % 2][:, :].rearrange("p (c n) -> p c n", c=4),
                                               ACT.Copy).then_inc(ot_ready, 1)
                        if new and u % 4 == 3 and (u < UNITS1 - 1 or more):
                            k_out(8 * b + u // 4 + 1, (u // 4 + 1) % 8)
                over_batches(act, step)
            if upto == "D":
                for g in range(4):
                    act.wait_ge(d_turned, g + 1)
                    act.activation(xmT[:, g * 512:(g + 1) * 512], banks[g][:, :], ACT.Copy).then_inc(d_copied, 1)
                act.wait_ge(r_shift, 1)
                act.activation(probs8, probs8, ACT.Exp).then_inc(r_exp, 1)
                for g in range(4):
                    act.wait_ge(xe_turned, g + 1)
                    act.activation(xeT[:, g * 512:(g + 1) * 512], banks[g][:, :], ACT.Copy).then_inc(xe_copied, 1)
                for i in range(2 * E1):
                    e = i // 2
                    if i % 2 == 0:
                        act.wait_ge(h1_made, i + 1)
                        if e >= 2:
                            act.wait_ge(y1_made, e - 1)
                        act.activation(h1[:, e % 2, 0:2, :], banks[4 + i % 2][:, :].rearrange("p (c n) -> p c n", c=2), ACT.Relu).then_inc(h1_act, 1)
                    elif e >= 1:
                        act.wait_ge(y1_made, e)
                        act.activation(ye[:, 2 * (e - 1):2 * e, :], banks[6 + (e - 1) % 2][:, 0:2 * D].rearrange("p (t d) -> p t d", t=2), ACT.Copy).then_inc(y1_copied, 1)
                act.wait_ge(y1_made, E1)
                act.activation(ye[:, 2 * (E1 - 1):2 * E1, :], banks[6 + (E1 - 1) % 2][:, 0:2 * D].rearrange("p (t d) -> p t d", t=2), ACT.Copy).then_inc(y1_copied, 1)

        @block.tensor
        def _(pe):
            mm = pe.matmul
            pe.sem_inc(prep_turned, 2)
            pe.sem_inc(c_turned, 1)
            pe.wait_ge(ctxT_in, 16)
            pe.wait_ge(w0_in, 64)
            for t in range(NT):
                i = mm(banks[t // 4][:, (t % 4) * P:(t % 4 + 1) * P], ctxT[:, t * P:(t + 1) * P], wvo[:, 0, :], start=True, stop=True)
                if t % 4 == 3:
                    i.then_inc(v0_made, 1)
            pe.wait_ge(const_in, 16)

            def turn(dst, src):
                return pe.transpose(dst, src, ident)

            with pe.Fori(0, B) as b:
                pe.wait_ge(prep_copied, 2 * b + 1)
                for k in range(2):
                    pe.wait_ge(prep_norm, 2 * b + k + 1)
                    for t in range(TB):
                        i = turn(banks[4 + k][:, t * P:(t + 1) * P], xnb[:, k, t, :])
                    i.then_inc(prep_turned, 1)

            def project(b, sl):
                n = SLOTS * b + sl
                at_least(pe, stack_ready, 2 * n)
                mm(PROJ[:, 0:S], wqk4[:, 0, 4 * sl:4 * sl + 4].rearrange("p i r d -> p (i r d)"), xnT[:, bass.ds(b * S, S)], start=True, stop=True)
                mm(PROJ[:, S:2 * S], wqk4[:, 1, 4 * sl:4 * sl + 4].rearrange("p i r d -> p (i r d)"), ctxT[:, bass.ds(b * S, S)],
                   start=True, stop=True).then_inc(proj_made, 1)

            pe.wait_ge(wqk4_ready, 2)
            pe.wait_ge(v0_copied, 4)
            pe.wait_ge(prep_copied, 2 * B + 1)
            for sl in range(SLOTS):
                project(0, sl)

            def step(b, new, old, more):
                for u in range(UNITS):
                    if new:
                        U = UNITS * b + u
                        sl, j = divmod(u, 4)
                        if j == 0:
                            pe.wait_ge(stack_ready, 2 * (SLOTS * b + sl + 1))
                        at_least(pe, rowmax_done, 2 * (U - 1))
                        rows = slice(32 * j, 32 * j + 32)
                        for t in range(TB):
                            i = mm(SC[u % 2][:, t * S:(t + 1) * S], qk[rows, sl, t * P:(t + 1) * P], qk[rows, sl, S:2 * S], start=True, stop=True)
                        i.then_inc(scores_made, 1)
                    unit = lagged(b, u, LT, new, old, UNITS)
                    if unit:
                        bv, v = unit
                        V = UNITS * bv + v
                        pe.wait_ge(shifted, 2 * V + 2)
                        at_least(pe, probs_ready, V - 1)
                        for kt in range(TB):
                            for t in range(TB):
                                i = turn(PT[v % 2][:, (2 * kt + t) * P:(2 * kt + t + 1) * P], zs[:, v % 4, t, kt * P:(kt + 1) * P])
                        i.then_inc(z_turned, 1)
                    unit = lagged(b, u, LP, new, old, UNITS)
                    if unit:
                        bv, v = unit
                        pe.wait_ge(probs_ready, UNITS * bv + v + 1)
                        if v == 0:
                            at_least(pe, pv_read, bv)
                        for t in range(TB):
                            for kt in range(TB):
                                i = mm(PO[t][:, v * 9:(v + 1) * 9], probsT[:, v % 4, (2 * kt + t) * P:(2 * kt + t + 1) * P],
                                       V0[:, bass.ds(bv * TB + kt, 1), v // 2, :].rearrange("p a c -> p (a c)"), start=(kt == 0), stop=(kt == TB - 1))
                        i.then_inc(pv_done, 1)
                    if more and u % 4 == 3:
                        project(b + 1, u // 4)
                    if old and u == 9:
                        pe.wait_ge(heads_ready, b)
                        pe.wait_ge(next_copied, b)
                        for t in range(TB):
                            i = turn(FIN[:, t * P:(t + 1) * P], o1[:, t * P:(t + 1) * P])
                        i.then_inc(heads_turned, 1)
                    if old and u == 12:
                        pe.wait_ge(headsT_ready, b)
                        for t in range(TB):
                            i = mm(FIN[:, S + t * P:S + (t + 1) * P], oT[:, t * P:(t + 1) * P], wvo[:, 1, :], start=True, stop=True)
                        i.then_inc(wo_done, 1)
                    if old and u == 20:
                        pe.wait_ge(next_norm, b)
                        for t in range(TB):
                            i = turn(FIN[:, t * P:(t + 1) * P], xnb[:, 0, t, :])
                        i.then_inc(next_turned, 1)
            over_batches(pe, step)

            if upto >= "B":
                pe.wait_ge(next_copied, B + 1)
                pe.wait_ge(small_in, 112)
                for t in range(NT):
                    i = mm(banks[0][:, t * E0:(t + 1) * E0], xmT[:, t * P:(t + 1) * P], gateT, start=True, stop=True)
                i.then_inc(gate_made, 1)
                pe.wait_ge(gate_biased, 1)
                pe.wait_ge(ffn_in, 80)
                pe.sem_inc(h_ready, 2)
                pe.sem_inc(acc_done, 2 * TPG)
                with pe.Fori(0, T // GT // 2) as gg:
                    def up(i):
                        G, e = divmod(i, E0)
                        for c, (h0, m) in enumerate(HCH):
                            k = i * 3 + c
                            K = gg * 54 + k
                            tok = xmT[:, bass.ds((gg * 2 + G) * GT, GT)]
                            pe.wait_ge(h_ready, K + 1)
                            mm(banks[k % 2][0:m, :], w1T[:, e * HID + h0:e * HID + h0 + m], tok, start=True, stop=True)
                            mm(banks[2 + k % 2][0:m, :], w3T[:, e * HID + h0:e * HID + h0 + m], tok, start=True, stop=True).then_inc(up_made, 1)

                    def down(i):
                        e = i % E0
                        N = gg * 2 * E0 + i
                        pe.wait_ge(h_ready, 2 + 3 * N + 3)
                        pe.wait_ge(acc_done, TPG * N + TPG)
                        for t in range(TPG):
                            for c, (h0, m) in enumerate(HCH):
                                j = mm(banks[4 + i % 2][:, t * P:(t + 1) * P], hs[0:m, i % 2, c, t * P:(t + 1) * P], w2s[0:m, e, c, :],
                                       start=(c == 0), stop=(c == 2))
                        j.then_inc(down_made, 1)
                    for i in range(2 * E0):
                        up(i)
                        if i > 0:
                            down(i - 1)
                    down(2 * E0 - 1)
            if upto >= "C":
                with pe.Fori(0, B) as b:
                    pe.wait_ge(c_norm, b + 1)
                    pe.wait_ge(c_copied, b + 1)
                    for t in range(TB):
                        i = turn(banks[6][:, t * P:(t + 1) * P], xnb[:, 1, t, :])
                    i.then_inc(c_turned, 1)
                pe.wait_ge(c_copied, B + 1)
                pe.wait_ge(w1_in, 48)

                def project1(n, b, c):
                    at_least(pe, k1_ready, n)
                    at_least(pe, q1_ready, n)
                    mm(banks[6][:, 0:S], Wkv[:, c * P:(c + 1) * P], xcT[:, bass.ds(b * S, S)], start=True, stop=True)
                    mm(banks[6][:, S:KV], Wkv[:, c * P:(c + 1) * P], xnT[:, bass.ds(b * S, S)], start=True, stop=True).then_inc(k1_made, 1)
                    mm(banks[7][:, 0:S], Wq[:, c * P:(c + 1) * P], xnT[:, bass.ds(b * S, S)], start=True, stop=True).then_inc(q1_made, 1)

                project1(0, 0, 0)
                pe.wait_ge(v1_ones, 1)

                def step(b, new, old, more):
                    for u in range(UNITS1):
                        if new:
                            U = UNITS1 * b + u
                            h, t = divmod(u, TB)
                            c, r = h // 2, slice(DH1 * (h % 2), DH1 * (h % 2) + DH1)
                            if u % 4 == 0:
                                pe.wait_ge(k1_ready, 8 * b + c + 1)
                                pe.wait_ge(q1_ready, 8 * b + c + 1)
                            at_least(pe, p1_ready, U - 1)
                            mm(banks[u % 2][:, :], QT[r, c % 2, t * P:(t + 1) * P], KT[r, c % 2, :], start=True, stop=True).then_inc(s1_made, 1)
                        unit = lagged(b, u, LT1, new, old, UNITS1)
                        if unit:
                            bv, v = unit
                            pe.wait_ge(p1_ready, UNITS1 * bv + v + 1)
                            at_least(pe, (p1t_dve, p1t_act)[v % 2], UNITS1 // 2 * bv + v // 2)
                            for kt in range(4):
                                i = turn(banks[2 + v % 2][:, kt * P:(kt + 1) * P], P1[:, v % 4, kt * P:(kt + 1) * P])
                            i.then_inc(p1_turned, 1)
                        if new and u == 4:
                            pe.wait_ge(kv_copied, 2 * b + 2)
                            for tt in range(4):
                                if tt == 0:
                                    pe.wait_ge(k1_ready, 8 * b + 2)
                                    pe.wait_ge(q1_ready, 8 * b + 2)
                                else:
                                    pe.wait_ge(v1_act, 4 * b + tt)
                                    pe.wait_ge(v1_dve, 4 * b + tt)
                                for half in range(2):
                                    mm(banks[6 + half][:, :], kvT[:, tt * P:(tt + 1) * P], Wkv[:, INNER + 512 * half:INNER + 512 * (half + 1)],
                                       start=True, stop=True).then_inc(v1_made, 1)
                        unit = lagged(b, u, LP1, new, old, UNITS1)
                        if unit:
                            bv, v = unit
                            if v == 0:
                                pe.wait_ge(v1_act, 4 * bv + 4)
                                pe.wait_ge(v1_dve, 4 * bv + 4)
                            pe.wait_ge((p1t_dve, p1t_act)[v % 2], UNITS1 // 2 * bv + v // 2 + 1)
                            at_least(pe, o1_ready, UNITS1 * bv + v - 1)
                            for kt in range(4):
                                i = mm(banks[4 + v % 2][:, 0:DH1 + 1], P1T[:, v % 4, kt * P:(kt + 1) * P], V1[:, kt, v // TB, :],
                                       start=(kt == 0), stop=(kt == 3))
                            i.then_inc(pv1_done, 1)
                        if old and u == 5:
                            pe.wait_ge(o1_ready, UNITS1 * b)
                            if new:
                                pe.wait_ge(v1_act, 4 * b + 4)
                                pe.wait_ge(v1_dve, 4 * b + 4)
                            for f in range(4):
                                if f >= 2:
                                    pe.wait_ge(ot_ready, 4 * (b - 1) + f - 1)
                                for c in range(4):
                                    at = (f % 2) * 512 + c * P
                                    i = turn(banks[6 + f % 2][:, c * P:(c + 1) * P], O1[:, f // 2, at:at + P])
                                i.then_inc(o1_part, 1)
                        if old and u == 6:
                            pe.wait_ge(ot_ready, 4 * (b - 1) + 4)
                            for t in range(TB):
                                for c in range(8):
                                    i = mm(banks[6][:, t * P:(t + 1) * P], OT[:, t, c, :], Wout[:, c, :], start=(c == 0), stop=(c == 7))
                            i.then_inc(out1_made, 1)
                        if new and u % 4 == 3 and (u < UNITS1 - 1 or more):
                            n = 8 * b + u // 4 + 1
                            if u == 7:
                                pe.wait_ge(v1_act, 4 * b + 4)
                                pe.wait_ge(v1_dve, 4 * b + 4)
                                if old:
                                    pe.wait_ge(x3_ready, b)
                            project1(n, b if u < UNITS1 - 1 else b + 1, (u // 4 + 1) % 8)
                over_batches(pe, step)

            if upto == "D":
                for g in range(4):
                    pe.wait_ge(d_norm, 2 * g + 2)
                    for t in range(4):
                        i = turn(banks[g][:, t * P:(t + 1) * P], xn_tok[:, 4 * g + t, :])
                    i.then_inc(d_turned, 1)
                for t in range(NT):
                    if t % 4 == 0:
                        pe.wait_ge(d_copied, t // 4 + 1)
                    i = mm(banks[4][:, t * E1:(t + 1) * E1], xmT[:, t * P:(t + 1) * P], WrT, start=True, stop=True)
                i.then_inc(r_made, 1)
                pe.wait_ge(oh_ready, 1)
                oh = oneh[:, :, :].rearrange("p t e -> p (t e)")
                mm(banks[5][:, 0:NT * E1], before, oh, start=True, stop=True)
                mm(banks[5][:, NT * E1:2 * NT * E1], ones[:, :], oh, start=True, stop=True).then_inc(rank_made, 1)
                pe.wait_ge(xe_in, 16)
                pe.wait_ge(slots_ready, 1)
                for g in range(4):
                    for t in range(4):
                        i = turn(banks[g][:, t * P:(t + 1) * P], xe[:, 4 * g + t, :])
                    i.then_inc(xe_turned, 1)
                pe.wait_ge(w1e_in, 160)

                def down1(e):
                    pe.wait_ge(h1_act, e + 1)
                    pe.wait_ge(h1_dve, e + 1)
                    if e >= 2:
                        pe.wait_ge(y1_copied, e - 1)
                    for t in range(2):
                        for c in range(4):
                            i = mm(banks[6 + e % 2][:, t * P:(t + 1) * P], h1[:, e % 2, c, t * P:(t + 1) * P], W2[:, e, c, :], start=(c == 0), stop=(c == 3))
                    i.then_inc(y1_made, 1)
                for e in range(E1):
                    pe.wait_ge(xe_copied, e // 2 + 1)
                    for half in range(2):
                        if e >= 1:
                            pe.wait_ge((h1_act, h1_dve)[half], e)
                        for k in range(2):
                            c = 2 * half + k
                            i = mm(banks[4 + half][:, k * CAP:(k + 1) * CAP], W1[:, e, c * P:(c + 1) * P], xeT[:, e * CAP:(e + 1) * CAP], start=True, stop=True)
                        i.then_inc(h1_made, 1)
                    if e >= 1:
                        down1(e - 1)
                down1(E1 - 1)


_SHAPES = [((B, S, D), "float32")]


def _constants():
    p = np.arange(P)
    ident = np.eye(P)
    before = p[:, None] < p[None, :]
    low = np.stack([-1.0 * (p % 32 >= 16), -1.0 * (p % 16 >= 8)], 1)
    iota = np.broadcast_to(np.arange(E0), (P, E0))
    return np.concatenate([ident, before, low, iota], 1).astype(np.float32)


def kernel(**inputs):
    import concourse.bacc as _bacc
    from concourse import mybir as _mybir
    from concourse.bass_utils import run_bass_kernel_spmd as _run

    i = {k: np.asarray(v) for k, v in inputs.items()}
    L0, F0, L1, F1_ = "L0_xattn_", "L0_ffn_", "L1_xattn_", "L1_ffn_"
    w1 = np.concatenate([i[F0 + "w1"], i[F0 + "new_w1"]], 0)
    w3 = np.concatenate([i[F0 + "w3"], i[F0 + "new_w3"]], 0)
    w2 = np.concatenate([i[F0 + "w2"], i[F0 + "new_w2"]], 0)
    laid = {
        "const": _constants(),
        "x": i["x"].reshape(T, D),
        "ctx": i["ctx_1024"].reshape(T, D),
        "ctxT": i["ctx_1024"].reshape(T, D).T,
        "mask": i["mask_Bx16xSxS2_ff0"].reshape(B * H0, S, S),
        "W_q": i[L0 + "W_q"], "W_k": i[L0 + "W_k"], "W_v": i[L0 + "W_v"], "W_o": i[L0 + "W_o"],
        "lambda_q1": i[L0 + "lambda_q1"].reshape(1, -1), "lambda_k1": i[L0 + "lambda_k1"].reshape(1, -1),
        "lambda_q2": i[L0 + "lambda_q2"].reshape(1, -1), "lambda_k2": i[L0 + "lambda_k2"].reshape(1, -1),
        "rms_scale": i[L0 + "rms_scale"].reshape(1, -1),
        "w1T": w1.reshape(E0 * HID, D).T, "w3T": w3.reshape(E0 * HID, D).T,
        "w2T": w2.transpose(0, 2, 1),
        "gateT": np.concatenate([i[F0 + "gate_weight"], i[F0 + "new_gate_weight"]], 0).T,
        "gate_bias": i[F0 + "gate_bias"].reshape(1, 1),
        "g1": i[L1 + "g1"].reshape(D, 1), "b1": i[L1 + "b1"].reshape(D, 1),
        "g2": i[L1 + "g2"].reshape(D, 1), "b2": i[L1 + "b2"].reshape(D, 1),
        "Wq": i[L1 + "Wq"], "Wkv": i[L1 + "Wkv"], "Wout": i[L1 + "Wout"],
        "Wr": i[F1_ + "Wr"], "W1": i[F1_ + "W1"], "W2": i[F1_ + "W2"],
    }
    nc = _bacc.Bacc("TRN2", target_bir_lowering=False, num_devices=1)
    arrays, args = {}, {}
    for name, v in laid.items():
        v = np.ascontiguousarray(v)
        arrays[f"in_{name}"] = v
        args[name] = nc.dram_tensor(f"in_{name}", v.shape, _mybir.dt.from_np(v.dtype), kind="ExternalInput").ap()
    o = nc.dram_tensor("out_x", (T, D), _mybir.dt.float32, kind="ExternalOutput").ap()
    build(nc, args, o, "D")
    r = _run(nc, [arrays], core_ids=[0])
    return r.results[0]["out_x"].reshape(B, S, D)
```

```python
from contextlib import ExitStack

import numpy as np

import concourse.bass as bass
from concourse import mybir

F32 = mybir.dt.float32
R32 = mybir.dt.float32r
U32 = mybir.dt.uint32
ALU = mybir.AluOpType
ACT = mybir.ActivationFunctionType
X = mybir.AxisListType.X

P = 128
B, S, D = 8, 256, 128
T = B * S
NT = T // P
TB = S // P
LOWEST = -3.0e38

H0, DH0 = 16, 8
SLOTS = 2 * H0 // 4
LAMBDA_INIT = 0.8
EPS = 1e-5

E0, HID = 9, 352
HCH = [(0, 128), (128, 128), (256, 96)]
GT = 512
TPG = GT // P

H1, DH1 = 16, 64
INNER = H1 * DH1
KV = 2 * S
SCALE1 = float(1.0 / np.sqrt(np.sqrt(DH1)))

E1, F1 = 8, 512
CAP = T // E1


def at_least(eng, sem, value):
    if isinstance(value, int) and value <= 0:
        return
    eng.wait_ge(sem, value)


def hold(eng, sem, value, passed):
    if isinstance(value, int):
        at_least(eng, sem, value)
    else:
        eng.wait_ge(sem, value)
        eng.sem_inc(passed, 1)


class OwnSteps:

    def __init__(self, eng, sem):
        self.eng, self.sem, self.n, self.base = eng, sem, 0, 0

    def did(self, instruction):
        instruction.then_inc(self.sem, 1)
        self.n += 1

    def settle(self):
        self.eng.wait_ge(self.sem, self.base + self.n)

    def loop(self, register, first, per_turn):
        self.start = self.n
        self.per_turn = per_turn
        self.base = (register - first) * per_turn if first else register * per_turn

    def end_loop(self, turns):
        assert self.n - self.start == self.per_turn, (self.n - self.start, self.per_turn)
        self.n = self.start + turns * self.per_turn
        self.base = 0


def bc(ap, n):
    return ap.unsqueeze(len(ap.shape)).to_broadcast([*ap.shape, n])


def build(nc, a, out, upto="D"):
    with ExitStack() as ctx:
        def sb(name, shape, dt=F32):
            return ctx.enter_context(nc.sbuf_tensor(name, shape, dt))

        def bank(name):
            return ctx.enter_context(nc.psum_tensor(name, [P, 512], F32))

        def sem(name):
            return ctx.enter_context(nc.semaphore(name))

        x = sb("x", [P, NT, D])
        const = sb("const", [P, 2 * P + 2 + E0])
        ident = const[:, 0:P]
        before = const[:, P:2 * P]
        low_part = const[:, 2 * P:2 * P + 2]
        iota9 = const[:, 2 * P + 2:2 * P + 2 + E0]
        ctxT = sb("ctxT", [P, T])
        OT = ctxT[:, 0:2 * S].rearrange("p (r q) -> p r q", r=2)
        outT = ctxT[:, 2 * S:3 * S]
        xnT = sb("xnT", [P, T])
        xmT = sb("xmT", [P, T])
        xcT = sb("xcT", [P, T])
        ffnw = sb("ffnw", [P, 2 * E0 * HID + 3 * E0 * D])
        w1T = ffnw[:, 0:E0 * HID]
        w3T = ffnw[:, E0 * HID:2 * E0 * HID]
        w2s = ffnw[:, 2 * E0 * HID:].rearrange("p (e c d) -> p e c d", e=E0, c=3)
        W1 = ffnw[:, 0:E1 * F1].rearrange("p (e f) -> p e f", e=E1)
        W2 = ffnw[:, E1 * F1:2 * E1 * F1].rearrange("p (e c d) -> p e c d", e=E1, d=D)
        wqk = sb("wqk", [P, 2, 2 * P])
        twice = sb("twice", [P, 2 * INNER])
        wqk4 = twice[:, :].rearrange("p (k i r d) -> p k i r d", k=2, r=4, d=DH0)
        Wout = twice[:, :].rearrange("p (h d) -> p h d", d=D)
        wvo = sb("wvo", [P, 2, P])
        shared = sb("shared", [P, 4 * INNER])
        VZ = shared[:, :].rearrange("p (t h n) -> p t h n", t=TB, h=H0)
        Wq = shared[:, 0:INNER]
        Wkv = shared[:, INNER:3 * INNER]
        qk = sb("qk", [P, SLOTS, 2 * S], R32)
        high = sb("high", [P, 2, 2 * S], R32)
        small = sb("small", [P, 1024])
        work = sb("work", [P, 6144])
        LATE = 4 * H1 * 2 * DH1
        with nc.sbuf_tensor("late", [P, LATE], F32) as late:
            pass
        v1_split = sb("v1_split", [P, LATE], R32)

        masks = work[:, 0:4096].rearrange("p (r h t k) -> p r h t k", r=4, h=2, t=TB)
        zs = late[:, 0:4096].rearrange("p (r s t k) -> p r s t k", r=4, s=2, t=TB)
        AT = late[:, 4096:5120].rearrange("p (r k q) -> p r k q", r=2, k=TB)
        V0 = work[:, 4096:6144].rearrange("p (t n) -> p t n", t=NT)
        at = 5120
        o1 = late[:, at:at + 256]
        o2 = late[:, at + 256:at + 512]
        oT = late[:, at + 512:at + 768]
        lnw = late[:, at + 768:at + 768 + 512].rearrange("p (k t d) -> p k t d", k=2, t=TB)
        xnb = sb("xnb", [P, TB, D])
        ctx_tok = work[:, 0:NT * D].rearrange("p (t d) -> p t d", t=NT)
        x_tok = work[:, NT * D:2 * NT * D].rearrange("p (t d) -> p t d", t=NT)
        squares = late[:, 6400:7424].rearrange("p (r t d) -> p r t d", r=2, d=D)
        hs = work[:, 0:3072].rearrange("p (r c n) -> p r c n", r=2, c=3)
        sil = work[:, 3072:4096].rearrange("p (r n) -> p r n", r=2)
        c0 = 0
        def take(n):
            nonlocal c0
            c0 += n
            return work[:, c0 - n:c0]
        P1 = take(4 * TB * KV).rearrange("p (r t k) -> p r t k", r=4, t=TB)
        KT = take(1024).rearrange("p (r k) -> p r k", r=2)
        QT = take(512).rearrange("p (r q) -> p r q", r=2)
        kvT = take(512)
        V1 = v1_split[:, :].rearrange("p (t h s d) -> p t h s d", t=4, h=H1, s=2)
        PTh, PTl = (qk[:, 4 * k:4 * k + 4, :].rearrange("p s n -> p (s n)").rearrange("p (r t q) -> p r t q", r=2, t=4) for k in range(2))
        xn_tok = work[:, 0:2048].rearrange("p (t d) -> p t d", t=NT)
        xe = work[:, 2048:4096].rearrange("p (t d) -> p t d", t=NT)
        xeT = work[:, 4096:6144]
        h1 = late[:, 0:2048].rearrange("p (r c n) -> p r c n", r=2, c=4)
        ye = late[:, 2048:4096].rearrange("p (t d) -> p t d", t=NT)
        yg = late[:, 4096:6144].rearrange("p (t d) -> p t d", t=NT)

        off = 0
        def tiny(n):
            nonlocal off
            off += n
            return small[:, off - n:off]
        rowmax = tiny(16).rearrange("p (r i) -> p r i", r=4)
        negmax = tiny(16).rearrange("p (r i) -> p r i", r=4)
        rowsum = tiny(16).rearrange("p (r i) -> p r i", r=4)
        coef = tiny(8).rearrange("p (r t) -> p r t", t=TB)
        rsum = tiny(64).rearrange("p (h s t) -> p h s t", s=2, t=TB)
        r1_old = tiny(32).rearrange("p (t h) -> p t h", t=TB)
        lam_in = sb("lam_in", [P, 4, H0 * DH0])
        lam = tiny(32).rearrange("p (k h) -> p k h", k=2)
        rms_w = tiny(DH0)
        ms = tiny(32)
        rr = tiny(32)
        minus_half = tiny(32)
        mean = tiny(2)
        var = tiny(2)
        rstd = tiny(2)
        g1b1 = tiny(4)
        bias9 = tiny(E0)
        gateT = tiny(E0)
        WrT = tiny(E1)
        nm1 = tiny(8).rearrange("p (r t) -> p r t", t=TB)
        sum1 = tiny(8).rearrange("p (r t) -> p r t", t=TB)
        rc1 = tiny(8).rearrange("p (r t) -> p r t", t=TB)
        means = tiny(8).rearrange("p (r t) -> p r t", r=2)
        vars_ = tiny(8).rearrange("p (r t) -> p r t", r=2)
        rstds = tiny(8).rearrange("p (r t) -> p r t", r=2)
        big = sb("big", [P, 1024])
        boff = 0
        def mid(n):
            nonlocal boff
            boff += n
            return big[:, boff - n:boff]
        score9 = mid(NT * E0).rearrange("p (t e) -> p t e", e=E0)
        cw = mid(NT * E0).rearrange("p (t e) -> p t e", e=E0)
        tmp9 = mid(NT * E0).rearrange("p (t e) -> p t e", e=E0)
        top8 = mid(NT * 8).rearrange("p (t e) -> p t e", e=8)
        idx8 = sb("idx8", [P, NT, 8], U32)
        idx_f = mid(NT * 2).rearrange("p (k t) -> p k t", k=2)
        wk = mid(NT * 2).rearrange("p (k t) -> p k t", k=2)
        wsum = mid(NT)
        keep = mid(NT)
        slot_f = mid(NT)
        slot_i = sb("slot_i", [P, NT], mybir.dt.uint32)
        p_tok = mid(NT)
        zeros = sb("zeros", [P, 512])
        ones = sb("ones", [P, P])
        probs8 = mid(NT * E1).rearrange("p (t e) -> p t e", e=E1)
        oneh = sb("oneh", [P, NT, E1])
        sums = sb("sums", [P, 2, NT, E1])

        xe_dram = nc.dram_tensor("xe_scratch", [E1 * CAP, D], F32, kind="Internal").ap()
        ye_dram = nc.dram_tensor("ye_scratch", [E1 * CAP, D], F32, kind="Internal").ap()

        banks = [bank(f"bank{i}") for i in range(8)]
        SC, PT, FIN, PROJ, PO = banks[0:4], banks[4], banks[5], banks[6], banks[7]

        def sems(names):
            return [sem(n) for n in names.split()]

        const_in, x_in, ctx_in, ctxT_in, w0_in, lam_sem, small_in = sems("const_in x_in ctx_in ctxT_in w0_in lam_sem small_in")
        ffn_in, w1_in, w1e_in = sems("ffn_in w1_in w1e_in")
        mask_in = [sem(f"mask_in{r}") for r in range(4)]
        dve_own = sem("dve_own")
        passed_dve, passed_pool, passed_act = sems("passed_dve passed_pool passed_act")
        setup_done, wqk4_ready, lam_sum, lam_exp = sems("setup_done wqk4_ready lam_sum lam_exp")
        ln_centred, ln_squared, ln_var, ln_rstd, ln_done = sems("ln_centred ln_squared ln_var ln_rstd ln_done")
        next_var, next_rstd = sems("next_var next_rstd")
        squared, rms_scaled, mean_ready, centred, deviated = sems("squared rms_scaled mean_ready centred deviated")
        prep_turned, prep_copied = sems("prep_turned prep_copied")
        v0_made, v0_copied = sems("v0_made v0_copied")
        proj_made, high_ready, stack_ready = sems("proj_made high_ready stack_ready")
        scores_made, rowmax_done, negmax_ready, exp_done = sems("scores_made rowmax_done negmax_ready exp_done")
        coef_ready, pv_read, attn_ready, attn_turned, attnT_ready, pv_done, sums_copied, sums_turned, vz_ready = sems(
            "coef_ready pv_read attn_ready attn_turned attnT_ready pv_done sums_copied sums_turned vz_ready")
        rms_in, rms_out, heads_ready, heads_turned, headsT_ready, wo_done, wo_added = sems("rms_in rms_out heads_ready heads_turned headsT_ready wo_done wo_added")
        next_norm, next_turned, next_copied = sems("next_norm next_turned next_copied")
        gate_made, gate_biased, gate_sig, cw_ready = sems("gate_made gate_biased gate_sig cw_ready")
        up_made, silu_done, h_ready, down_made, acc_done = sems("up_made silu_done h_ready down_made acc_done")
        c_turned, c_copied, kv_copied, k1_made, q1_made, k1_ready, q1_ready = sems(
            "c_turned c_copied kv_copied k1_made q1_made k1_ready q1_ready")
        v1_made, v1_high, v1_ready = sems("v1_made v1_high v1_ready")
        s1_made, nm1_ready, exp1_done, rc1_ready, p1_ready, p1_turned, p1_high, p1_split = sems(
            "s1_made nm1_ready exp1_done rc1_ready p1_ready p1_turned p1_high p1_split")
        pv1_done, o1_ready, wout_done, outT_ready, out_turned, x3_ready = sems(
            "pv1_done o1_ready wout_done outT_ready out_turned x3_ready")
        d_turned, d_copied, r_made, r_shift, r_exp = sems("d_turned d_copied r_made r_shift r_exp")
        oh_ready, rank_made, slots_ready = sems("oh_ready rank_made slots_ready")
        zero_ready, zeroed, scattered, xe_in, xe_turned, xe_copied = sems("zero_ready zeroed scattered xe_in xe_turned xe_copied")
        h1_made, h1_act, h1_dve, y1_made, y1_copied, ye_out = sems("h1_made h1_act h1_dve y1_made y1_copied ye_out")
        yg_zero, gathered, y_ready, stored = sems("yg_zero gathered y_ready stored")

        LC, LT, LA, LP = 2, 4, 4, 5
        LR1, LT1, LP1, LO1, LW1 = 1, 2, 3, 4, 5

        out_rows = out.rearrange("(t p) d -> p t d", p=P)
        mask_rows = a["mask"].rearrange("n (t p) k -> p n t k", p=P)

        SA, TU, KB, VB, OB, WB = banks[0:2], banks[2:4], banks[4], banks[5], banks[6], banks[7]

        def values_of(b, h, new, more):
            if h % 2 == 0:
                return None
            if h == 1:
                return (8 * b + 3, 0, 3) if new else None
            if h <= 9:
                return (8 * b + 4 + (h - 3) // 2, 1, (h - 3) // 2) if new else None
            return (8 * (b + 1) + (h - 11) // 2, 0, (h - 11) // 2) if more else None

        block = ctx.enter_context(nc.Block())

        def over_batches(eng, step, own=None, per_turn=0):
            step(0, True, False, True)
            with eng.Fori(1, B - 1) as b:
                if own:
                    own.loop(b, 1, per_turn)
                step(b, True, True, True)
            if own:
                own.end_loop(B - 2)
            step(B - 1, True, True, False)
            step(B, False, True, False)

        def lagged(b, u, lag, new, old, units):
            if u >= lag:
                return (b, u - lag) if new else None
            return (b - 1, u - lag + units) if old else None

        @block.sync
        def _(sp):
            def load(dst, src, s):
                sp.dma_start(dst, src).then_inc(s, 16)

            load(ctx_tok, a["ctx"].rearrange("(t p) d -> p t d", p=P), ctx_in)
            load(x[:, :, :], a["x"].rearrange("(t p) d -> p t d", p=P), x_in)
            load(wqk[:, 0, :], a["W_q"], w0_in)
            load(wqk[:, 1, :], a["W_k"], w0_in)
            load(wvo[:, 0, :], a["W_v"], w0_in)
            load(wvo[:, 1, :], a["W_o"], w0_in)
            load(ctxT[:, :], a["ctxT"], ctxT_in)

            sp.wait_ge(prep_turned, 8)

            def step(b, new, old, more):
                if not new:
                    return
                for pair in range(H0 // 2):
                    at_least(sp, rowmax_done, 4 * H0 * b + 8 * (pair - 3))
                    sp.dma_start(masks[:, pair % 4], mask_rows[:, bass.ds(b * H0 + 2 * pair, 2)]).then_inc(mask_in[pair % 4], 16)
                if isinstance(b, int) and b == 0:
                    load(w1T, a["w1T"], ffn_in)
                    load(w3T, a["w3T"], ffn_in)
                    for c, (h0, m) in enumerate(HCH):
                        load(w2s[0:m, :, c, :], a["w2T"][:, h0:h0 + m, :].rearrange("e p d -> p e d"), ffn_in)
            over_batches(sp, step)
            sp.wait_ge(pv_done, H0 * B)
            load(Wq, a["Wq"], w1_in)
            load(Wkv, a["Wkv"], w1_in)
            for half in range(2):
                load(Wout[half * DH1:(half + 1) * DH1], a["Wout"].rearrange("(h p) d -> p h d", p=DH1), w1_in)

            if upto == "A":
                sp.wait_ge(next_norm, B)
                sp.wait_ge(ffn_in, 16)
            if upto >= "B":
                sp.wait_ge(acc_done, 2 * TPG + TPG * E0 * (T // GT))
            if upto >= "C":
                for e0 in (0, 4):
                    load(W1[:, e0:e0 + 4], a["W1"][e0:e0 + 4].rearrange("e d f -> d e f"), w1e_in)
                    for e in range(e0, e0 + 4):
                        load(W2[:, e], a["W2"][e].rearrange("(c p) d -> p c d", p=P), w1e_in)
                sp.wait_ge(x3_ready, B)
            if upto == "D":
                sp.wait_ge(scattered, 16 * NT)
                load(xe, xe_dram.rearrange("(t p) d -> p t d", p=P), xe_in)
                for e in range(E1):
                    sp.wait_ge(y1_copied, e + 1)
                    sp.dma_start(ye_dram.rearrange("(t p) d -> p t d", p=P)[:, 2 * e:2 * e + 2], ye[:, 2 * e:2 * e + 2, :]).then_inc(ye_out, 16)
                for q in range(4):
                    sp.wait_ge(y_ready, q + 1)
                    sp.dma_start(out_rows[:, 4 * q:4 * q + 4], x[:, 4 * q:4 * q + 4, :]).then_inc(stored, 16)
                sp.wait_ge(stored, 64)
            else:
                sp.dma_start(out_rows, x[:, :, :]).then_inc(stored, 16)
                sp.wait_ge(stored, 16)

        @block.gpsimd
        def _(pool):
            pool.memset(minus_half, -0.5).then_inc(setup_done, 1)
            pool.memset(bias9[:, 0:E0 - 1], 0.0).then_inc(setup_done, 1)
            pool.memset(shared[:, :], 0.0).then_inc(setup_done, 1)
            pool.memset(ones[:, :], 1.0).then_inc(setup_done, 1)
            pool.memset(zeros[:, :], 0.0).then_inc(zero_ready, 1)
            pool.dma_start(const[:, :], a["const"]).then_inc(const_in, 16)
            for n, name in enumerate(("lambda_q1", "lambda_k1", "lambda_q2", "lambda_k2")):
                pool.dma_start(lam_in[:, n, :], a[name].to_broadcast([P, H0 * DH0])).then_inc(lam_sem, 16)
            pool.dma_start(rms_w, a["rms_scale"].to_broadcast([P, DH0])).then_inc(lam_sem, 16)
            for n, name in enumerate(("g1", "b1", "g2", "b2")):
                pool.dma_start(g1b1[:, n:n + 1], a[name]).then_inc(small_in, 16)
            pool.dma_start(bias9[:, E0 - 1:E0], a["gate_bias"].to_broadcast([P, 1])).then_inc(small_in, 16)
            pool.dma_start(gateT, a["gateT"]).then_inc(small_in, 16)
            pool.dma_start(WrT, a["Wr"]).then_inc(small_in, 16)
            pool.wait_ge(zero_ready, 1)
            for q in range(4):
                pool.dma_start(xe_dram.rearrange("(p t) d -> p (t d)", p=P)[:, 512 * q:512 * q + 512], zeros[:, :]).then_inc(zeroed, 16)

            def inverse_roots(first, n):
                for k in range(first, first + n):
                    pool.wait_ge(ln_var, k + 1)
                    pool.tensor_tensor(rstds[:, k % 2], vars_[:, k % 2], minus_half[:, 0:4], ALU.pow).then_inc(ln_rstd, 1)

            pool.wait_ge(setup_done, 4)
            inverse_roots(0, 8)

            def place_values(b):
                for t in range(TB):
                    dst = VZ[:, t].rearrange("p h n -> p (h n)")
                    dst = bass.AP(dst.tensor, dst.offset, [dst.ap[0], [P + DH0, H0], [1, DH0]])
                    pool.tensor_copy(dst, V0[:, bass.ds(b * TB + t, 1), :].rearrange("p a (h d) -> p (a h) d", d=DH0)).then_inc(vz_ready, 1)

            pool.wait_ge(v0_copied, 4)

            def step(b, new, old, more):
                if new:
                    if old:
                        hold(pool, pv_done, H0 * b, passed_pool)
                    place_values(b)
                if old:
                    hold(pool, pv_read, b, passed_pool)
                    pool.tensor_tensor(o2, o1, o1, ALU.mult).then_inc(squared, 1)
                    hold(pool, rms_in, b, passed_pool)
                    pool.tensor_tensor(rr, ms, minus_half, ALU.pow).then_inc(rms_out, 1)
                    hold(pool, rms_out, b, passed_pool)
                    oh = o1.rearrange("p (h d) -> p h d", d=DH0)
                    pool.tensor_tensor(oh, oh, bc(rr, DH0), ALU.mult).then_inc(rms_scaled, 1)
                    hold(pool, rms_scaled, b, passed_pool)
                    pool.tensor_tensor(oh, oh, rms_w.unsqueeze(1).to_broadcast([P, 32, DH0]), ALU.mult).then_inc(heads_ready, 1)
                    hold(pool, mean_ready, b, passed_pool)
                    pool.tensor_tensor(lnw[:, 0], x[:, bass.ds((b - 1) * TB, TB), :], bc(mean, D), ALU.subtract).then_inc(centred, 1)
                    hold(pool, centred, b, passed_pool)
                    pool.tensor_tensor(lnw[:, 1], lnw[:, 0], lnw[:, 0], ALU.mult).then_inc(deviated, 1)
                    hold(pool, next_var, b, passed_pool)
                    pool.tensor_tensor(rstd, var, minus_half[:, 0:2], ALU.pow).then_inc(next_rstd, 1)
                    hold(pool, next_rstd, b, passed_pool)
                    pool.tensor_tensor(xnb[:, :, :], lnw[:, 0], bc(rstd, D), ALU.mult).then_inc(next_norm, 1)
            over_batches(pool, step)

            if upto >= "C":
                inverse_roots(8, 8)

                def copy_kv(b):
                    pool.tensor_copy(kvT[:, 0:S], xcT[:, bass.ds(b * S, S)]).then_inc(kv_copied, 1)
                    pool.tensor_copy(kvT[:, S:KV], xnT[:, bass.ds(b * S, S)]).then_inc(kv_copied, 1)
                pool.wait_ge(c_copied, 4)
                copy_kv(0)

                def step(b, new, old, more):
                    for h in range(H1):
                        head = lagged(b, h, LR1, new, old, H1)
                        if head:
                            bv, v = head
                            hold(pool, rc1_ready, H1 * bv + v + 1, passed_pool)
                            for t in range(TB):
                                pool.tensor_scalar(P1[:, v % 4, t, :], P1[:, v % 4, t, :], rc1[:, v % 4, t:t + 1], 1.0,
                                                   ALU.mult, ALU.mult).then_inc(p1_ready, 1)
                        if more and h == 9:
                            hold(pool, v1_made, 8 * b + 8, passed_pool)
                            copy_kv(b + 1)
                over_batches(pool, step)
            if upto == "D":
                inverse_roots(16, 4)
                pool.memset(yg, 0.0).then_inc(yg_zero, 1)
                pool.wait_ge(slots_ready, 1)
                pool.wait_ge(ln_done, 20)
                pool.wait_ge(zeroed, 64)
                for t in range(NT):
                    pool.indirect_dma_start(xe_dram, bass.IndirectOffsetOnAxis(slot_i[:, t:t + 1], 0), xn_tok[:, t, :], None,
                                            bounds_check=E1 * CAP - 1, oob_is_err=False).then_inc(scattered, 16)
                pool.wait_ge(yg_zero, 1)
                pool.wait_ge(ye_out, 16 * E1)
                for t in range(NT):
                    pool.indirect_dma_start(yg[:, t, :], None, ye_dram, bass.IndirectOffsetOnAxis(slot_i[:, t:t + 1], 0),
                                            bounds_check=E1 * CAP - 1, oob_is_err=False).then_inc(gathered, 16)

        @block.vector
        def _(dve):
            own = OwnSteps(dve, dve_own)
            did, settle = own.did, own.settle

            def normalise(first, chunks):
                n = len(chunks)
                for i in range(n + 2):
                    if i < n:
                        src, dst = chunks[i]
                        m = means[:, (first + i) % 2]
                        if i >= 4:
                            dve.wait_ge(ln_done, first + i - 3)
                        did(dve.tensor_reduce(m, src, X, ALU.add))
                        settle()
                        did(dve.tensor_scalar(m, m, 1.0 / D, None, ALU.mult))
                        settle()
                        dve.tensor_tensor(dst, src, bc(m, D), ALU.subtract).then_inc(ln_centred, 1)
                    if 0 <= i - 1 < n:
                        k = first + i - 1
                        dve.wait_ge(ln_squared, k + 1)
                        did(dve.tensor_reduce(vars_[:, k % 2], squares[:, k % 2], X, ALU.add))
                        settle()
                        dve.tensor_scalar(vars_[:, k % 2], vars_[:, k % 2], 1.0 / D, EPS, ALU.mult, ALU.add).then_inc(ln_var, 1)
                    if i >= 2:
                        k = first + i - 2
                        dst = chunks[i - 2][1]
                        dve.wait_ge(ln_rstd, k + 1)
                        dve.tensor_tensor(dst, dst, bc(rstds[:, k % 2], D), ALU.mult).then_inc(ln_done, 1)

            dve.wait_ge(w0_in, 64)
            for k, scale in enumerate((float(1.0 / np.sqrt(DH0)), 1.0)):
                dve.tensor_scalar(wqk4[:, k], wqk[:, k, :].rearrange("p (i d) -> p i d", d=DH0).unsqueeze(2).to_broadcast([P, 32, 4, DH0]),
                                  scale, None, ALU.mult).then_inc(wqk4_ready, 1)
            dve.wait_ge(lam_sem, 80)
            for k in range(2):
                did(dve.tensor_tensor(lam_in[:, 2 * k, :], lam_in[:, 2 * k, :], lam_in[:, 2 * k + 1, :], ALU.mult))
                settle()
                dve.tensor_reduce(lam[:, k, :], lam_in[:, 2 * k, :].rearrange("p (h d) -> p h d", d=DH0), X, ALU.add).then_inc(lam_sum, 1)
            dve.wait_ge(lam_exp, 1)
            did(dve.tensor_tensor(lam[:, 0, :], lam[:, 0, :], lam[:, 1, :], ALU.subtract))
            settle()
            did(dve.tensor_scalar(lam[:, 0, :], lam[:, 0, :], LAMBDA_INIT, -1.0, ALU.add, ALU.mult))
            did(dve.tensor_scalar(rms_w, rms_w, 1.0 - LAMBDA_INIT, None, ALU.mult))
            settle()
            dve.wait_ge(setup_done, 4)
            for g in range(4):
                dve.wait_ge(v0_made, g + 1)
                dve.tensor_copy(V0[:, 4 * g:4 * g + 4, :], banks[g][:, :].rearrange("p (t n) -> p t n", t=4)).then_inc(v0_copied, 1)
            dve.wait_ge(x_in, 16)
            dve.wait_ge(ctx_in, 16)
            four = [slice(4 * g, 4 * g + 4) for g in range(4)]
            normalise(0, [(x[:, g, :], x_tok[:, g, :]) for g in four] + [(ctx_tok[:, g, :], ctx_tok[:, g, :]) for g in four])

            def split(b, sl, PROJ=PROJ):
                dve.wait_ge(high_ready, SLOTS * b + sl + 1)
                for k in range(2):
                    half = slice(k * S, (k + 1) * S)
                    dve.scalar_tensor_tensor(out=qk[:, sl, half], in0=high[:, sl % 2, half].bitcast(F32), scalar=low_part[:, k:k + 1],
                                             in1=PROJ[:, half], op0=ALU.mult, op1=ALU.add).then_inc(stack_ready, 1)

            dve.wait_ge(const_in, 16)
            for sl in range(SLOTS):
                split(0, sl, banks[sl % 4])

            def step(b, new, old, more):
                for h in range(H0):
                    if new:
                        N = H0 * b + h
                        if h % 2 == 0:
                            dve.wait_ge(mask_in[(h // 2) % 4], 16 * (2 * b + h // 8 + 1))
                        at_least(dve, attn_turned, N - 3)
                        hold(dve, scores_made, 2 * N + 2, passed_dve)
                        for s in range(2):
                            for t in range(TB):
                                dve.tensor_tensor_reduce(zs[:, h % 4, s, t, :], SC[2 * (h % 2) + s][:, t * S:(t + 1) * S], masks[:, (h // 2) % 4, h % 2, t, :],
                                                         1.0, LOWEST, ALU.add, ALU.max, rowmax[:, h % 4, 2 * s + t:2 * s + t + 1]).then_inc(rowmax_done, 1)
                        dve.wait_ge(rowmax_done, 4 * N + 4)
                        dve.tensor_scalar(negmax[:, h % 4, :], rowmax[:, h % 4, :], -1.0, None, ALU.mult).then_inc(negmax_ready, 1)
                    if more and h % 2 == 1:
                        split(b + 1, h // 2)
                    item = lagged(b, h, LC, new, old, H0)
                    if item:
                        bv, v = item
                        dve.wait_ge(exp_done, 4 * (H0 * bv + v) + 4)
                        did(dve.reciprocal(rsum[:, v].rearrange("p s t -> p (s t)"), rowsum[:, v % 4, :]))
                        settle()
                        dve.scalar_tensor_tensor(out=coef[:, v % 4, :], in0=rowsum[:, v % 4, 0:2], scalar=lam[:, 0, v:v + 1],
                                                 in1=rsum[:, v, 1, :], op0=ALU.mult, op1=ALU.mult).then_inc(coef_ready, 1)
                        dve.wait_ge(coef_ready, H0 * bv + v + 1)
                        for t in range(TB):
                            dve.scalar_tensor_tensor(out=zs[:, v % 4, 0, t, :], in0=zs[:, v % 4, 1, t, :], scalar=coef[:, v % 4, t:t + 1],
                                                     in1=zs[:, v % 4, 0, t, :], op0=ALU.mult, op1=ALU.add).then_inc(attn_ready, 1)
                    if old and h == 1:
                        did(dve.tensor_copy(r1_old, rsum[:, :, 0, :].rearrange("p h t -> p t h")))
                        settle()
                    if old and h == 7:
                        dve.wait_ge(sums_turned, b)
                        i = dve.tensor_tensor(o1.rearrange("p (t h d) -> p t h d", t=TB, d=DH0), FIN[:, 0:S].rearrange("p (t h d) -> p t h d", t=TB, d=DH0),
                                              bc(r1_old, DH0), ALU.mult)
                        i.then_inc(pv_read, 1)
                    if old and h == 8:
                        dve.wait_ge(squared, b)
                        did(dve.tensor_reduce(ms, o2.rearrange("p (h d) -> p h d", d=DH0), X, ALU.add))
                        settle()
                        dve.tensor_scalar(ms, ms, 1.0 / DH0, EPS, ALU.mult, ALU.add).then_inc(rms_in, 1)
                    if old and h == 13:
                        dve.wait_ge(wo_done, b)
                        xb = x[:, bass.ds((b - 1) * TB, TB), :]
                        dve.tensor_tensor(xb, FIN[:, 0:S].rearrange("p (t d) -> p t d", t=TB), xb, ALU.add).then_inc(wo_added, 1)
                        hold(dve, wo_added, b, passed_dve)
                        did(dve.tensor_reduce(mean, xb, X, ALU.add))
                        settle()
                        dve.tensor_scalar(mean, mean, 1.0 / D, None, ALU.mult).then_inc(mean_ready, 1)
                    if old and h == 14:
                        dve.wait_ge(deviated, b)
                        did(dve.tensor_reduce(var, lnw[:, 1], X, ALU.add))
                        settle()
                        dve.tensor_scalar(var, var, 1.0 / D, EPS, ALU.mult, ALU.add).then_inc(next_var, 1)
            over_batches(dve, step, own, 20)

            if upto >= "B":
                dve.wait_ge(gate_made, 1)
                dve.wait_ge(small_in, 112)
                gate = banks[0][:, 0:NT * E0].rearrange("p (t e) -> p t e", e=E0)
                dve.tensor_tensor(score9, gate, bias9.unsqueeze(1).to_broadcast([P, NT, E0]), ALU.add).then_inc(gate_biased, 1)
                dve.wait_ge(gate_sig, 1)
                for t in range(NT):
                    did(dve.max(top8[:, t, :], score9[:, t, :]))
                settle()
                for t in range(NT):
                    did(dve.max_index(idx8[:, t, :], top8[:, t, :], score9[:, t, :]))
                settle()
                did(dve.tensor_copy(idx_f, idx8[:, :, 0:2].rearrange("p t k -> p k t")))
                did(dve.tensor_tensor(wsum, top8[:, :, 0], top8[:, :, 1], ALU.add))
                settle()
                did(dve.tensor_scalar(wsum, wsum, 1e-20, None, ALU.add))
                settle()
                did(dve.reciprocal(wsum, wsum))
                settle()
                did(dve.tensor_tensor(wk, top8[:, :, 0:2].rearrange("p t k -> p k t"), wsum.unsqueeze(1).to_broadcast([P, 2, NT]), ALU.mult))
                iota = iota9.unsqueeze(1).to_broadcast([P, NT, E0])
                did(dve.tensor_tensor(cw, iota, bc(idx_f[:, 0], E0), ALU.is_equal))
                did(dve.tensor_tensor(tmp9, iota, bc(idx_f[:, 1], E0), ALU.is_equal))
                settle()
                did(dve.tensor_tensor(cw, cw, bc(wk[:, 0], E0), ALU.mult))
                did(dve.tensor_tensor(tmp9, tmp9, bc(wk[:, 1], E0), ALU.mult))
                settle()
                did(dve.tensor_tensor(cw, cw, tmp9, ALU.add))
                settle()

                with dve.Fori(0, T // GT // 2) as gg:
                    def add_expert(i):
                        G, e = divmod(i, E0)
                        N = gg * 2 * E0 + i
                        dve.wait_ge(acc_done, 2 * TPG + TPG * N)
                        dve.wait_ge(down_made, N + 1)
                        for t in range(TPG):
                            tile = gg * 2 * TPG + G * TPG + t
                            xt = x[:, bass.ds(tile, 1), :].rearrange("p a d -> p (a d)")
                            w = cw[:, bass.ds(tile, 1), e:e + 1].rearrange("p a e -> p (a e)")
                            dve.scalar_tensor_tensor(out=xt, in0=banks[4 + i % 2][:, t * P:(t + 1) * P], scalar=w,
                                                     in1=xt, op0=ALU.mult, op1=ALU.add).then_inc(acc_done, 1)
                    for i in range(2 * E0):
                        for c, (_, m) in enumerate(HCH):
                            k = i * 3 + c
                            dve.wait_ge(silu_done, gg * 54 + k + 1)
                            dve.tensor_tensor(hs[0:m, i % 2, c, :], banks[2 + k % 2][0:m, :], sil[0:m, k % 2, :], ALU.mult).then_inc(h_ready, 1)
                        if i > 0:
                            add_expert(i - 1)
                    add_expert(2 * E0 - 1)
                dve.wait_ge(acc_done, 2 * TPG + TPG * E0 * (T // GT))

            if upto >= "C":
                normalise(8, [(x[:, g, :], x_tok[:, g, :]) for g in four] + [(x_tok[:, g, :], x_tok[:, g, :]) for g in four])

                def q_out(n, c):
                    dve.wait_ge(q1_made, n + 1)
                    dve.tensor_scalar(QT[:, c % 2, :], VB[:, 0:S], SCALE1, None, ALU.mult).then_inc(q1_ready, 1)

                def v_low(n, half, kt):
                    dve.wait_ge(v1_high, n + 1)
                    dve.tensor_tensor(V1[:, kt, 8 * half:8 * half + 8, 1, :], VB[:, :].rearrange("p (h d) -> p h d", d=DH1),
                                      V1[:, kt, 8 * half:8 * half + 8, 0, :].bitcast(F32), ALU.subtract).then_inc(v1_ready, 1)

                dve.wait_ge(c_copied, 4)
                q_out(0, 0)
                for kt in range(3):
                    v_low(kt, 0, kt)

                def step(b, new, old, more):
                    for h in range(H1):
                        if new:
                            N = H1 * b + h
                            for t in range(TB):
                                dve.wait_ge(s1_made, TB * N + t + 1)
                                dve.tensor_reduce(nm1[:, h % 4, t:t + 1], SA[t][:, :], X, ALU.max, negate=True).then_inc(nm1_ready, 1)
                        head = lagged(b, h, LR1, new, old, H1)
                        if head:
                            bv, v = head
                            dve.wait_ge(exp1_done, TB * (H1 * bv + v) + TB)
                            dve.reciprocal(rc1[:, v % 4, :], sum1[:, v % 4, :]).then_inc(rc1_ready, 1)
                        head = lagged(b, h, LT1, new, old, H1)
                        if head:
                            bv, v = head
                            for k in range(2):
                                dve.wait_ge(p1_high, 2 * (H1 * bv + v) + k + 1)
                                dve.tensor_tensor(PTl[:, v % 2, 2 * k:2 * k + 2, :], TU[k][:, :].rearrange("p (t q) -> p t q", t=2),
                                                  PTh[:, v % 2, 2 * k:2 * k + 2, :].bitcast(F32), ALU.subtract).then_inc(p1_split, 1)
                        if h % 2 == 0 and (new and h < H1 - 2 or more):
                            q_out(8 * b + h // 2 + 1, (h // 2 + 1) % 8)
                        values = values_of(b, h, new, more)
                        if values:
                            v_low(*values)
                        if old and h == 7:
                            dve.wait_ge(out_turned, b)
                            xb = x[:, bass.ds((b - 1) * TB, TB), :]
                            dve.tensor_tensor(xb, KB[:, 0:TB * D].rearrange("p (t d) -> p t d", t=TB), xb, ALU.add).then_inc(x3_ready, 1)
                over_batches(dve, step)
                dve.wait_ge(x3_ready, B)

            if upto == "D":
                normalise(16, [(x[:, g, :], xn_tok[:, g, :]) for g in four])
                dve.wait_ge(r_made, 1)
                logits = banks[4][:, 0:NT * E1].rearrange("p (t e) -> p t e", e=E1)
                did(dve.tensor_reduce(wsum, logits, X, ALU.max))
                settle()
                dve.tensor_tensor(probs8, logits, bc(wsum, E1), ALU.subtract).then_inc(r_shift, 1)
                dve.wait_ge(r_exp, 1)
                did(dve.tensor_reduce(wsum, probs8, X, ALU.add))
                settle()
                did(dve.reciprocal(wsum, wsum))
                settle()
                did(dve.tensor_tensor(probs8, probs8, bc(wsum, E1), ALU.mult))
                settle()
                for t in range(NT):
                    did(dve.max(top8[:, t, :], probs8[:, t, :]))
                settle()
                for t in range(NT):
                    did(dve.max_index(idx8[:, t, :], top8[:, t, :], probs8[:, t, :]))
                settle()
                did(dve.tensor_copy(idx_f[:, 0], idx8[:, :, 0]))
                settle()
                dve.tensor_tensor(oneh[:, :, :], iota9[:, 0:E1].unsqueeze(1).to_broadcast([P, NT, E1]), bc(idx_f[:, 0], E1), ALU.is_equal).then_inc(oh_ready, 1)
                dve.wait_ge(rank_made, 1)
                tile_rank = banks[5][:, 0:NT * E1].rearrange("p (t e) -> p t e", e=E1)
                totals = banks[5][:, NT * E1:2 * NT * E1].rearrange("p (t e) -> p t e", e=E1)
                did(dve.tensor_copy(sums[:, 0], totals))
                settle()
                cur = 0
                for d in (1, 2, 4, 8):
                    did(dve.tensor_tensor(sums[:, 1 - cur, d:, :], sums[:, cur, d:, :], sums[:, cur, 0:NT - d, :], ALU.add))
                    did(dve.tensor_copy(sums[:, 1 - cur, 0:d, :], sums[:, cur, 0:d, :]))
                    settle()
                    cur = 1 - cur
                did(dve.tensor_tensor(sums[:, 1 - cur], tile_rank, sums[:, cur], ALU.add))
                settle()
                did(dve.tensor_tensor(sums[:, cur], totals, sums[:, 1 - cur], ALU.subtract))
                settle()
                did(dve.tensor_tensor(sums[:, 1 - cur], sums[:, cur], oneh[:, :, :], ALU.mult))
                settle()
                did(dve.tensor_reduce(keep, sums[:, 1 - cur], X, ALU.add, negate=True))
                settle()
                did(dve.tensor_scalar(slot_f, idx_f[:, 0], float(CAP), None, ALU.mult))
                settle()
                did(dve.tensor_tensor(slot_f, slot_f, keep, ALU.add))
                did(dve.tensor_scalar(keep, keep, float(CAP), float(E1 * CAP), ALU.is_ge, ALU.mult))
                settle()
                did(dve.tensor_tensor(slot_f, slot_f, keep, ALU.add))
                settle()
                dve.tensor_copy(slot_i[:, :], slot_f).then_inc(slots_ready, 1)
                for i in range(2 * E1):
                    if i % 2 == 1:
                        dve.wait_ge(h1_made, i + 1)
                        e = i // 2
                        if e >= 2:
                            dve.wait_ge(y1_made, e - 1)
                        dve.tensor_scalar(h1[:, e % 2, 2:4, :], banks[4 + i % 2][:, :].rearrange("p (c n) -> p c n", c=2), 0.0, None,
                                          ALU.max).then_inc(h1_dve, 1)
                dve.wait_ge(gathered, 16 * NT)
                for q in range(4):
                    g = yg[:, 4 * q:4 * q + 4, :]
                    did(dve.tensor_tensor(g, g, bc(top8[:, 4 * q:4 * q + 4, 0], D), ALU.mult))
                    settle()
                    dve.tensor_tensor(x[:, 4 * q:4 * q + 4, :], x[:, 4 * q:4 * q + 4, :], g, ALU.add).then_inc(y_ready, 1)

        @block.scalar
        def _(act):
            act.sem_inc(next_copied, 1)
            act.wait_ge(lam_sum, 2)
            act.activation(lam[:, :, :], lam[:, :, :], ACT.Exp).then_inc(lam_exp, 1)
            act.wait_ge(small_in, 112)

            def square(k, rows):
                act.wait_ge(ln_centred, k + 1)
                if k >= 2:
                    act.wait_ge(ln_var, k - 1)
                act.activation(squares[:, k % 2], rows, ACT.Square).then_inc(ln_squared, 1)

            for k in range(8 + 3):
                if k < 8:
                    square(k, (x_tok, ctx_tok)[k // 4][:, 4 * (k % 4):4 * (k % 4) + 4, :])
                if k >= 3:
                    g = k - 3
                    act.wait_ge(prep_turned, g + 1)
                    if g < 4:
                        act.activation(xnT[:, g * 512:(g + 1) * 512], banks[4 + g % 4][:, :], ACT.Copy).then_inc(prep_copied, 1)
                    else:
                        act.activation(xcT[:, (g - 4) * 512:(g - 3) * 512], banks[4 + g % 4][:, :], ACT.Identity, bias=g1b1[:, 1:2],
                                       scale=g1b1[:, 0:1]).then_inc(prep_copied, 1)

            def high_parts(b, sl, PROJ=PROJ):
                n = SLOTS * b + sl
                act.wait_ge(proj_made, n + 1)
                at_least(act, stack_ready, 2 * (n - 1))
                act.activation(high[:, sl % 2, :], PROJ[:, :], ACT.Copy).then_inc(high_ready, 1)

            for sl in range(SLOTS):
                high_parts(0, sl, banks[sl % 4])

            def step(b, new, old, more):
                for h in range(H0):
                    if more and h % 2 == 1:
                        high_parts(b + 1, h // 2)
                    if old and h == 5:
                        act.wait_ge(pv_done, H0 * b)
                        act.activation(oT, PO[:, 0:S], ACT.Copy).then_inc(sums_copied, 1)
                    if old and h == 12:
                        act.wait_ge(heads_turned, b)
                        act.activation(oT, FIN[:, 0:S], ACT.Copy).then_inc(headsT_ready, 1)
                    item = lagged(b, h, LA, new, old, H0)
                    if item:
                        bv, v = item
                        V = H0 * bv + v
                        act.wait_ge(attn_turned, V + 1)
                        at_least(act, pv_done, V - 1)
                        act.activation(AT[:, v % 2], PT[:, :].rearrange("p (k q) -> p k q", k=TB), ACT.Copy).then_inc(attnT_ready, 1)
                    if new:
                        N = H0 * b + h
                        act.wait_ge(negmax_ready, N + 1)
                        at_least(act, coef_ready, N - 3)
                        for s in range(2):
                            for t in range(TB):
                                k = 2 * s + t
                                act.activation(zs[:, h % 4, s, t, :], zs[:, h % 4, s, t, :], ACT.Exp, bias=negmax[:, h % 4, k:k + 1],
                                               accum_out=rowsum[:, h % 4, k:k + 1]).then_inc(exp_done, 1)
                    if old and h == 15:
                        hold(act, next_turned, b, passed_act)
                        act.activation(xmT[:, bass.ds((b - 1) * S, S)], FIN[:, 0:S], ACT.Copy).then_inc(next_copied, 1)
            over_batches(act, step)

            if upto >= "B":
                act.wait_ge(gate_biased, 1)
                act.activation(score9, score9, ACT.Sigmoid).then_inc(gate_sig, 1)
                with act.Fori(0, T // GT // 2) as gg:
                    for i in range(2 * E0):
                        for c, (_, m) in enumerate(HCH):
                            k = i * 3 + c
                            act.wait_ge(up_made, gg * 54 + k + 1)
                            act.wait_ge(h_ready, gg * 54 + k + 1)
                            act.activation(sil[0:m, k % 2, :], banks[k % 2][0:m, :], ACT.Silu).then_inc(silu_done, 1)
            if upto >= "C":
                for k in range(8):
                    square(8 + k, x_tok[:, 4 * (k % 4):4 * (k % 4) + 4, :])
                for g in range(4):
                    act.wait_ge(c_turned, g + 1)
                    act.activation(xnT[:, g * 512:(g + 1) * 512], banks[g][:, :], ACT.Identity, bias=g1b1[:, 3:4], scale=g1b1[:, 2:3]).then_inc(c_copied, 1)

                def k_out(n, c):
                    act.wait_ge(k1_made, n + 1)
                    act.activation(KT[:, c % 2, :], KB[:, :], ACT.Copy, scale=SCALE1).then_inc(k1_ready, 1)

                def v_high(n, half, kt):
                    act.wait_ge(v1_made, n + 1)
                    act.activation(V1[:, kt, 8 * half:8 * half + 8, 0, :], VB[:, :].rearrange("p (h d) -> p h d", d=DH1), ACT.Copy).then_inc(v1_high, 1)

                k_out(0, 0)
                for kt in range(3):
                    v_high(kt, 0, kt)

                def step(b, new, old, more):
                    for h in range(H1):
                        head = lagged(b, h, LO1, new, old, H1)
                        if head:
                            bv, v = head
                            act.wait_ge(pv1_done, H1 * bv + v + 1)
                            at_least(act, wout_done, H1 * bv + v - 1)
                            act.activation(OT[:, v % 2, :], OB[:, 0:S], ACT.Copy).then_inc(o1_ready, 1)
                        if old and h == 5:
                            act.wait_ge(wout_done, H1 * b)
                            act.activation(outT, WB[:, 0:S], ACT.Copy).then_inc(outT_ready, 1)
                        head = lagged(b, h, LT1, new, old, H1)
                        if head:
                            bv, v = head
                            V = H1 * bv + v
                            at_least(act, pv1_done, V - 1)
                            for k in range(2):
                                act.wait_ge(p1_turned, 2 * V + k + 1)
                                act.activation(PTh[:, v % 2, 2 * k:2 * k + 2, :], TU[k][:, :].rearrange("p (t q) -> p t q", t=2), ACT.Copy).then_inc(p1_high, 1)
                        if new:
                            N = H1 * b + h
                            at_least(act, p1_turned, 2 * (N - 3))
                            for t in range(TB):
                                act.wait_ge(nm1_ready, TB * N + t + 1)
                                act.activation(P1[:, h % 4, t, :], SA[t][:, :], ACT.Exp, bias=nm1[:, h % 4, t:t + 1],
                                               accum_out=sum1[:, h % 4, t:t + 1]).then_inc(exp1_done, 1)
                        if h % 2 == 0 and (new and h < H1 - 2 or more):
                            k_out(8 * b + h // 2 + 1, (h // 2 + 1) % 8)
                        values = values_of(b, h, new, more)
                        if values:
                            v_high(*values)
                over_batches(act, step)
            if upto == "D":
                for k in range(4):
                    square(16 + k, xn_tok[:, 4 * k:4 * k + 4, :])
                for g in range(4):
                    act.wait_ge(d_turned, g + 1)
                    act.activation(xmT[:, g * 512:(g + 1) * 512], banks[g][:, :], ACT.Copy).then_inc(d_copied, 1)
                act.wait_ge(r_shift, 1)
                act.activation(probs8, probs8, ACT.Exp).then_inc(r_exp, 1)
                for g in range(4):
                    act.wait_ge(xe_turned, g + 1)
                    act.activation(xeT[:, g * 512:(g + 1) * 512], banks[g][:, :], ACT.Copy).then_inc(xe_copied, 1)
                for i in range(2 * E1):
                    e = i // 2
                    if i % 2 == 0:
                        act.wait_ge(h1_made, i + 1)
                        if e >= 2:
                            act.wait_ge(y1_made, e - 1)
                        act.activation(h1[:, e % 2, 0:2, :], banks[4 + i % 2][:, :].rearrange("p (c n) -> p c n", c=2), ACT.Relu).then_inc(h1_act, 1)
                    elif e >= 1:
                        act.wait_ge(y1_made, e)
                        act.activation(ye[:, 2 * (e - 1):2 * e, :], banks[6 + (e - 1) % 2][:, 0:2 * D].rearrange("p (t d) -> p t d", t=2), ACT.Copy).then_inc(y1_copied, 1)
                act.wait_ge(y1_made, E1)
                act.activation(ye[:, 2 * (E1 - 1):2 * E1, :], banks[6 + (E1 - 1) % 2][:, 0:2 * D].rearrange("p (t d) -> p t d", t=2), ACT.Copy).then_inc(y1_copied, 1)

        @block.tensor
        def _(pe):
            mm = pe.matmul
            pe.wait_ge(ctxT_in, 16)
            pe.wait_ge(w0_in, 64)
            for t in range(NT):
                i = mm(banks[t // 4][:, (t % 4) * P:(t % 4 + 1) * P], ctxT[:, t * P:(t + 1) * P], wvo[:, 0, :], start=True, stop=True)
                if t % 4 == 3:
                    i.then_inc(v0_made, 1)
            pe.wait_ge(const_in, 16)

            def turn(dst, src):
                return pe.transpose(dst, src, ident)

            for g in range(8):
                pe.wait_ge(ln_done, g + 1)
                if g >= 4:
                    pe.wait_ge(prep_copied, g - 3)
                for t in range(4):
                    i = turn(banks[4 + g % 4][:, t * P:(t + 1) * P], (x_tok, ctx_tok)[g // 4][:, 4 * (g % 4) + t, :])
                i.then_inc(prep_turned, 1)

            def project(b, sl, PROJ=PROJ, reused=1):
                n = SLOTS * b + sl
                at_least(pe, stack_ready, 2 * (n + 1 - reused))
                mm(PROJ[:, 0:S], wqk4[:, 0, 4 * sl:4 * sl + 4].rearrange("p i r d -> p (i r d)"), xnT[:, bass.ds(b * S, S)], start=True, stop=True)
                mm(PROJ[:, S:2 * S], wqk4[:, 1, 4 * sl:4 * sl + 4].rearrange("p i r d -> p (i r d)"), ctxT[:, bass.ds(b * S, S)],
                   start=True, stop=True).then_inc(proj_made, 1)

            pe.wait_ge(wqk4_ready, 2)
            pe.wait_ge(v0_copied, 4)
            pe.wait_ge(prep_copied, 8)
            for sl in range(SLOTS):
                project(0, sl, banks[sl % 4], 4)
            pe.wait_ge(stack_ready, 2 * SLOTS)

            def step(b, new, old, more):
                for h in range(H0):
                    item = lagged(b, h, LT, new, old, H0)
                    if item:
                        bv, v = item
                        V = H0 * bv + v
                        pe.wait_ge(attn_ready, 2 * V + 2)
                        at_least(pe, attnT_ready, V)
                        for kt in range(TB):
                            for t in range(TB):
                                i = turn(PT[:, (2 * kt + t) * P:(2 * kt + t + 1) * P], zs[:, v % 4, 0, t, kt * P:(kt + 1) * P])
                        i.then_inc(attn_turned, 1)
                    if new:
                        N = H0 * b + h
                        for s in range(2):
                            sl, j = divmod(2 * h + s, 4)
                            if j == 0:
                                pe.wait_ge(stack_ready, 2 * (SLOTS * b + sl + 1))
                            at_least(pe, rowmax_done, 4 * (N - 2) + 2 * s + 2)
                            rows = slice(32 * j, 32 * j + 32)
                            for t in range(TB):
                                i = mm(SC[2 * (h % 2) + s][:, t * S:(t + 1) * S], qk[rows, sl, t * P:(t + 1) * P], qk[rows, sl, S:2 * S], start=True, stop=True)
                            i.then_inc(scores_made, 1)
                    item = lagged(b, h, LP, new, old, H0)
                    if item:
                        bv, v = item
                        pe.wait_ge(attnT_ready, H0 * bv + v + 1)
                        if v == 0:
                            pe.wait_ge(vz_ready, 2 * bv + 2)
                            at_least(pe, sums_copied, bv)
                        for kt in range(TB):
                            i = mm(PO[:, 0:S], VZ[:, kt, v, :], AT[:, v % 2, kt, :], start=(v == 0 and kt == 0), stop=(v == H0 - 1 and kt == TB - 1))
                        i.then_inc(pv_done, 1)
                    if more and h % 2 == 0:
                        project(b + 1, h // 2)
                    if old and h == 6:
                        pe.wait_ge(sums_copied, b)
                        pe.wait_ge(next_copied, b)
                        for t in range(TB):
                            i = turn(FIN[:, t * P:(t + 1) * P], oT[:, t * P:(t + 1) * P])
                        i.then_inc(sums_turned, 1)
                    if old and h == 11:
                        pe.wait_ge(heads_ready, b)
                        for t in range(TB):
                            i = turn(FIN[:, t * P:(t + 1) * P], o1[:, t * P:(t + 1) * P])
                        i.then_inc(heads_turned, 1)
                    if old and h == 12:
                        pe.wait_ge(headsT_ready, b)
                        for t in range(TB):
                            i = mm(FIN[:, t * P:(t + 1) * P], oT[:, t * P:(t + 1) * P], wvo[:, 1, :], start=True, stop=True)
                        i.then_inc(wo_done, 1)
                    if old and h == 15:
                        pe.wait_ge(next_norm, b)
                        for t in range(TB):
                            i = turn(FIN[:, t * P:(t + 1) * P], xnb[:, t, :])
                        i.then_inc(next_turned, 1)
            over_batches(pe, step)

            if upto >= "B":
                pe.wait_ge(next_copied, B + 1)
                pe.wait_ge(small_in, 112)
                for t in range(NT):
                    i = mm(banks[0][:, t * E0:(t + 1) * E0], xmT[:, t * P:(t + 1) * P], gateT, start=True, stop=True)
                i.then_inc(gate_made, 1)
                pe.wait_ge(gate_biased, 1)
                pe.wait_ge(ffn_in, 80)
                pe.sem_inc(h_ready, 2)
                pe.sem_inc(acc_done, 2 * TPG)
                with pe.Fori(0, T // GT // 2) as gg:
                    def up(i):
                        G, e = divmod(i, E0)
                        for c, (h0, m) in enumerate(HCH):
                            k = i * 3 + c
                            K = gg * 54 + k
                            tok = xmT[:, bass.ds((gg * 2 + G) * GT, GT)]
                            pe.wait_ge(h_ready, K + 1)
                            mm(banks[k % 2][0:m, :], w1T[:, e * HID + h0:e * HID + h0 + m], tok, start=True, stop=True)
                            mm(banks[2 + k % 2][0:m, :], w3T[:, e * HID + h0:e * HID + h0 + m], tok, start=True, stop=True).then_inc(up_made, 1)

                    def down(i):
                        e = i % E0
                        N = gg * 2 * E0 + i
                        pe.wait_ge(h_ready, 2 + 3 * N + 3)
                        pe.wait_ge(acc_done, TPG * N + TPG)
                        for t in range(TPG):
                            for c, (h0, m) in enumerate(HCH):
                                j = mm(banks[4 + i % 2][:, t * P:(t + 1) * P], hs[0:m, i % 2, c, t * P:(t + 1) * P], w2s[0:m, e, c, :],
                                       start=(c == 0), stop=(c == 2))
                        j.then_inc(down_made, 1)
                    for i in range(2 * E0):
                        up(i)
                        if i > 0:
                            down(i - 1)
                    down(2 * E0 - 1)
            if upto >= "C":
                for g in range(4):
                    pe.wait_ge(ln_done, 12 + g + 1)
                    for t in range(4):
                        i = turn(banks[g][:, t * P:(t + 1) * P], x_tok[:, 4 * g + t, :])
                    i.then_inc(c_turned, 1)
                pe.wait_ge(c_copied, 4)
                pe.wait_ge(w1_in, 64)

                def project1(n, b, c):
                    at_least(pe, k1_ready, n)
                    mm(KB[:, 0:S], Wkv[:, c * P:(c + 1) * P], xcT[:, bass.ds(b * S, S)], start=True, stop=True)
                    mm(KB[:, S:KV], Wkv[:, c * P:(c + 1) * P], xnT[:, bass.ds(b * S, S)], start=True, stop=True).then_inc(k1_made, 1)
                    mm(VB[:, 0:S], Wq[:, c * P:(c + 1) * P], xnT[:, bass.ds(b * S, S)], start=True, stop=True).then_inc(q1_made, 1)

                def make_values(n, half, kt):
                    mm(VB[:, :], kvT[:, kt * P:(kt + 1) * P], Wkv[:, INNER + 512 * half:INNER + 512 * (half + 1)],
                       start=True, stop=True).then_inc(v1_made, 1)

                project1(0, 0, 0)
                pe.wait_ge(kv_copied, 2)
                pe.wait_ge(q1_ready, 1)
                for kt in range(3):
                    at_least(pe, v1_ready, kt)
                    make_values(kt, 0, kt)

                def step(b, new, old, more):
                    for h in range(H1):
                        if new:
                            N = H1 * b + h
                            c, r = h // 2, slice(DH1 * (h % 2), DH1 * (h % 2) + DH1)
                            if h % 2 == 0:
                                pe.wait_ge(k1_ready, 8 * b + c + 1)
                                pe.wait_ge(q1_ready, 8 * b + c + 1)
                            for t in range(TB):
                                at_least(pe, exp1_done, TB * (N - 1) + t + 1)
                                mm(SA[t][:, :], QT[r, c % 2, t * P:(t + 1) * P], KT[r, c % 2, :], start=True, stop=True).then_inc(s1_made, 1)
                        head = lagged(b, h, LT1, new, old, H1)
                        if head:
                            bv, v = head
                            V = H1 * bv + v
                            pe.wait_ge(p1_ready, TB * V + TB)
                            for k in range(2):
                                at_least(pe, p1_split, 2 * (V - 1) + k + 1)
                                for j in range(2):
                                    for t in range(TB):
                                        kt = 2 * k + j
                                        i = turn(TU[k][:, (2 * j + t) * P:(2 * j + t + 1) * P], P1[:, v % 4, t, kt * P:(kt + 1) * P])
                                i.then_inc(p1_turned, 1)
                        head = lagged(b, h, LP1, new, old, H1)
                        if head:
                            bv, v = head
                            V = H1 * bv + v
                            if v % 8 == 0:
                                pe.wait_ge(v1_ready, 8 * bv + 4 + 4 * (v // 8))
                            pe.wait_ge(p1_split, 2 * V + 2)
                            at_least(pe, o1_ready, V)
                            for kt in range(4):
                                stationary = V1[:, kt, v].rearrange("p s d -> p (s d)")
                                mm(OB[:, 0:S], stationary, PTh[:, v % 2, kt, :], start=(kt == 0), stop=False)
                                i = mm(OB[:, 0:S], stationary, PTl[:, v % 2, kt, :], start=False, stop=(kt == 3))
                            i.then_inc(pv1_done, 1)
                        if h % 2 == 0 and (new and h < H1 - 2 or more):
                            n = 8 * b + h // 2 + 1
                            made = 8 * b + (3 if h == 0 else min(4 + (h - 2) // 2, 15 if more else 8))
                            at_least(pe, v1_ready, made)
                            if old and h == 8:
                                pe.wait_ge(x3_ready, b)
                            project1(n, b if h < H1 - 2 else b + 1, (h // 2 + 1) % 8)
                        values = values_of(b, h, new, more)
                        if values:
                            last = 8 * b + h // 2 + 2 if (new and h < H1 - 1 or more) else 8 * B
                            pe.wait_ge(q1_ready, last)
                            if h == 11:
                                pe.wait_ge(kv_copied, 2 * (b + 1) + 2)
                            make_values(*values)
                        head = lagged(b, h, LW1, new, old, H1)
                        if head:
                            bv, v = head
                            pe.wait_ge(o1_ready, H1 * bv + v + 1)
                            if v == 0:
                                at_least(pe, outT_ready, bv)
                            mm(WB[:, 0:S], Wout[:, v, :], OT[:, v % 2, :], start=(v == 0), stop=(v == H1 - 1)).then_inc(wout_done, 1)
                        if old and h == 7:
                            pe.wait_ge(outT_ready, b)
                            if new:
                                pe.wait_ge(k1_ready, 8 * b + h // 2 + 2)
                            for t in range(TB):
                                i = turn(KB[:, t * P:(t + 1) * P], outT[:, t * P:(t + 1) * P])
                            i.then_inc(out_turned, 1)
                over_batches(pe, step)

            if upto == "D":
                for g in range(4):
                    pe.wait_ge(ln_done, 16 + g + 1)
                    for t in range(4):
                        i = turn(banks[g][:, t * P:(t + 1) * P], xn_tok[:, 4 * g + t, :])
                    i.then_inc(d_turned, 1)
                for t in range(NT):
                    if t % 4 == 0:
                        pe.wait_ge(d_copied, t // 4 + 1)
                    i = mm(banks[4][:, t * E1:(t + 1) * E1], xmT[:, t * P:(t + 1) * P], WrT, start=True, stop=True)
                i.then_inc(r_made, 1)
                pe.wait_ge(oh_ready, 1)
                oh = oneh[:, :, :].rearrange("p t e -> p (t e)")
                mm(banks[5][:, 0:NT * E1], before, oh, start=True, stop=True)
                mm(banks[5][:, NT * E1:2 * NT * E1], ones[:, :], oh, start=True, stop=True).then_inc(rank_made, 1)
                pe.wait_ge(xe_in, 16)
                pe.wait_ge(slots_ready, 1)
                for g in range(4):
                    for t in range(4):
                        i = turn(banks[g][:, t * P:(t + 1) * P], xe[:, 4 * g + t, :])
                    i.then_inc(xe_turned, 1)
                pe.wait_ge(w1e_in, 160)

                def down1(e):
                    pe.wait_ge(h1_act, e + 1)
                    pe.wait_ge(h1_dve, e + 1)
                    if e >= 2:
                        pe.wait_ge(y1_copied, e - 1)
                    for t in range(2):
                        for c in range(4):
                            i = mm(banks[6 + e % 2][:, t * P:(t + 1) * P], h1[:, e % 2, c, t * P:(t + 1) * P], W2[:, e, c, :], start=(c == 0), stop=(c == 3))
                    i.then_inc(y1_made, 1)
                for e in range(E1):
                    pe.wait_ge(xe_copied, e // 2 + 1)
                    for half in range(2):
                        if e >= 1:
                            pe.wait_ge((h1_act, h1_dve)[half], e)
                        for k in range(2):
                            c = 2 * half + k
                            i = mm(banks[4 + half][:, k * CAP:(k + 1) * CAP], W1[:, e, c * P:(c + 1) * P], xeT[:, e * CAP:(e + 1) * CAP], start=True, stop=True)
                        i.then_inc(h1_made, 1)
                    if e >= 1:
                        down1(e - 1)
                down1(E1 - 1)


_SHAPES = [((B, S, D), "float32")]


def _constants():
    p = np.arange(P)
    ident = np.eye(P)
    before = p[:, None] < p[None, :]
    low = np.stack([-1.0 * (p % 32 >= 16), -1.0 * (p % 16 >= 8)], 1)
    iota = np.broadcast_to(np.arange(E0), (P, E0))
    return np.concatenate([ident, before, low, iota], 1).astype(np.float32)


def kernel(**inputs):
    import concourse.bacc as _bacc
    from concourse import mybir as _mybir
    from concourse.bass_utils import run_bass_kernel_spmd as _run

    i = {k: np.asarray(v) for k, v in inputs.items()}
    L0, F0, L1, F1_ = "L0_xattn_", "L0_ffn_", "L1_xattn_", "L1_ffn_"
    w1 = np.concatenate([i[F0 + "w1"], i[F0 + "new_w1"]], 0)
    w3 = np.concatenate([i[F0 + "w3"], i[F0 + "new_w3"]], 0)
    w2 = np.concatenate([i[F0 + "w2"], i[F0 + "new_w2"]], 0)
    laid = {
        "const": _constants(),
        "x": i["x"].reshape(T, D),
        "ctx": i["ctx_1024"].reshape(T, D),
        "ctxT": i["ctx_1024"].reshape(T, D).T,
        "mask": i["mask_Bx16xSxS2_ff0"].reshape(B * H0, S, S),
        "W_q": i[L0 + "W_q"], "W_k": i[L0 + "W_k"], "W_v": i[L0 + "W_v"], "W_o": i[L0 + "W_o"],
        "lambda_q1": i[L0 + "lambda_q1"].reshape(1, -1), "lambda_k1": i[L0 + "lambda_k1"].reshape(1, -1),
        "lambda_q2": i[L0 + "lambda_q2"].reshape(1, -1), "lambda_k2": i[L0 + "lambda_k2"].reshape(1, -1),
        "rms_scale": i[L0 + "rms_scale"].reshape(1, -1),
        "w1T": w1.reshape(E0 * HID, D).T, "w3T": w3.reshape(E0 * HID, D).T,
        "w2T": w2.transpose(0, 2, 1),
        "gateT": np.concatenate([i[F0 + "gate_weight"], i[F0 + "new_gate_weight"]], 0).T,
        "gate_bias": i[F0 + "gate_bias"].reshape(1, 1),
        "g1": i[L1 + "g1"].reshape(D, 1), "b1": i[L1 + "b1"].reshape(D, 1),
        "g2": i[L1 + "g2"].reshape(D, 1), "b2": i[L1 + "b2"].reshape(D, 1),
        "Wq": i[L1 + "Wq"], "Wkv": i[L1 + "Wkv"], "Wout": i[L1 + "Wout"],
        "Wr": i[F1_ + "Wr"], "W1": i[F1_ + "W1"], "W2": i[F1_ + "W2"],
    }
    nc = _bacc.Bacc("TRN2", target_bir_lowering=False, num_devices=1)
    arrays, args = {}, {}
    for name, v in laid.items():
        v = np.ascontiguousarray(v)
        arrays[f"in_{name}"] = v
        args[name] = nc.dram_tensor(f"in_{name}", v.shape, _mybir.dt.from_np(v.dtype), kind="ExternalInput").ap()
    o = nc.dram_tensor("out_x", (T, D), _mybir.dt.float32, kind="ExternalOutput").ap()
    build(nc, args, o, "D")
    r = _run(nc, [arrays], core_ids=[0])
    return r.results[0]["out_x"].reshape(B, S, D)
```

```python
from contextlib import ExitStack

import numpy as np

import concourse.bass as bass
from concourse import mybir

F32 = mybir.dt.float32
R32 = mybir.dt.float32r
U32 = mybir.dt.uint32
ALU = mybir.AluOpType
ACT = mybir.ActivationFunctionType
X = mybir.AxisListType.X

P = 128
B, S, D = 8, 256, 128
T = B * S
NT = T // P
TB = S // P
LOWEST = -3.0e38

H0, DH0 = 16, 8
SLOTS = 2 * H0 // 4
LAMBDA_INIT = 0.8
EPS = 1e-5

E0, HID = 9, 352
HCH = [(0, 128), (128, 128), (256, 96)]
GT = 512
TPG = GT // P

H1, DH1 = 16, 64
INNER = H1 * DH1
KV = 2 * S
SCALE1 = float(1.0 / np.sqrt(np.sqrt(DH1)))

E1, F1 = 8, 512
CAP = T // E1


def at_least(eng, sem, value):
    if isinstance(value, int) and value <= 0:
        return
    eng.wait_ge(sem, value)


def hold(eng, sem, value, passed):
    if isinstance(value, int):
        at_least(eng, sem, value)
    else:
        eng.wait_ge(sem, value)
        eng.sem_inc(passed, 1)


class OwnSteps:

    def __init__(self, eng, sem):
        self.eng, self.sem, self.n, self.base = eng, sem, 0, 0

    def did(self, instruction):
        instruction.then_inc(self.sem, 1)
        self.n += 1

    def settle(self):
        self.eng.wait_ge(self.sem, self.base + self.n)

    def loop(self, register, first, per_turn):
        self.start = self.n
        self.per_turn = per_turn
        self.base = (register - first) * per_turn if first else register * per_turn

    def end_loop(self, turns):
        assert self.n - self.start == self.per_turn, (self.n - self.start, self.per_turn)
        self.n = self.start + turns * self.per_turn
        self.base = 0


def bc(ap, n):
    return ap.unsqueeze(len(ap.shape)).to_broadcast([*ap.shape, n])


def build(nc, a, out):
    with ExitStack() as ctx:
        def sb(name, shape, dt=F32):
            return ctx.enter_context(nc.sbuf_tensor(name, shape, dt))

        def bank(name):
            return ctx.enter_context(nc.psum_tensor(name, [P, 512], F32))

        def sem(name):
            return ctx.enter_context(nc.semaphore(name))

        x = sb("x", [P, NT, D])
        const = sb("const", [P, 2 * P + 3 + E0])
        ident = const[:, 0:P]
        before = const[:, P:2 * P]
        low_part = const[:, 2 * P:2 * P + 3]
        iota9 = const[:, 2 * P + 3:2 * P + 3 + E0]
        ctxT = sb("ctxT", [P, T])
        OT = ctxT[:, 0:2 * S].rearrange("p (r q) -> p r q", r=2)
        outT = ctxT[:, 2 * S:3 * S]
        xnT = sb("xnT", [P, T])
        xmT = sb("xmT", [P, T])
        xcT = sb("xcT", [P, T])
        SPLIT1 = 10 * INNER
        with nc.sbuf_tensor("ffnw", [P, SPLIT1], F32) as ffnw:
            pass
        split1 = sb("split1", [P, SPLIT1], R32)
        W1h, W1l = (split1[:, k * 5 * INNER:(k + 1) * 5 * INNER] for k in range(2))
        w1T = ffnw[:, 0:E0 * HID]
        w3T = ffnw[:, E0 * HID:2 * E0 * HID]
        w2s = ffnw[:, 2 * E0 * HID:2 * E0 * HID + 3 * E0 * D].rearrange("p (e c d) -> p e c d", e=E0, c=3)
        W1 = ffnw[:, 0:E1 * F1].rearrange("p (e f) -> p e f", e=E1)
        W2 = ffnw[:, E1 * F1:2 * E1 * F1].rearrange("p (e c d) -> p e c d", e=E1, d=D)
        wqk = sb("wqk", [P, 2, 2 * P])
        twice = sb("twice", [P, 2 * INNER])
        wqk4 = twice[:, :].rearrange("p (k i r d) -> p k i r d", k=2, r=4, d=DH0)
        Wout = twice[:, :].rearrange("p (h d) -> p h d", d=D)
        wvo = sb("wvo", [P, 2, P])
        with nc.sbuf_tensor("shared", [P, 4 * INNER], F32) as shared:
            pass
        keys1 = sb("keys1", [P, 4 * INNER], R32)
        KH, KL = (keys1[:, k * INNER:(k + 1) * INNER].rearrange("p (r k) -> p r k", r=2) for k in range(2))
        kvh, kvl = (keys1[:, 2 * INNER + k * KV:2 * INNER + (k + 1) * KV] for k in range(2))
        VZ = shared[:, :].rearrange("p (t h n) -> p t h n", t=TB, h=H0)
        W1raw = shared[:, 0:3 * INNER]
        qk = sb("qk", [P, SLOTS, 2 * S], R32)
        high = sb("high", [P, 2, 2 * S], R32)
        QH, QS = (high[:, k, :].rearrange("p (r q) -> p r q", r=2) for k in range(2))
        small = sb("small", [P, 1024])
        work = sb("work", [P, 6144])
        LATE = 4 * H1 * 2 * DH1
        with nc.sbuf_tensor("late", [P, LATE], F32) as late:
            pass
        v1_split = sb("v1_split", [P, LATE], R32)

        masks = work[:, 0:4096].rearrange("p (r h t k) -> p r h t k", r=4, h=2, t=TB)
        zs = late[:, 0:4096].rearrange("p (r s t k) -> p r s t k", r=4, s=2, t=TB)
        AT = late[:, 4096:5120].rearrange("p (r k q) -> p r k q", r=2, k=TB)
        V0 = work[:, 4096:6144].rearrange("p (t n) -> p t n", t=NT)
        at = 5120
        o1 = late[:, at:at + 256]
        o2 = late[:, at + 256:at + 512]
        oT = late[:, at + 512:at + 768]
        lnw = late[:, at + 768:at + 768 + 512].rearrange("p (k t d) -> p k t d", k=2, t=TB)
        xnb = sb("xnb", [P, TB, D])
        ctx_tok = work[:, 0:NT * D].rearrange("p (t d) -> p t d", t=NT)
        x_tok = work[:, NT * D:2 * NT * D].rearrange("p (t d) -> p t d", t=NT)
        squares = late[:, 6400:7424].rearrange("p (r t d) -> p r t d", r=2, d=D)
        hs = work[:, 0:3072].rearrange("p (r c n) -> p r c n", r=2, c=3)
        sil = work[:, 3072:4096].rearrange("p (r n) -> p r n", r=2)
        P1 = work[:, 0:4 * TB * KV].rearrange("p (r t k) -> p r t k", r=4, t=TB)
        V1 = v1_split[:, :].rearrange("p (t h s d) -> p t h s d", t=4, h=H1, s=2)
        PTh, PTl = (qk[:, 4 * k:4 * k + 4, :].rearrange("p s n -> p (s n)").rearrange("p (r t q) -> p r t q", r=2, t=4) for k in range(2))
        xn_tok = work[:, 0:2048].rearrange("p (t d) -> p t d", t=NT)
        xe = work[:, 2048:4096].rearrange("p (t d) -> p t d", t=NT)
        xeT = work[:, 4096:6144]
        h1 = late[:, 0:2048].rearrange("p (r c n) -> p r c n", r=2, c=4)
        ye = late[:, 2048:4096].rearrange("p (t d) -> p t d", t=NT)
        yg = late[:, 4096:6144].rearrange("p (t d) -> p t d", t=NT)

        off = 0
        def tiny(n):
            nonlocal off
            off += n
            return small[:, off - n:off]
        rowmax = tiny(16).rearrange("p (r i) -> p r i", r=4)
        negmax = tiny(16).rearrange("p (r i) -> p r i", r=4)
        rowsum = tiny(16).rearrange("p (r i) -> p r i", r=4)
        coef = tiny(8).rearrange("p (r t) -> p r t", t=TB)
        rsum = tiny(64).rearrange("p (h s t) -> p h s t", s=2, t=TB)
        r1_old = tiny(32).rearrange("p (t h) -> p t h", t=TB)
        lam_in = sb("lam_in", [P, 4, H0 * DH0])
        lam = tiny(32).rearrange("p (k h) -> p k h", k=2)
        rms_w = tiny(DH0)
        ms = tiny(32)
        rr = tiny(32)
        minus_half = tiny(32)
        mean = tiny(2)
        var = tiny(2)
        rstd = tiny(2)
        g1b1 = tiny(4)
        bias9 = tiny(E0)
        gateT = tiny(E0)
        WrT = tiny(E1)
        nm1 = tiny(8).rearrange("p (r t) -> p r t", t=TB)
        sum1 = tiny(8).rearrange("p (r t) -> p r t", t=TB)
        rc1 = tiny(8).rearrange("p (r t) -> p r t", t=TB)
        means = tiny(8).rearrange("p (r t) -> p r t", r=2)
        vars_ = tiny(8).rearrange("p (r t) -> p r t", r=2)
        rstds = tiny(8).rearrange("p (r t) -> p r t", r=2)
        routing = sb("routing", [P, 1024])
        used = 0
        def entries(n):
            nonlocal used
            used += n
            return routing[:, used - n:used]
        score9 = entries(NT * E0).rearrange("p (t e) -> p t e", e=E0)
        cw = entries(NT * E0).rearrange("p (t e) -> p t e", e=E0)
        tmp9 = entries(NT * E0).rearrange("p (t e) -> p t e", e=E0)
        top8 = entries(NT * 8).rearrange("p (t e) -> p t e", e=8)
        idx8 = sb("idx8", [P, NT, 8], U32)
        idx_f = entries(NT * 2).rearrange("p (k t) -> p k t", k=2)
        wk = entries(NT * 2).rearrange("p (k t) -> p k t", k=2)
        wsum = entries(NT)
        keep = entries(NT)
        slot_f = entries(NT)
        slot_i = sb("slot_i", [P, NT], mybir.dt.uint32)
        zeros = sb("zeros", [P, 512])
        ones = sb("ones", [P, P])
        probs8 = entries(NT * E1).rearrange("p (t e) -> p t e", e=E1)
        oneh = sb("oneh", [P, NT, E1])
        sums = sb("sums", [P, 2, NT, E1])

        xe_dram = nc.dram_tensor("xe_scratch", [E1 * CAP, D], F32, kind="Internal").ap()
        ye_dram = nc.dram_tensor("ye_scratch", [E1 * CAP, D], F32, kind="Internal").ap()

        banks = [bank(f"bank{i}") for i in range(8)]
        SC, PT, FIN, PROJ, PO = banks[0:4], banks[4], banks[5], banks[6], banks[7]

        def sems(names):
            return [sem(n) for n in names.split()]

        const_in, x_in, ctx_in, ctxT_in, w0_in, lam_sem, small_in = sems("const_in x_in ctx_in ctxT_in w0_in lam_sem small_in")
        ffn_in, w1_in, w1e_in = sems("ffn_in w1_in w1e_in")
        mask_in = [sem(f"mask_in{r}") for r in range(4)]
        dve_own = sem("dve_own")
        passed_dve, passed_pool, passed_act = sems("passed_dve passed_pool passed_act")
        setup_done, wqk4_ready, lam_sum, lam_exp = sems("setup_done wqk4_ready lam_sum lam_exp")
        ln_centred, ln_squared, ln_var, ln_rstd, ln_done = sems("ln_centred ln_squared ln_var ln_rstd ln_done")
        next_var, next_rstd = sems("next_var next_rstd")
        rms_scaled, mean_ready, centred, deviated = sems("rms_scaled mean_ready centred deviated")
        prep_turned, prep_copied = sems("prep_turned prep_copied")
        v0_made, v0_copied = sems("v0_made v0_copied")
        proj_made, high_ready, stack_ready = sems("proj_made high_ready stack_ready")
        scores_made, rowmax_done, negmax_ready, exp_done = sems("scores_made rowmax_done negmax_ready exp_done")
        coef_ready, pv_read, weighed, attn_ready, attn_ready_pool, attn_turned, attnT_ready, pv_done, sums_copied, sums_turned, vz_ready = sems(
            "coef_ready pv_read weighed attn_ready attn_ready_pool attn_turned attnT_ready pv_done sums_copied sums_turned vz_ready")
        rms_in, rms_out, heads_ready, heads_turned, headsT_ready, wo_done, wo_added = sems("rms_in rms_out heads_ready heads_turned headsT_ready wo_done wo_added")
        next_norm, next_turned, next_copied = sems("next_norm next_turned next_copied")
        gate_made, gate_biased, gate_sig, cw_ready = sems("gate_made gate_biased gate_sig cw_ready")
        up_made, silu_done, h_ready, down_made, acc_done = sems("up_made silu_done h_ready down_made acc_done")
        c_turned, c_copied, w1_high, w1_split, kv_high, kv_split, k1_high, q1_high, k1_made, q1_made, k1_ready, q1_ready = sems(
            "c_turned c_copied w1_high w1_split kv_high kv_split k1_high q1_high k1_made q1_made k1_ready q1_ready")
        v1_made, v1_high, v1_ready = sems("v1_made v1_high v1_ready")
        s1_made, nm1_ready, exp1_done, rc1_ready, p1_ready, p1_turned, p1_high, p1_split = sems(
            "s1_made nm1_ready exp1_done rc1_ready p1_ready p1_turned p1_high p1_split")
        pv1_done, o1_ready, wout_done, outT_ready, out_turned, x3_ready = sems(
            "pv1_done o1_ready wout_done outT_ready out_turned x3_ready")
        d_turned, d_copied, r_made, r_shift, r_exp = sems("d_turned d_copied r_made r_shift r_exp")
        oh_ready, rank_made, slots_ready = sems("oh_ready rank_made slots_ready")
        zero_ready, zeroed, scattered, xe_in, xe_turned, xe_copied = sems("zero_ready zeroed scattered xe_in xe_turned xe_copied")
        h1_made, h1_act, h1_dve, y1_made, y1_copied, ye_out = sems("h1_made h1_act h1_dve y1_made y1_copied ye_out")
        yg_zero, y_ready, stored = sems("yg_zero y_ready stored")
        gathered = [sem(f"gathered{q}") for q in range(4)]

        LC, LT, LA, LP = 2, 4, 4, 5
        LR1, LT1, LP1, LO1, LW1 = 1, 2, 3, 4, 5

        out_rows = out.rearrange("(t p) d -> p t d", p=P)
        mask_rows = a["mask"].rearrange("n (t p) k -> p n t k", p=P)

        SA, TU, KB, VB, OB, WB = banks[0:2], banks[2:4], banks[4], banks[5], banks[6], banks[7]

        pieces1 = [(0, 0, SCALE1), (0, 1, SCALE1), (1, 0, SCALE1), (1, 1, SCALE1), (2, 0, 1.0)]

        def weight1(w, k, r):
            if k < 2:
                return w[:, 2 * k * INNER:2 * (k + 1) * INNER].rearrange("p (h r d) -> p h r d", r=2, d=DH1)[:, :, r, :]
            return w[:, 4 * INNER:5 * INNER].rearrange("p (h d) -> p h d", d=DH1)

        def raw1(k):
            return W1raw[:, k * INNER:(k + 1) * INNER].rearrange("p (h d) -> p h d", d=DH1)

        def values_of(b, h, new, more):
            if h <= 2:
                return (8 * b + 1 + h, 0, 1 + h) if new else None
            if h in (3, 5, 7, 9):
                return (8 * b + 4 + (h - 3) // 2, 1, (h - 3) // 2) if new else None
            return (8 * (b + 1), 0, 0) if h == 15 and more else None

        def values_made(b, h, more):
            return 8 * b + (h + 2 if h <= 3 else min(5 + (h - 3) // 2, 8) if h < 15 or not more else 9)

        def projects(h, new, more):
            return new and h < H1 - 2 or more

        block = ctx.enter_context(nc.Block())

        def over_batches(eng, step, own=None, per_turn=0):
            step(0, True, False, True)
            with eng.Fori(1, B - 1) as b:
                if own:
                    own.loop(b, 1, per_turn)
                step(b, True, True, True)
            if own:
                own.end_loop(B - 2)
            step(B - 1, True, True, False)
            step(B, False, True, False)

        def lagged(b, u, lag, new, old, units):
            if u >= lag:
                return (b, u - lag) if new else None
            return (b - 1, u - lag + units) if old else None

        @block.sync
        def _(sp):
            def load(dst, src, s):
                sp.dma_start(dst, src).then_inc(s, 16)

            load(ctx_tok, a["ctx"].rearrange("(t p) d -> p t d", p=P), ctx_in)
            load(x[:, :, :], a["x"].rearrange("(t p) d -> p t d", p=P), x_in)
            load(wqk[:, 0, :], a["W_q"], w0_in)
            load(wqk[:, 1, :], a["W_k"], w0_in)
            load(wvo[:, 0, :], a["W_v"], w0_in)
            load(wvo[:, 1, :], a["W_o"], w0_in)
            load(ctxT[:, :], a["ctxT"], ctxT_in)

            sp.wait_ge(prep_turned, 8)

            def step(b, new, old, more):
                if not new:
                    return
                for pair in range(H0 // 2):
                    at_least(sp, rowmax_done, 4 * H0 * b + 8 * (pair - 3))
                    sp.dma_start(masks[:, pair % 4], mask_rows[:, bass.ds(b * H0 + 2 * pair, 2)]).then_inc(mask_in[pair % 4], 16)
                if isinstance(b, int) and b == 0:
                    load(w1T, a["w1T"], ffn_in)
                    load(w3T, a["w3T"], ffn_in)
                    for c, (h0, m) in enumerate(HCH):
                        load(w2s[0:m, :, c, :], a["w2T"][:, h0:h0 + m, :].rearrange("e p d -> p e d"), ffn_in)
            over_batches(sp, step)
            sp.wait_ge(pv_done, H0 * B)
            load(W1raw[:, 0:INNER], a["Wq"], w1_in)
            load(W1raw[:, INNER:], a["Wkv"], w1_in)
            for half in range(2):
                load(Wout[half * DH1:(half + 1) * DH1], a["Wout"].rearrange("(h p) d -> p h d", p=DH1), w1_in)

            sp.wait_ge(acc_done, 2 * TPG + TPG * E0 * (T // GT))
            sp.wait_ge(x3_ready, B)
            for e0 in (0, 4):
                load(W1[:, e0:e0 + 4], a["W1"][e0:e0 + 4].rearrange("e d f -> d e f"), w1e_in)
                for e in range(e0, e0 + 4):
                    load(W2[:, e], a["W2"][e].rearrange("(c p) d -> p c d", p=P), w1e_in)
            sp.wait_ge(scattered, 16 * NT)
            load(xe, xe_dram.rearrange("(t p) d -> p t d", p=P), xe_in)
            for e in range(E1):
                sp.wait_ge(y1_copied, e + 1)
                sp.dma_start(ye_dram.rearrange("(t p) d -> p t d", p=P)[:, 2 * e:2 * e + 2], ye[:, 2 * e:2 * e + 2, :]).then_inc(ye_out, 16)
            for q in range(4):
                sp.wait_ge(y_ready, q + 1)
                sp.dma_start(out_rows[:, 4 * q:4 * q + 4], x[:, 4 * q:4 * q + 4, :]).then_inc(stored, 16)
            sp.wait_ge(stored, 64)

        @block.gpsimd
        def _(pool):
            pool.memset(minus_half, -0.5).then_inc(setup_done, 1)
            pool.memset(bias9[:, 0:E0 - 1], 0.0).then_inc(setup_done, 1)
            pool.memset(shared[:, :], 0.0).then_inc(setup_done, 1)
            pool.memset(ones[:, :], 1.0).then_inc(setup_done, 1)
            pool.memset(zeros[:, :], 0.0).then_inc(zero_ready, 1)
            pool.dma_start(const[:, :], a["const"]).then_inc(const_in, 16)
            for n, name in enumerate(("lambda_q1", "lambda_k1", "lambda_q2", "lambda_k2")):
                pool.dma_start(lam_in[:, n, :], a[name].to_broadcast([P, H0 * DH0])).then_inc(lam_sem, 16)
            pool.dma_start(rms_w, a["rms_scale"].to_broadcast([P, DH0])).then_inc(lam_sem, 16)
            for n, name in enumerate(("g1", "b1", "g2", "b2")):
                pool.dma_start(g1b1[:, n:n + 1], a[name]).then_inc(small_in, 16)
            pool.dma_start(bias9[:, E0 - 1:E0], a["gate_bias"].to_broadcast([P, 1])).then_inc(small_in, 16)
            pool.dma_start(gateT, a["gateT"]).then_inc(small_in, 16)
            pool.dma_start(WrT, a["Wr"]).then_inc(small_in, 16)
            pool.wait_ge(zero_ready, 1)
            for q in range(4):
                pool.dma_start(xe_dram.rearrange("(p t) d -> p (t d)", p=P)[:, 512 * q:512 * q + 512], zeros[:, :]).then_inc(zeroed, 16)

            def inverse_roots(first, n):
                for k in range(first, first + n):
                    pool.wait_ge(ln_var, k + 1)
                    pool.tensor_tensor(rstds[:, k % 2], vars_[:, k % 2], minus_half[:, 0:4], ALU.pow).then_inc(ln_rstd, 1)

            pool.wait_ge(setup_done, 4)
            inverse_roots(0, 8)

            def place_values(b):
                for t in range(TB):
                    dst = VZ[:, t].rearrange("p h n -> p (h n)")
                    dst = bass.AP(dst.tensor, dst.offset, [dst.ap[0], [P + DH0, H0], [1, DH0]])
                    pool.tensor_copy(dst, V0[:, bass.ds(b * TB + t, 1), :].rearrange("p a (h d) -> p (a h) d", d=DH0)).then_inc(vz_ready, 1)

            pool.wait_ge(v0_copied, 4)

            def step(b, new, old, more):
                oh = o1.rearrange("p (h d) -> p h d", d=DH0)
                for h in range(H0):
                    item = lagged(b, h, LC, new, old, H0)
                    if item:
                        bv, v = item
                        hold(pool, coef_ready, H0 * bv + v + 1, passed_pool)
                        pool.tensor_scalar(zs[:, v % 4, 1, 1, :], zs[:, v % 4, 1, 1, :], coef[:, v % 4, 1:2], 1.0, ALU.mult, ALU.mult).then_inc(weighed, 1)
                        hold(pool, weighed, H0 * bv + v + 1, passed_pool)
                        pool.tensor_tensor(zs[:, v % 4, 0, 1, :], zs[:, v % 4, 0, 1, :], zs[:, v % 4, 1, 1, :], ALU.add).then_inc(attn_ready_pool, 1)
                    if new and h == 4:
                        if old:
                            hold(pool, pv_done, H0 * b, passed_pool)
                        place_values(b)
                    if old and h in (6, 7):
                        if h == 6:
                            hold(pool, rms_in, b, passed_pool)
                        part = slice(16 * (h - 6), 16 * (h - 5))
                        pool.tensor_tensor(rr[:, part], ms[:, part], minus_half[:, part], ALU.pow).then_inc(rms_out, 1)
                    if old and h == 8:
                        hold(pool, rms_out, 2 * b, passed_pool)
                        pool.tensor_tensor(oh, oh, bc(rr, DH0), ALU.mult).then_inc(rms_scaled, 1)
                        hold(pool, rms_scaled, b, passed_pool)
                        pool.tensor_tensor(oh, oh, rms_w.unsqueeze(1).to_broadcast([P, 32, DH0]), ALU.mult).then_inc(heads_ready, 1)
                    if old and h == 12:
                        hold(pool, mean_ready, b, passed_pool)
                        pool.tensor_tensor(lnw[:, 0], x[:, bass.ds((b - 1) * TB, TB), :], bc(mean, D), ALU.subtract).then_inc(centred, 1)
                        hold(pool, centred, b, passed_pool)
                        pool.tensor_tensor(lnw[:, 1], lnw[:, 0], lnw[:, 0], ALU.mult).then_inc(deviated, 1)
                    if old and h == 13:
                        hold(pool, next_var, b, passed_pool)
                        pool.tensor_tensor(rstd, var, minus_half[:, 0:2], ALU.pow).then_inc(next_rstd, 1)
                        hold(pool, next_rstd, b, passed_pool)
                        pool.tensor_tensor(xnb[:, :, :], lnw[:, 0], bc(rstd, D), ALU.mult).then_inc(next_norm, 1)
            over_batches(pool, step)

            inverse_roots(8, 8)

            def step(b, new, old, more):
                for h in range(H1):
                    head = lagged(b, h, LR1, new, old, H1)
                    if head:
                        bv, v = head
                        hold(pool, rc1_ready, H1 * bv + v + 1, passed_pool)
                        for t in range(TB):
                            pool.tensor_scalar(P1[:, v % 4, t, :], P1[:, v % 4, t, :], rc1[:, v % 4, t:t + 1], 1.0,
                                               ALU.mult, ALU.mult).then_inc(p1_ready, 1)
            over_batches(pool, step)
            inverse_roots(16, 4)
            pool.memset(yg, 0.0).then_inc(yg_zero, 1)
            pool.wait_ge(slots_ready, 1)
            pool.wait_ge(ln_done, 20)
            pool.wait_ge(zeroed, 64)
            for t in range(NT):
                pool.indirect_dma_start(xe_dram, bass.IndirectOffsetOnAxis(slot_i[:, t:t + 1], 0), xn_tok[:, t, :], None,
                                        bounds_check=E1 * CAP - 1, oob_is_err=False).then_inc(scattered, 16)
            pool.wait_ge(yg_zero, 1)
            pool.wait_ge(ye_out, 16 * E1)
            for t in range(NT):
                pool.indirect_dma_start(yg[:, t, :], None, ye_dram, bass.IndirectOffsetOnAxis(slot_i[:, t:t + 1], 0),
                                        bounds_check=E1 * CAP - 1, oob_is_err=False).then_inc(gathered[t // 4], 16)

        @block.vector
        def _(dve):
            own = OwnSteps(dve, dve_own)
            did, settle = own.did, own.settle

            def normalise(first, chunks):
                n = len(chunks)
                for i in range(n + 2):
                    if i < n:
                        src, dst = chunks[i]
                        m = means[:, (first + i) % 2]
                        if i >= 4:
                            dve.wait_ge(ln_done, first + i - 3)
                        did(dve.tensor_reduce(m, src, X, ALU.add))
                        settle()
                        did(dve.tensor_scalar(m, m, 1.0 / D, None, ALU.mult))
                        settle()
                        dve.tensor_tensor(dst, src, bc(m, D), ALU.subtract).then_inc(ln_centred, 1)
                    if 0 <= i - 1 < n:
                        k = first + i - 1
                        dve.wait_ge(ln_squared, k + 1)
                        did(dve.tensor_reduce(vars_[:, k % 2], squares[:, k % 2], X, ALU.add))
                        settle()
                        dve.tensor_scalar(vars_[:, k % 2], vars_[:, k % 2], 1.0 / D, EPS, ALU.mult, ALU.add).then_inc(ln_var, 1)
                    if i >= 2:
                        k = first + i - 2
                        dst = chunks[i - 2][1]
                        dve.wait_ge(ln_rstd, k + 1)
                        dve.tensor_tensor(dst, dst, bc(rstds[:, k % 2], D), ALU.mult).then_inc(ln_done, 1)

            dve.wait_ge(w0_in, 64)
            for k, scale in enumerate((float(1.0 / np.sqrt(DH0)), 1.0)):
                dve.tensor_scalar(wqk4[:, k], wqk[:, k, :].rearrange("p (i d) -> p i d", d=DH0).unsqueeze(2).to_broadcast([P, 32, 4, DH0]),
                                  scale, None, ALU.mult).then_inc(wqk4_ready, 1)
            dve.wait_ge(lam_sem, 80)
            for k in range(2):
                did(dve.tensor_tensor(lam_in[:, 2 * k, :], lam_in[:, 2 * k, :], lam_in[:, 2 * k + 1, :], ALU.mult))
                settle()
                dve.tensor_reduce(lam[:, k, :], lam_in[:, 2 * k, :].rearrange("p (h d) -> p h d", d=DH0), X, ALU.add).then_inc(lam_sum, 1)
            dve.wait_ge(lam_exp, 1)
            did(dve.tensor_tensor(lam[:, 0, :], lam[:, 0, :], lam[:, 1, :], ALU.subtract))
            settle()
            did(dve.tensor_scalar(lam[:, 0, :], lam[:, 0, :], LAMBDA_INIT, -1.0, ALU.add, ALU.mult))
            did(dve.tensor_scalar(rms_w, rms_w, 1.0 - LAMBDA_INIT, None, ALU.mult))
            settle()
            dve.wait_ge(setup_done, 4)
            for g in range(4):
                dve.wait_ge(v0_made, g + 1)
                dve.tensor_copy(V0[:, 4 * g:4 * g + 4, :], banks[g][:, :].rearrange("p (t n) -> p t n", t=4)).then_inc(v0_copied, 1)
            dve.wait_ge(x_in, 16)
            dve.wait_ge(ctx_in, 16)
            four = [slice(4 * g, 4 * g + 4) for g in range(4)]
            normalise(0, [(x[:, g, :], x_tok[:, g, :]) for g in four] + [(ctx_tok[:, g, :], ctx_tok[:, g, :]) for g in four])

            def split(b, sl, PROJ=PROJ):
                dve.wait_ge(high_ready, SLOTS * b + sl + 1)
                for k in range(2):
                    half = slice(k * S, (k + 1) * S)
                    dve.scalar_tensor_tensor(out=qk[:, sl, half], in0=high[:, sl % 2, half].bitcast(F32), scalar=low_part[:, k:k + 1],
                                             in1=PROJ[:, half], op0=ALU.mult, op1=ALU.add).then_inc(stack_ready, 1)

            dve.wait_ge(const_in, 16)
            for sl in range(SLOTS):
                split(0, sl, banks[sl % 4])

            def step(b, new, old, more):
                for h in range(H0):
                    if new:
                        N = H0 * b + h
                        if h % 2 == 0:
                            dve.wait_ge(mask_in[(h // 2) % 4], 16 * (2 * b + h // 8 + 1))
                        at_least(dve, attn_turned, N - 3)
                        hold(dve, scores_made, 2 * N + 2, passed_dve)
                        for s in range(2):
                            for t in range(TB):
                                dve.tensor_tensor_reduce(zs[:, h % 4, s, t, :], SC[2 * (h % 2) + s][:, t * S:(t + 1) * S], masks[:, (h // 2) % 4, h % 2, t, :],
                                                         1.0, LOWEST, ALU.add, ALU.max, rowmax[:, h % 4, 2 * s + t:2 * s + t + 1]).then_inc(rowmax_done, 1)
                        dve.wait_ge(rowmax_done, 4 * N + 4)
                        dve.tensor_scalar(negmax[:, h % 4, :], rowmax[:, h % 4, :], -1.0, None, ALU.mult).then_inc(negmax_ready, 1)
                    if more and h % 2 == 1:
                        split(b + 1, h // 2)
                    item = lagged(b, h, LC, new, old, H0)
                    if item:
                        bv, v = item
                        dve.wait_ge(exp_done, 4 * (H0 * bv + v) + 4)
                        did(dve.reciprocal(rsum[:, v].rearrange("p s t -> p (s t)"), rowsum[:, v % 4, :]))
                        settle()
                        dve.scalar_tensor_tensor(out=coef[:, v % 4, :], in0=rowsum[:, v % 4, 0:2], scalar=lam[:, 0, v:v + 1],
                                                 in1=rsum[:, v, 1, :], op0=ALU.mult, op1=ALU.mult).then_inc(coef_ready, 1)
                        dve.wait_ge(coef_ready, H0 * bv + v + 1)
                        dve.scalar_tensor_tensor(out=zs[:, v % 4, 0, 0, :], in0=zs[:, v % 4, 1, 0, :], scalar=coef[:, v % 4, 0:1],
                                                 in1=zs[:, v % 4, 0, 0, :], op0=ALU.mult, op1=ALU.add).then_inc(attn_ready, 1)
                    if old and h == 1:
                        did(dve.tensor_copy(r1_old, rsum[:, :, 0, :].rearrange("p h t -> p t h")))
                        settle()
                    if old and h == 6:
                        dve.wait_ge(sums_turned, b)
                        i = dve.tensor_tensor(o1.rearrange("p (t h d) -> p t h d", t=TB, d=DH0), FIN[:, 0:S].rearrange("p (t h d) -> p t h d", t=TB, d=DH0),
                                              bc(r1_old, DH0), ALU.mult)
                        i.then_inc(pv_read, 1)
                        dve.wait_ge(pv_read, b)
                        did(dve.tensor_tensor(o2, o1, o1, ALU.mult))
                        settle()
                        did(dve.tensor_reduce(ms, o2.rearrange("p (h d) -> p h d", d=DH0), X, ALU.add))
                        settle()
                        dve.tensor_scalar(ms, ms, 1.0 / DH0, EPS, ALU.mult, ALU.add).then_inc(rms_in, 1)
                    if old and h == 12:
                        dve.wait_ge(wo_done, b)
                        xb = x[:, bass.ds((b - 1) * TB, TB), :]
                        dve.tensor_tensor(xb, FIN[:, 0:S].rearrange("p (t d) -> p t d", t=TB), xb, ALU.add).then_inc(wo_added, 1)
                        hold(dve, wo_added, b, passed_dve)
                        did(dve.tensor_reduce(mean, xb, X, ALU.add))
                        settle()
                        dve.tensor_scalar(mean, mean, 1.0 / D, None, ALU.mult).then_inc(mean_ready, 1)
                    if old and h == 13:
                        dve.wait_ge(deviated, b)
                        did(dve.tensor_reduce(var, lnw[:, 1], X, ALU.add))
                        settle()
                        dve.tensor_scalar(var, var, 1.0 / D, EPS, ALU.mult, ALU.add).then_inc(next_var, 1)
            over_batches(dve, step, own, 21)

            dve.wait_ge(gate_made, 1)
            dve.wait_ge(small_in, 112)
            gate = banks[0][:, 0:NT * E0].rearrange("p (t e) -> p t e", e=E0)
            dve.tensor_tensor(score9, gate, bias9.unsqueeze(1).to_broadcast([P, NT, E0]), ALU.add).then_inc(gate_biased, 1)
            dve.wait_ge(gate_sig, 1)
            for t in range(NT):
                did(dve.max(top8[:, t, :], score9[:, t, :]))
            settle()
            for t in range(NT):
                did(dve.max_index(idx8[:, t, :], top8[:, t, :], score9[:, t, :]))
            settle()
            did(dve.tensor_copy(idx_f, idx8[:, :, 0:2].rearrange("p t k -> p k t")))
            did(dve.tensor_tensor(wsum, top8[:, :, 0], top8[:, :, 1], ALU.add))
            settle()
            did(dve.tensor_scalar(wsum, wsum, 1e-20, None, ALU.add))
            settle()
            did(dve.reciprocal(wsum, wsum))
            settle()
            did(dve.tensor_tensor(wk, top8[:, :, 0:2].rearrange("p t k -> p k t"), wsum.unsqueeze(1).to_broadcast([P, 2, NT]), ALU.mult))
            iota = iota9.unsqueeze(1).to_broadcast([P, NT, E0])
            did(dve.tensor_tensor(cw, iota, bc(idx_f[:, 0], E0), ALU.is_equal))
            did(dve.tensor_tensor(tmp9, iota, bc(idx_f[:, 1], E0), ALU.is_equal))
            settle()
            did(dve.tensor_tensor(cw, cw, bc(wk[:, 0], E0), ALU.mult))
            did(dve.tensor_tensor(tmp9, tmp9, bc(wk[:, 1], E0), ALU.mult))
            settle()
            did(dve.tensor_tensor(cw, cw, tmp9, ALU.add))
            settle()

            with dve.Fori(0, T // GT // 2) as gg:
                def add_expert(i):
                    G, e = divmod(i, E0)
                    N = gg * 2 * E0 + i
                    dve.wait_ge(acc_done, 2 * TPG + TPG * N)
                    dve.wait_ge(down_made, N + 1)
                    for t in range(TPG):
                        tile = gg * 2 * TPG + G * TPG + t
                        xt = x[:, bass.ds(tile, 1), :].rearrange("p a d -> p (a d)")
                        w = cw[:, bass.ds(tile, 1), e:e + 1].rearrange("p a e -> p (a e)")
                        dve.scalar_tensor_tensor(out=xt, in0=banks[4 + i % 2][:, t * P:(t + 1) * P], scalar=w,
                                                 in1=xt, op0=ALU.mult, op1=ALU.add).then_inc(acc_done, 1)
                for i in range(2 * E0):
                    for c, (_, m) in enumerate(HCH):
                        k = i * 3 + c
                        dve.wait_ge(silu_done, gg * 54 + k + 1)
                        dve.tensor_tensor(hs[0:m, i % 2, c, :], banks[2 + k % 2][0:m, :], sil[0:m, k % 2, :], ALU.mult).then_inc(h_ready, 1)
                    if i > 0:
                        add_expert(i - 1)
                add_expert(2 * E0 - 1)
            dve.wait_ge(acc_done, 2 * TPG + TPG * E0 * (T // GT))

            normalise(8, [(x[:, g, :], x_tok[:, g, :]) for g in four] + [(x_tok[:, g, :], x_tok[:, g, :]) for g in four])

            for n, (k, r, scale) in enumerate(pieces1):
                dve.wait_ge(w1_high, n + 1)
                dve.scalar_tensor_tensor(out=weight1(W1l, k, r), in0=raw1(k), scalar=scale, in1=weight1(W1h, k, r).bitcast(F32),
                                         op0=ALU.mult, op1=ALU.subtract).then_inc(w1_split, 1)

            def kv_low(b):
                hold(dve, kv_high, 2 * b + 2, passed_dve)
                for k, rows in enumerate((xcT, xnT)):
                    dve.tensor_tensor(kvl[:, k * S:(k + 1) * S], rows[:, bass.ds(b * S, S)], kvh[:, k * S:(k + 1) * S].bitcast(F32),
                                      ALU.subtract).then_inc(kv_split, 1)

            def kq_low(n, h):
                dve.wait_ge(k1_high, n + 1)
                dve.tensor_tensor(KL[:, h % 2, :], KB[:, :], KH[:, h % 2, :].bitcast(F32), ALU.subtract).then_inc(k1_ready, 1)
                dve.wait_ge(q1_high, n + 1)
                dve.scalar_tensor_tensor(out=QS[:, h % 2, :], in0=QH[:, h % 2, :].bitcast(F32), scalar=low_part[:, 2:3],
                                         in1=VB[:, 0:S], op0=ALU.mult, op1=ALU.add).then_inc(q1_ready, 1)

            def v_low(n, half, kt):
                dve.wait_ge(v1_high, n + 1)
                dve.tensor_tensor(V1[:, kt, 8 * half:8 * half + 8, 1, :], VB[:, :].rearrange("p (h d) -> p h d", d=DH1),
                                  V1[:, kt, 8 * half:8 * half + 8, 0, :].bitcast(F32), ALU.subtract).then_inc(v1_ready, 1)

            kv_low(0)
            kq_low(0, 0)
            kq_low(1, 1)
            v_low(0, 0, 0)

            def step(b, new, old, more):
                for h in range(H1):
                    if new:
                        N = H1 * b + h
                        for t in range(TB):
                            dve.wait_ge(s1_made, TB * N + t + 1)
                            dve.tensor_reduce(nm1[:, h % 4, t:t + 1], SA[t][:, :], X, ALU.max, negate=True).then_inc(nm1_ready, 1)
                    if old and h == 7:
                        dve.wait_ge(out_turned, b)
                        xb = x[:, bass.ds((b - 1) * TB, TB), :]
                        dve.tensor_tensor(xb, KB[:, 0:TB * D].rearrange("p (t d) -> p t d", t=TB), xb, ALU.add).then_inc(x3_ready, 1)
                    head = lagged(b, h, LR1, new, old, H1)
                    if head:
                        bv, v = head
                        dve.wait_ge(exp1_done, TB * (H1 * bv + v) + TB)
                        dve.reciprocal(rc1[:, v % 4, :], sum1[:, v % 4, :]).then_inc(rc1_ready, 1)
                    head = lagged(b, h, LT1, new, old, H1)
                    if head:
                        bv, v = head
                        for k in range(2):
                            dve.wait_ge(p1_high, 2 * (H1 * bv + v) + k + 1)
                            dve.tensor_tensor(PTl[:, v % 2, 2 * k:2 * k + 2, :], TU[k][:, :].rearrange("p (t q) -> p t q", t=2),
                                              PTh[:, v % 2, 2 * k:2 * k + 2, :].bitcast(F32), ALU.subtract).then_inc(p1_split, 1)
                    values = values_of(b, h, new, more)
                    if values:
                        v_low(*values)
                    if projects(h, new, more):
                        kq_low(H1 * b + h + 2, (h + 2) % H1)
                    if more and h == 13:
                        kv_low(b + 1)
            over_batches(dve, step)
            dve.wait_ge(x3_ready, B)

            normalise(16, [(x[:, g, :], xn_tok[:, g, :]) for g in four])
            dve.wait_ge(r_made, 1)
            logits = banks[4][:, 0:NT * E1].rearrange("p (t e) -> p t e", e=E1)
            did(dve.tensor_reduce(wsum, logits, X, ALU.max))
            settle()
            dve.tensor_tensor(probs8, logits, bc(wsum, E1), ALU.subtract).then_inc(r_shift, 1)
            dve.wait_ge(r_exp, 1)
            did(dve.tensor_reduce(wsum, probs8, X, ALU.add))
            settle()
            did(dve.reciprocal(wsum, wsum))
            settle()
            did(dve.tensor_tensor(probs8, probs8, bc(wsum, E1), ALU.mult))
            settle()
            for t in range(NT):
                did(dve.max(top8[:, t, :], probs8[:, t, :]))
            settle()
            for t in range(NT):
                did(dve.max_index(idx8[:, t, :], top8[:, t, :], probs8[:, t, :]))
            settle()
            did(dve.tensor_copy(idx_f[:, 0], idx8[:, :, 0]))
            settle()
            dve.tensor_tensor(oneh[:, :, :], iota9[:, 0:E1].unsqueeze(1).to_broadcast([P, NT, E1]), bc(idx_f[:, 0], E1), ALU.is_equal).then_inc(oh_ready, 1)
            dve.wait_ge(rank_made, 1)
            tile_rank = banks[5][:, 0:NT * E1].rearrange("p (t e) -> p t e", e=E1)
            totals = banks[5][:, NT * E1:2 * NT * E1].rearrange("p (t e) -> p t e", e=E1)
            did(dve.tensor_copy(sums[:, 0], totals))
            settle()
            cur = 0
            for d in (1, 2, 4, 8):
                did(dve.tensor_tensor(sums[:, 1 - cur, d:, :], sums[:, cur, d:, :], sums[:, cur, 0:NT - d, :], ALU.add))
                did(dve.tensor_copy(sums[:, 1 - cur, 0:d, :], sums[:, cur, 0:d, :]))
                settle()
                cur = 1 - cur
            did(dve.tensor_tensor(sums[:, 1 - cur], tile_rank, sums[:, cur], ALU.add))
            settle()
            did(dve.tensor_tensor(sums[:, cur], totals, sums[:, 1 - cur], ALU.subtract))
            settle()
            did(dve.tensor_tensor(sums[:, 1 - cur], sums[:, cur], oneh[:, :, :], ALU.mult))
            settle()
            did(dve.tensor_reduce(keep, sums[:, 1 - cur], X, ALU.add, negate=True))
            settle()
            did(dve.tensor_scalar(slot_f, idx_f[:, 0], float(CAP), None, ALU.mult))
            settle()
            did(dve.tensor_tensor(slot_f, slot_f, keep, ALU.add))
            did(dve.tensor_scalar(keep, keep, float(CAP), float(E1 * CAP), ALU.is_ge, ALU.mult))
            settle()
            did(dve.tensor_tensor(slot_f, slot_f, keep, ALU.add))
            settle()
            dve.tensor_copy(slot_i[:, :], slot_f).then_inc(slots_ready, 1)
            for i in range(2 * E1):
                if i % 2 == 1:
                    dve.wait_ge(h1_made, i + 1)
                    e = i // 2
                    if e >= 2:
                        dve.wait_ge(y1_made, e - 1)
                    dve.tensor_scalar(h1[:, e % 2, 2:4, :], banks[4 + i % 2][:, :].rearrange("p (c n) -> p c n", c=2), 0.0, None,
                                      ALU.max).then_inc(h1_dve, 1)
            for q in range(4):
                dve.wait_ge(gathered[q], 64)
                g = yg[:, 4 * q:4 * q + 4, :]
                did(dve.tensor_tensor(g, g, bc(top8[:, 4 * q:4 * q + 4, 0], D), ALU.mult))
                settle()
                dve.tensor_tensor(x[:, 4 * q:4 * q + 4, :], x[:, 4 * q:4 * q + 4, :], g, ALU.add).then_inc(y_ready, 1)

        @block.scalar
        def _(act):
            act.sem_inc(next_copied, 1)
            act.wait_ge(lam_sum, 2)
            act.activation(lam[:, :, :], lam[:, :, :], ACT.Exp).then_inc(lam_exp, 1)
            act.wait_ge(small_in, 112)

            def square(k, rows):
                act.wait_ge(ln_centred, k + 1)
                if k >= 2:
                    act.wait_ge(ln_var, k - 1)
                act.activation(squares[:, k % 2], rows, ACT.Square).then_inc(ln_squared, 1)

            for k in range(8 + 3):
                if k < 8:
                    square(k, (x_tok, ctx_tok)[k // 4][:, 4 * (k % 4):4 * (k % 4) + 4, :])
                if k >= 3:
                    g = k - 3
                    act.wait_ge(prep_turned, g + 1)
                    if g < 4:
                        act.activation(xnT[:, g * 512:(g + 1) * 512], banks[4 + g % 4][:, :], ACT.Copy).then_inc(prep_copied, 1)
                    else:
                        act.activation(xcT[:, (g - 4) * 512:(g - 3) * 512], banks[4 + g % 4][:, :], ACT.Identity, bias=g1b1[:, 1:2],
                                       scale=g1b1[:, 0:1]).then_inc(prep_copied, 1)

            def high_parts(b, sl, PROJ=PROJ):
                n = SLOTS * b + sl
                act.wait_ge(proj_made, n + 1)
                at_least(act, stack_ready, 2 * (n - 1))
                act.activation(high[:, sl % 2, :], PROJ[:, :], ACT.Copy).then_inc(high_ready, 1)

            for sl in range(SLOTS):
                high_parts(0, sl, banks[sl % 4])

            def step(b, new, old, more):
                for h in range(H0):
                    if more and h % 2 == 1:
                        high_parts(b + 1, h // 2)
                    if old and h == 5:
                        act.wait_ge(pv_done, H0 * b)
                        act.activation(oT, PO[:, 0:S], ACT.Copy).then_inc(sums_copied, 1)
                    if old and h == 11:
                        act.wait_ge(heads_turned, b)
                        act.activation(oT, FIN[:, 0:S], ACT.Copy).then_inc(headsT_ready, 1)
                    item = lagged(b, h, LA, new, old, H0)
                    if item:
                        bv, v = item
                        V = H0 * bv + v
                        act.wait_ge(attn_turned, V + 1)
                        at_least(act, pv_done, V - 1)
                        act.activation(AT[:, v % 2], PT[:, :].rearrange("p (k q) -> p k q", k=TB), ACT.Copy).then_inc(attnT_ready, 1)
                    if new:
                        N = H0 * b + h
                        act.wait_ge(negmax_ready, N + 1)
                        at_least(act, coef_ready, N - 3)
                        for s in range(2):
                            for t in range(TB):
                                k = 2 * s + t
                                act.activation(zs[:, h % 4, s, t, :], zs[:, h % 4, s, t, :], ACT.Exp, bias=negmax[:, h % 4, k:k + 1],
                                               accum_out=rowsum[:, h % 4, k:k + 1]).then_inc(exp_done, 1)
                    if old and h == 15:
                        hold(act, next_turned, b, passed_act)
                        act.activation(xmT[:, bass.ds((b - 1) * S, S)], FIN[:, 0:S], ACT.Copy).then_inc(next_copied, 1)
            over_batches(act, step)

            act.wait_ge(gate_biased, 1)
            act.activation(score9, score9, ACT.Sigmoid).then_inc(gate_sig, 1)
            with act.Fori(0, T // GT // 2) as gg:
                for i in range(2 * E0):
                    for c, (_, m) in enumerate(HCH):
                        k = i * 3 + c
                        act.wait_ge(up_made, gg * 54 + k + 1)
                        act.wait_ge(h_ready, gg * 54 + k + 1)
                        act.activation(sil[0:m, k % 2, :], banks[k % 2][0:m, :], ACT.Silu).then_inc(silu_done, 1)
            for k in range(8):
                square(8 + k, x_tok[:, 4 * (k % 4):4 * (k % 4) + 4, :])
            for g in range(4):
                act.wait_ge(c_turned, g + 1)
                act.activation(xnT[:, g * 512:(g + 1) * 512], banks[g][:, :], ACT.Identity, bias=g1b1[:, 3:4], scale=g1b1[:, 2:3]).then_inc(c_copied, 1)

            act.wait_ge(w1_in, 64)
            act.wait_ge(acc_done, 2 * TPG + TPG * E0 * (T // GT))
            for k, r, scale in pieces1:
                act.activation(weight1(W1h, k, r), raw1(k), ACT.Copy, scale=scale).then_inc(w1_high, 1)

            def kv_highs(b):
                if not (isinstance(b, int) and b == 0):
                    hold(act, q1_made, H1 * b, passed_act)
                for k, rows in enumerate((xcT, xnT)):
                    act.activation(kvh[:, k * S:(k + 1) * S], rows[:, bass.ds(b * S, S)], ACT.Copy).then_inc(kv_high, 1)

            def k_high(n, h):
                act.wait_ge(k1_made, n + 1)
                act.activation(KH[:, h % 2, :], KB[:, :], ACT.Copy).then_inc(k1_high, 1)

            def q_high(n, h):
                act.wait_ge(q1_made, n + 1)
                act.activation(QH[:, h % 2, :], VB[:, 0:S], ACT.Copy).then_inc(q1_high, 1)

            def v_high(n, half, kt):
                act.wait_ge(v1_made, n + 1)
                act.activation(V1[:, kt, 8 * half:8 * half + 8, 0, :], VB[:, :].rearrange("p (h d) -> p h d", d=DH1), ACT.Copy).then_inc(v1_high, 1)

            act.wait_ge(w1_split, len(pieces1))
            kv_highs(0)
            for h in range(2):
                k_high(h, h)
                q_high(h, h)
            v_high(0, 0, 0)

            def step(b, new, old, more):
                for h in range(H1):
                    head = lagged(b, h, LO1, new, old, H1)
                    if head:
                        bv, v = head
                        act.wait_ge(pv1_done, H1 * bv + v + 1)
                        at_least(act, wout_done, H1 * bv + v - 1)
                        act.activation(OT[:, v % 2, :], OB[:, 0:S], ACT.Copy).then_inc(o1_ready, 1)
                    if old and h == 5:
                        act.wait_ge(wout_done, H1 * b)
                        act.activation(outT, WB[:, 0:S], ACT.Copy).then_inc(outT_ready, 1)
                    head = lagged(b, h, LT1, new, old, H1)
                    if head:
                        bv, v = head
                        V = H1 * bv + v
                        at_least(act, pv1_done, V - 1)
                        for k in range(2):
                            act.wait_ge(p1_turned, 2 * V + k + 1)
                            act.activation(PTh[:, v % 2, 2 * k:2 * k + 2, :], TU[k][:, :].rearrange("p (t q) -> p t q", t=2), ACT.Copy).then_inc(p1_high, 1)
                    values = values_of(b, h, new, more)
                    if values:
                        v_high(*values)
                    if new:
                        N = H1 * b + h
                        at_least(act, p1_turned, 2 * (N - 3))
                        for t in range(TB):
                            if t == 1 and projects(h, new, more):
                                k_high(H1 * b + h + 2, (h + 2) % H1)
                            act.wait_ge(nm1_ready, TB * N + t + 1)
                            act.activation(P1[:, h % 4, t, :], SA[t][:, :], ACT.Exp, bias=nm1[:, h % 4, t:t + 1],
                                           accum_out=sum1[:, h % 4, t:t + 1]).then_inc(exp1_done, 1)
                    if projects(h, new, more):
                        q_high(H1 * b + h + 2, (h + 2) % H1)
                    if more and h == 13:
                        kv_highs(b + 1)
            over_batches(act, step)
            for k in range(4):
                square(16 + k, xn_tok[:, 4 * k:4 * k + 4, :])
            for g in range(4):
                act.wait_ge(d_turned, g + 1)
                act.activation(xmT[:, g * 512:(g + 1) * 512], banks[g][:, :], ACT.Copy).then_inc(d_copied, 1)
            act.wait_ge(r_shift, 1)
            act.activation(probs8, probs8, ACT.Exp).then_inc(r_exp, 1)
            for g in range(4):
                act.wait_ge(xe_turned, g + 1)
                act.activation(xeT[:, g * 512:(g + 1) * 512], banks[g][:, :], ACT.Copy).then_inc(xe_copied, 1)
            for i in range(2 * E1):
                e = i // 2
                if i % 2 == 0:
                    act.wait_ge(h1_made, i + 1)
                    if e >= 2:
                        act.wait_ge(y1_made, e - 1)
                    act.activation(h1[:, e % 2, 0:2, :], banks[4 + i % 2][:, :].rearrange("p (c n) -> p c n", c=2), ACT.Relu).then_inc(h1_act, 1)
                elif e >= 1:
                    act.wait_ge(y1_made, e)
                    act.activation(ye[:, 2 * (e - 1):2 * e, :], banks[6 + (e - 1) % 2][:, 0:2 * D].rearrange("p (t d) -> p t d", t=2), ACT.Copy).then_inc(y1_copied, 1)
            act.wait_ge(y1_made, E1)
            act.activation(ye[:, 2 * (E1 - 1):2 * E1, :], banks[6 + (E1 - 1) % 2][:, 0:2 * D].rearrange("p (t d) -> p t d", t=2), ACT.Copy).then_inc(y1_copied, 1)

        @block.tensor
        def _(pe):
            mm = pe.matmul
            pe.wait_ge(ctxT_in, 16)
            pe.wait_ge(w0_in, 64)
            for t in range(NT):
                i = mm(banks[t // 4][:, (t % 4) * P:(t % 4 + 1) * P], ctxT[:, t * P:(t + 1) * P], wvo[:, 0, :], start=True, stop=True)
                if t % 4 == 3:
                    i.then_inc(v0_made, 1)
            pe.wait_ge(const_in, 16)

            def turn(dst, src):
                return pe.transpose(dst, src, ident)

            for g in range(8):
                pe.wait_ge(ln_done, g + 1)
                if g >= 4:
                    pe.wait_ge(prep_copied, g - 3)
                for t in range(4):
                    i = turn(banks[4 + g % 4][:, t * P:(t + 1) * P], (x_tok, ctx_tok)[g // 4][:, 4 * (g % 4) + t, :])
                i.then_inc(prep_turned, 1)

            def project(b, sl, PROJ=PROJ, reused=1):
                n = SLOTS * b + sl
                at_least(pe, stack_ready, 2 * (n + 1 - reused))
                mm(PROJ[:, 0:S], wqk4[:, 0, 4 * sl:4 * sl + 4].rearrange("p i r d -> p (i r d)"), xnT[:, bass.ds(b * S, S)], start=True, stop=True)
                mm(PROJ[:, S:2 * S], wqk4[:, 1, 4 * sl:4 * sl + 4].rearrange("p i r d -> p (i r d)"), ctxT[:, bass.ds(b * S, S)],
                   start=True, stop=True).then_inc(proj_made, 1)

            pe.wait_ge(wqk4_ready, 2)
            pe.wait_ge(v0_copied, 4)
            pe.wait_ge(prep_copied, 8)
            for sl in range(SLOTS):
                project(0, sl, banks[sl % 4], 4)
            pe.wait_ge(stack_ready, 2 * SLOTS)

            def step(b, new, old, more):
                for h in range(H0):
                    if new:
                        N = H0 * b + h
                        for s in range(2):
                            sl, j = divmod(2 * h + s, 4)
                            if j == 0:
                                pe.wait_ge(stack_ready, 2 * (SLOTS * b + sl + 1))
                            at_least(pe, rowmax_done, 4 * (N - 2) + 2 * s + 2)
                            rows = slice(32 * j, 32 * j + 32)
                            for t in range(TB):
                                i = mm(SC[2 * (h % 2) + s][:, t * S:(t + 1) * S], qk[rows, sl, t * P:(t + 1) * P], qk[rows, sl, S:2 * S], start=True, stop=True)
                            i.then_inc(scores_made, 1)
                    item = lagged(b, h, LT, new, old, H0)
                    if item:
                        bv, v = item
                        V = H0 * bv + v
                        pe.wait_ge(attn_ready, V + 1)
                        pe.wait_ge(attn_ready_pool, V + 1)
                        at_least(pe, attnT_ready, V)
                        for kt in range(TB):
                            for t in range(TB):
                                i = turn(PT[:, (2 * kt + t) * P:(2 * kt + t + 1) * P], zs[:, v % 4, 0, t, kt * P:(kt + 1) * P])
                        i.then_inc(attn_turned, 1)
                    item = lagged(b, h, LP, new, old, H0)
                    if item:
                        bv, v = item
                        pe.wait_ge(attnT_ready, H0 * bv + v + 1)
                        if v == 0:
                            pe.wait_ge(vz_ready, 2 * bv + 2)
                            at_least(pe, sums_copied, bv)
                        for kt in range(TB):
                            i = mm(PO[:, 0:S], VZ[:, kt, v, :], AT[:, v % 2, kt, :], start=(v == 0 and kt == 0), stop=(v == H0 - 1 and kt == TB - 1))
                        i.then_inc(pv_done, 1)
                    if more and h % 2 == 0:
                        project(b + 1, h // 2)
                    if old and h == 5:
                        pe.wait_ge(sums_copied, b)
                        pe.wait_ge(next_copied, b)
                        for t in range(TB):
                            i = turn(FIN[:, t * P:(t + 1) * P], oT[:, t * P:(t + 1) * P])
                        i.then_inc(sums_turned, 1)
                    if old and h == 10:
                        pe.wait_ge(heads_ready, b)
                        for t in range(TB):
                            i = turn(FIN[:, t * P:(t + 1) * P], o1[:, t * P:(t + 1) * P])
                        i.then_inc(heads_turned, 1)
                    if old and h == 11:
                        pe.wait_ge(headsT_ready, b)
                        for t in range(TB):
                            i = mm(FIN[:, t * P:(t + 1) * P], oT[:, t * P:(t + 1) * P], wvo[:, 1, :], start=True, stop=True)
                        i.then_inc(wo_done, 1)
                    if old and h == 15:
                        pe.wait_ge(next_norm, b)
                        for t in range(TB):
                            i = turn(FIN[:, t * P:(t + 1) * P], xnb[:, t, :])
                        i.then_inc(next_turned, 1)
            over_batches(pe, step)

            pe.wait_ge(next_copied, B + 1)
            pe.wait_ge(small_in, 112)
            for t in range(NT):
                i = mm(banks[0][:, t * E0:(t + 1) * E0], xmT[:, t * P:(t + 1) * P], gateT, start=True, stop=True)
            i.then_inc(gate_made, 1)
            pe.wait_ge(gate_biased, 1)
            pe.wait_ge(ffn_in, 80)
            pe.sem_inc(h_ready, 2)
            pe.sem_inc(acc_done, 2 * TPG)
            with pe.Fori(0, T // GT // 2) as gg:
                def up(i):
                    G, e = divmod(i, E0)
                    for c, (h0, m) in enumerate(HCH):
                        k = i * 3 + c
                        K = gg * 54 + k
                        tok = xmT[:, bass.ds((gg * 2 + G) * GT, GT)]
                        pe.wait_ge(h_ready, K + 1)
                        mm(banks[k % 2][0:m, :], w1T[:, e * HID + h0:e * HID + h0 + m], tok, start=True, stop=True)
                        mm(banks[2 + k % 2][0:m, :], w3T[:, e * HID + h0:e * HID + h0 + m], tok, start=True, stop=True).then_inc(up_made, 1)

                def down(i):
                    e = i % E0
                    N = gg * 2 * E0 + i
                    pe.wait_ge(h_ready, 2 + 3 * N + 3)
                    pe.wait_ge(acc_done, TPG * N + TPG)
                    for t in range(TPG):
                        for c, (h0, m) in enumerate(HCH):
                            j = mm(banks[4 + i % 2][:, t * P:(t + 1) * P], hs[0:m, i % 2, c, t * P:(t + 1) * P], w2s[0:m, e, c, :],
                                   start=(c == 0), stop=(c == 2))
                    j.then_inc(down_made, 1)
                for i in range(2 * E0):
                    up(i)
                    if i > 0:
                        down(i - 1)
                down(2 * E0 - 1)
            for g in range(4):
                pe.wait_ge(ln_done, 12 + g + 1)
                for t in range(4):
                    i = turn(banks[g][:, t * P:(t + 1) * P], x_tok[:, 4 * g + t, :])
                i.then_inc(c_turned, 1)
            pe.wait_ge(c_copied, 4)
            pe.wait_ge(w1_in, 64)

            def passes(dst, high_w, low_w, high_x, low_x, sem):
                mm(dst, high_w, high_x, start=True, stop=False)
                mm(dst, low_w, high_x, start=False, stop=False)
                mm(dst, high_w, low_x, start=False, stop=True).then_inc(sem, 1)

            def head_twice(w, at, h):
                return w[:, 2 * (at + h * DH1):2 * (at + (h + 1) * DH1)]

            def make_keys(n, h):
                at_least(pe, k1_ready, n)
                passes(KB[:, :], head_twice(W1h, INNER, h), head_twice(W1l, INNER, h), kvh, kvl, k1_made)

            def make_queries(n, h, values=0):
                at_least(pe, q1_ready, n)
                at_least(pe, v1_ready, values)
                passes(VB[:, 0:S], head_twice(W1h, 0, h), head_twice(W1l, 0, h), kvh[:, S:KV], kvl[:, S:KV], q1_made)

            def make_values(n, half, kt):
                part = slice(4 * INNER + 512 * half, 4 * INNER + 512 * (half + 1))
                rows = slice(kt * P, (kt + 1) * P)
                passes(VB[:, :], kvh[:, rows], kvl[:, rows], W1h[:, part], W1l[:, part], v1_made)

            pe.wait_ge(w1_split, len(pieces1))
            pe.wait_ge(kv_split, 2)
            for h in range(2):
                make_keys(h, h)
                make_queries(h, h)
            pe.wait_ge(q1_ready, 2)
            make_values(0, 0, 0)
            pe.wait_ge(v1_ready, 1)

            def step(b, new, old, more):
                for h in range(H1):
                    if old and h == 7:
                        pe.wait_ge(outT_ready, b)
                        if new:
                            pe.wait_ge(k1_ready, H1 * b + h + 2)
                        for t in range(TB):
                            i = turn(KB[:, t * P:(t + 1) * P], outT[:, t * P:(t + 1) * P])
                        i.then_inc(out_turned, 1)
                    if new:
                        N = H1 * b + h
                        pe.wait_ge(k1_ready, N + 1)
                        pe.wait_ge(q1_ready, N + 1)
                        for t in range(TB):
                            at_least(pe, exp1_done, TB * (N - 1) + t + 1)
                            q = QS[:, h % 2, t * P:(t + 1) * P]
                            mm(SA[t][:, :], q, KH[:, h % 2, :], start=True, stop=False)
                            mm(SA[t][:, :], q, KL[:, h % 2, :], start=False, stop=True).then_inc(s1_made, 1)
                    head = lagged(b, h, LT1, new, old, H1)
                    if head:
                        bv, v = head
                        V = H1 * bv + v
                        pe.wait_ge(p1_ready, TB * V + TB)
                        for k in range(2):
                            at_least(pe, p1_split, 2 * (V - 1) + k + 1)
                            for j in range(2):
                                for t in range(TB):
                                    kt = 2 * k + j
                                    i = turn(TU[k][:, (2 * j + t) * P:(2 * j + t + 1) * P], P1[:, v % 4, t, kt * P:(kt + 1) * P])
                            i.then_inc(p1_turned, 1)
                    values = values_of(b, h, new, more)
                    if values:
                        pe.wait_ge(q1_ready, H1 * b + h + 2)
                        make_values(*values)
                    if projects(h, new, more):
                        if old and h == 7:
                            pe.wait_ge(x3_ready, b)
                        if more and h == 14:
                            pe.wait_ge(kv_split, 2 * b + 4)
                        make_keys(H1 * b + h + 2, (h + 2) % H1)
                    head = lagged(b, h, LW1, new, old, H1)
                    if head:
                        bv, v = head
                        pe.wait_ge(o1_ready, H1 * bv + v + 1)
                        if v == 0:
                            at_least(pe, outT_ready, bv)
                        mm(WB[:, 0:S], Wout[:, v, :], OT[:, v % 2, :], start=(v == 0), stop=(v == H1 - 1)).then_inc(wout_done, 1)
                    head = lagged(b, h, LP1, new, old, H1)
                    if head:
                        bv, v = head
                        V = H1 * bv + v
                        if v % 8 == 0:
                            pe.wait_ge(v1_ready, 8 * bv + 4 + 4 * (v // 8))
                        pe.wait_ge(p1_split, 2 * V + 2)
                        at_least(pe, o1_ready, V)
                        for kt in range(4):
                            both = V1[:, kt, v].rearrange("p s d -> p (s d)")
                            mm(OB[:, 0:S], both, PTh[:, v % 2, kt, :], start=(kt == 0), stop=False)
                            i = mm(OB[:, 0:S], both, PTl[:, v % 2, kt, :], start=False, stop=(kt == 3))
                        i.then_inc(pv1_done, 1)
                    if projects(h, new, more):
                        make_queries(H1 * b + h + 2, (h + 2) % H1, values_made(b, h, more))
            over_batches(pe, step)

            for g in range(4):
                pe.wait_ge(ln_done, 16 + g + 1)
                for t in range(4):
                    i = turn(banks[g][:, t * P:(t + 1) * P], xn_tok[:, 4 * g + t, :])
                i.then_inc(d_turned, 1)
            for t in range(NT):
                if t % 4 == 0:
                    pe.wait_ge(d_copied, t // 4 + 1)
                i = mm(banks[4][:, t * E1:(t + 1) * E1], xmT[:, t * P:(t + 1) * P], WrT, start=True, stop=True)
            i.then_inc(r_made, 1)
            pe.wait_ge(oh_ready, 1)
            oh = oneh[:, :, :].rearrange("p t e -> p (t e)")
            mm(banks[5][:, 0:NT * E1], before, oh, start=True, stop=True)
            mm(banks[5][:, NT * E1:2 * NT * E1], ones[:, :], oh, start=True, stop=True).then_inc(rank_made, 1)
            pe.wait_ge(xe_in, 16)
            pe.wait_ge(slots_ready, 1)
            for g in range(4):
                for t in range(4):
                    i = turn(banks[g][:, t * P:(t + 1) * P], xe[:, 4 * g + t, :])
                i.then_inc(xe_turned, 1)
            pe.wait_ge(w1e_in, 160)

            def down1(e):
                pe.wait_ge(h1_act, e + 1)
                pe.wait_ge(h1_dve, e + 1)
                if e >= 2:
                    pe.wait_ge(y1_copied, e - 1)
                for t in range(2):
                    for c in range(4):
                        i = mm(banks[6 + e % 2][:, t * P:(t + 1) * P], h1[:, e % 2, c, t * P:(t + 1) * P], W2[:, e, c, :], start=(c == 0), stop=(c == 3))
                i.then_inc(y1_made, 1)
            for e in range(E1):
                pe.wait_ge(xe_copied, e // 2 + 1)
                for half in range(2):
                    if e >= 1:
                        pe.wait_ge((h1_act, h1_dve)[half], e)
                    for k in range(2):
                        c = 2 * half + k
                        i = mm(banks[4 + half][:, k * CAP:(k + 1) * CAP], W1[:, e, c * P:(c + 1) * P], xeT[:, e * CAP:(e + 1) * CAP], start=True, stop=True)
                    i.then_inc(h1_made, 1)
                if e >= 1:
                    down1(e - 1)
            down1(E1 - 1)


_SHAPES = [((B, S, D), "float32")]


def _constants():
    p = np.arange(P)
    ident = np.eye(P)
    before = p[:, None] < p[None, :]
    low = np.stack([-1.0 * (p % 32 >= 16), -1.0 * (p % 16 >= 8), -1.0 * (p >= DH1)], 1)
    iota = np.broadcast_to(np.arange(E0), (P, E0))
    return np.concatenate([ident, before, low, iota], 1).astype(np.float32)


def kernel(**inputs):
    import concourse.bacc as _bacc
    from concourse import mybir as _mybir
    from concourse.bass_utils import run_bass_kernel_spmd as _run

    i = {k: np.asarray(v) for k, v in inputs.items()}
    L0, F0, L1, F1_ = "L0_xattn_", "L0_ffn_", "L1_xattn_", "L1_ffn_"
    w1 = np.concatenate([i[F0 + "w1"], i[F0 + "new_w1"]], 0)
    w3 = np.concatenate([i[F0 + "w3"], i[F0 + "new_w3"]], 0)
    w2 = np.concatenate([i[F0 + "w2"], i[F0 + "new_w2"]], 0)
    laid = {
        "const": _constants(),
        "x": i["x"].reshape(T, D),
        "ctx": i["ctx_1024"].reshape(T, D),
        "ctxT": i["ctx_1024"].reshape(T, D).T,
        "mask": i["mask_Bx16xSxS2_ff0"].reshape(B * H0, S, S),
        "W_q": i[L0 + "W_q"], "W_k": i[L0 + "W_k"], "W_v": i[L0 + "W_v"], "W_o": i[L0 + "W_o"],
        "lambda_q1": i[L0 + "lambda_q1"].reshape(1, -1), "lambda_k1": i[L0 + "lambda_k1"].reshape(1, -1),
        "lambda_q2": i[L0 + "lambda_q2"].reshape(1, -1), "lambda_k2": i[L0 + "lambda_k2"].reshape(1, -1),
        "rms_scale": i[L0 + "rms_scale"].reshape(1, -1),
        "w1T": w1.reshape(E0 * HID, D).T, "w3T": w3.reshape(E0 * HID, D).T,
        "w2T": w2.transpose(0, 2, 1),
        "gateT": np.concatenate([i[F0 + "gate_weight"], i[F0 + "new_gate_weight"]], 0).T,
        "gate_bias": i[F0 + "gate_bias"].reshape(1, 1),
        "g1": i[L1 + "g1"].reshape(D, 1), "b1": i[L1 + "b1"].reshape(D, 1),
        "g2": i[L1 + "g2"].reshape(D, 1), "b2": i[L1 + "b2"].reshape(D, 1),
        "Wq": i[L1 + "Wq"], "Wkv": i[L1 + "Wkv"], "Wout": i[L1 + "Wout"],
        "Wr": i[F1_ + "Wr"], "W1": i[F1_ + "W1"], "W2": i[F1_ + "W2"],
    }
    nc = _bacc.Bacc("TRN2", target_bir_lowering=False, num_devices=1)
    arrays, args = {}, {}
    for name, v in laid.items():
        v = np.ascontiguousarray(v)
        arrays[f"in_{name}"] = v
        args[name] = nc.dram_tensor(f"in_{name}", v.shape, _mybir.dt.from_np(v.dtype), kind="ExternalInput").ap()
    o = nc.dram_tensor("out_x", (T, D), _mybir.dt.float32, kind="ExternalOutput").ap()
    build(nc, args, o)
    r = _run(nc, [arrays], core_ids=[0])
    return r.results[0]["out_x"].reshape(B, S, D)
```
